# Optimizing a Trainium2 kernel written in Bass

```python
import numpy as np
import jax
import jax.numpy as jnp

def _softmax(x, axis=-1):
    return jax.nn.softmax(x, axis=axis)

def _gelu(x):
    return jax.nn.gelu(x, approximate=True)

def _silu(x):
    return jax.nn.silu(x)

def _sigmoid(x):
    return jax.nn.sigmoid(x)

def _layernorm(x, axis=-1, eps=1e-05):
    m = jnp.mean(x, axis=axis, keepdims=True)
    v = jnp.var(x, axis=axis, keepdims=True)
    return (x - m) / jnp.sqrt(v + eps)

def _scatter_add(tgt, idx, src, axis=0):
    return tgt.at[idx].add(src)

def _segment_sum(src, seg, n):
    return jax.ops.segment_sum(src, seg, n)
kernel_name = 'mk_xattn_ffn_d4_seqx_r8_5fcd25'

def setup_inputs(seed: int=0):
    np.random.seed(seed)
    _w = jnp.asarray

    def _rec_inputs():
        import jax
        import jax.numpy as jnp
        _rk = jax.random.key(seed)
        x = 7.22e-05 + 1 * jax.random.normal(jax.random.fold_in(_rk, 1), (8, 100, 128), jnp.float32)
        _lenS = 100 - jax.random.randint(jax.random.fold_in(_rk, 7), (8,), 0, max(1, 100 // 4) + 1, jnp.int32)
        _lenS2 = 1444 - jax.random.randint(jax.random.fold_in(_rk, 8), (8,), 0, max(1, 1444 // 4) + 1, jnp.int32)
        _ctx_1024P = jax.random.normal(jax.random.fold_in(_rk, 11), (8, 16, 128), jnp.float32)
        _ctx_1024c = jax.random.dirichlet(jax.random.fold_in(_rk, 511), 0.3 * jnp.ones((16,), jnp.float32), (8, 1444))
        _ctx_1024t = jnp.einsum('bsk,bkd->bsd', _ctx_1024c, _ctx_1024P)
        _ctx_1024t = _ctx_1024t * jax.lax.rsqrt(jnp.mean(jnp.square(_ctx_1024t)) + 1e-12) * 0.953939
        ctx_1024 = -0.000514642 + 1.00011 * (_ctx_1024t + 0.3 * jax.random.normal(jax.random.fold_in(_rk, 611), (8, 1444, 128), jnp.float32))
        _validS = jnp.arange(100)[None, :] < _lenS[:, None]
        _validS2 = jnp.arange(1444)[None, :] < _lenS2[:, None]
        _causal = jnp.tril(jnp.ones((100, 100), dtype=bool))
        mask_BxS2_bk0 = jnp.logical_not(jnp.broadcast_to(_validS2[:, :], (8, 1444)))
        mask_BxSxS2_if1 = jnp.where(jnp.ones((8, 100, 1444), dtype=bool), 1, 0).astype(jnp.int32)
        return (x, ctx_1024, mask_BxS2_bk0, mask_BxSxS2_if1)
    x, ctx_1024, mask_BxS2_bk0, mask_BxSxS2_if1 = _rec_inputs()

    def _L0_xattn_setup():
        import jax, jax.numpy as jnp
        import numpy as np
        DIM = 128
        COND_DIM = 128
        H = 16
        D = DIM // H
        EPS = 1e-06

        def rms_norm(x, gamma):
            xf = x.astype(jnp.float32)
            rms = jax.lax.rsqrt(jnp.mean(xf * xf, axis=-1, keepdims=True) + EPS)
            return (xf * rms * gamma[None, :, None, :]).astype(x.dtype)
        key = jax.random.key(seed)
        ks = jax.random.split(key, 12)
        B, N, M = (2, 512, 128)
        s_in = 1.0 / np.sqrt(DIM)
        s_c = 1.0 / np.sqrt(COND_DIM)
        return {'x': jax.random.normal(ks[0], (B, N, DIM), jnp.float32), 'context': jax.random.normal(ks[1], (B, M, COND_DIM), jnp.float32), 'context_mask': jax.random.randint(ks[2], (B, M), 0, 2) > 0, 'Wq': jax.random.normal(ks[3], (DIM, DIM), jnp.float32) * s_in, 'bq': jnp.zeros((DIM,), jnp.float32), 'Wkv': jax.random.normal(ks[4], (2 * DIM, COND_DIM), jnp.float32) * s_c, 'bkv': jnp.zeros((2 * DIM,), jnp.float32), 'gq': jnp.ones((H, D), jnp.float32), 'gk': jnp.ones((H, D), jnp.float32), 'Wo': jax.random.normal(ks[5], (DIM, DIM), jnp.float32) * s_in, 'bo': jnp.zeros((DIM,), jnp.float32)}
    _L0_xattn_all = _L0_xattn_setup()
    _L0_xattn_in = {k: v for k, v in _L0_xattn_all.items() if k in ('Wq', 'bq', 'Wkv', 'bkv', 'gq', 'gk', 'Wo', 'bo')}
    del _L0_xattn_all

    def _L0_ffn_setup():
        import jax, jax.numpy as jnp
        import numpy as np
        N_EXPERTS = 8
        N_GROUP = 4
        TOPK_GROUP = 2
        TOP_K = 2
        HIDDEN = 128
        INTER = 256
        B, S = (1, 128)

        def _grouped_topk(scores):
            T, E = scores.shape
            per_group = E // N_GROUP
            group_scores = scores.reshape(T, N_GROUP, per_group).max(-1)
            _, gidx = jax.lax.top_k(group_scores, TOPK_GROUP)
            gmask = jnp.zeros((T, N_GROUP), scores.dtype).at[jnp.arange(T)[:, None], gidx].set(1.0)
            smask = jnp.repeat(gmask, per_group, axis=1)
            masked = jnp.where(smask > 0, scores, 0.0)
            topk_w, topk_ids = jax.lax.top_k(masked, TOP_K)
            topk_w = topk_w / topk_w.sum(-1, keepdims=True)
            return (topk_ids, topk_w)
        key = jax.random.key(seed)
        k1, k2, k3, k4 = jax.random.split(key, 4)
        return {'hidden_states': jax.random.normal(k1, (B, S, HIDDEN), jnp.float32), 'gate_w': jax.random.normal(k2, (N_EXPERTS, HIDDEN), jnp.float32) * 0.02, 'w13_weight': jax.random.normal(k3, (N_EXPERTS, 2 * INTER, HIDDEN), jnp.float32) * 0.02, 'w2_weight': jax.random.normal(k4, (N_EXPERTS, HIDDEN, INTER), jnp.float32) * 0.02}
    _L0_ffn_all = _L0_ffn_setup()
    _L0_ffn_in = {k: v for k, v in _L0_ffn_all.items() if k in ('gate_w', 'w13_weight', 'w2_weight')}
    del _L0_ffn_all

    def _L1_xattn_setup():
        import jax, jax.numpy as jnp
        import numpy as np
        DIM = 128
        H = 16
        DH = 64
        INNER = H * DH
        SCALE = DH ** (-0.5)
        key = jax.random.key(seed)
        ks = jax.random.split(key, 6)
        B, L, R = (4, 512, 64)
        x = jax.random.normal(ks[0], (B, L, DIM), dtype=jnp.float32)
        context = jax.random.normal(ks[1], (B, R, DIM), dtype=jnp.float32)
        s = DIM ** (-0.5)
        Wq = jax.random.normal(ks[2], (DIM, INNER), dtype=jnp.float32) * s
        Wk = jax.random.normal(ks[3], (DIM, INNER), dtype=jnp.float32) * s
        Wv = jax.random.normal(ks[4], (DIM, INNER), dtype=jnp.float32) * s
        Wo = jax.random.normal(ks[5], (INNER, DIM), dtype=jnp.float32) * INNER ** (-0.5)
        return {'x': x, 'context': context, 'Wq': Wq, 'Wk': Wk, 'Wv': Wv, 'Wo': Wo}
    _L1_xattn_all = _L1_xattn_setup()
    _L1_xattn_in = {k: v for k, v in _L1_xattn_all.items() if k in ('Wq', 'Wk', 'Wv', 'Wo')}
    del _L1_xattn_all

    def _L1_ffn_setup():
        import jax, jax.numpy as jnp
        import numpy as np
        B, T, DIM = (4, 128, 128)
        H, E, DH, K = (8, 5, 64, 3)

        def _topk_mask(s, k):
            idx = jax.lax.top_k(s, k)[1]
            return jnp.sum(jax.nn.one_hot(idx, s.shape[-1], dtype=s.dtype), axis=-2)
        key = jax.random.key(seed)
        ks = jax.random.split(key, 6)
        w = lambda k, shape: jax.random.normal(k, shape, jnp.float32) * 0.02
        return {'x': jax.random.normal(ks[0], (B, T, DIM), jnp.float32), 'Wq': w(ks[1], (DIM, H * E * DH)), 'Wkv': w(ks[2], (DIM, 2 * H * E * DH)), 'Ws': w(ks[3], (DIM, H * E)), 'Wd': w(ks[4], (DIM, H * E)), 'Wo': w(ks[5], (DH, E * DIM))}
    _L1_ffn_all = _L1_ffn_setup()
    _L1_ffn_in = {k: v for k, v in _L1_ffn_all.items() if k in ('Wq', 'Wkv', 'Ws', 'Wd', 'Wo')}
    del _L1_ffn_all

    def _L2_xattn_setup():
        import jax, jax.numpy as jnp
        import numpy as np
        HIDDEN = 128
        HEADS = 16
        HEAD_DIM = HIDDEN // HEADS
        key = jax.random.key(seed)
        ks = jax.random.split(key, 11)
        B, S = (4, 256)
        scale = 1.0 / np.sqrt(HIDDEN)
        inp = {'queries': jax.random.normal(ks[0], (B, S, HIDDEN), jnp.float32), 'keys': jax.random.normal(ks[1], (B, S, HIDDEN), jnp.float32), 'values': jax.random.normal(ks[2], (B, S, HIDDEN), jnp.float32), 'Wq': jax.random.normal(ks[3], (HIDDEN, HIDDEN), jnp.float32) * scale, 'bq': jnp.zeros((HIDDEN,), jnp.float32), 'Wk': jax.random.normal(ks[4], (HIDDEN, HIDDEN), jnp.float32) * scale, 'bk': jnp.zeros((HIDDEN,), jnp.float32), 'Wv': jax.random.normal(ks[5], (HIDDEN, HIDDEN), jnp.float32) * scale, 'bv': jnp.zeros((HIDDEN,), jnp.float32), 'Wo': jax.random.normal(ks[6], (HIDDEN, HIDDEN), jnp.float32) * scale, 'bo': jnp.zeros((HIDDEN,), jnp.float32)}
        return inp
    _L2_xattn_all = _L2_xattn_setup()
    _L2_xattn_in = {k: v for k, v in _L2_xattn_all.items() if k in ('Wq', 'bq', 'Wk', 'bk', 'Wv', 'bv', 'Wo', 'bo')}
    del _L2_xattn_all

    def _L2_ffn_setup():
        import jax, jax.numpy as jnp
        import numpy as np
        N_EXPERTS = 16
        TOP_K = 4
        HIDDEN = 128
        INTER = 64
        B, S = (2, 128)
        key = jax.random.key(seed)
        k1, k2, k3, k4, k5 = jax.random.split(key, 5)
        return {'hidden_states': jax.random.normal(k1, (B, S, HIDDEN), dtype=jnp.float32), 'gate_w': jax.random.normal(k2, (N_EXPERTS, HIDDEN), dtype=jnp.float32) * 0.02, 'w1': jax.random.normal(k3, (N_EXPERTS, HIDDEN, INTER), dtype=jnp.float32) * 0.02, 'w3': jax.random.normal(k4, (N_EXPERTS, HIDDEN, INTER), dtype=jnp.float32) * 0.02, 'w2': jax.random.normal(k5, (N_EXPERTS, INTER, HIDDEN), dtype=jnp.float32) * 0.02}
    _L2_ffn_all = _L2_ffn_setup()
    _L2_ffn_in = {k: v for k, v in _L2_ffn_all.items() if k in ('gate_w', 'w1', 'w3', 'w2')}
    del _L2_ffn_all

    def _L3_xattn_setup():
        import jax, jax.numpy as jnp
        import numpy as np
        import math
        D_MODEL = 128
        N_HEAD = 16
        D_K = D_MODEL // N_HEAD
        key = jax.random.key(seed)
        ks = jax.random.split(key, 12)
        B, S = (2, 256)
        scale = 1.0 / math.sqrt(D_MODEL)
        inp = {'q': jax.random.normal(ks[0], (B, S, D_MODEL), dtype=jnp.float32), 'k': jax.random.normal(ks[1], (B, S, D_MODEL), dtype=jnp.float32), 'v': jax.random.normal(ks[2], (B, S, D_MODEL), dtype=jnp.float32), 'mask': jnp.ones((B, S, S), dtype=jnp.int32), 'Wq': jax.random.normal(ks[3], (D_MODEL, D_MODEL), dtype=jnp.float32) * scale, 'bq': jnp.zeros((D_MODEL,), dtype=jnp.float32), 'Wk': jax.random.normal(ks[4], (D_MODEL, D_MODEL), dtype=jnp.float32) * scale, 'bk': jnp.zeros((D_MODEL,), dtype=jnp.float32), 'Wv': jax.random.normal(ks[5], (D_MODEL, D_MODEL), dtype=jnp.float32) * scale, 'bv': jnp.zeros((D_MODEL,), dtype=jnp.float32), 'Wo': jax.random.normal(ks[6], (D_MODEL, D_MODEL), dtype=jnp.float32) * scale, 'bo': jnp.zeros((D_MODEL,), dtype=jnp.float32)}
        return inp
    _L3_xattn_all = _L3_xattn_setup()
    _L3_xattn_in = {k: v for k, v in _L3_xattn_all.items() if k in ('Wq', 'bq', 'Wk', 'bk', 'Wv', 'bv', 'Wo', 'bo')}
    del _L3_xattn_all

    def _L3_ffn_setup():
        import jax, jax.numpy as jnp
        import numpy as np
        N_EMBD = 128
        N_EXP = 8
        TOP_K = 2
        CAPACITY = 512
        D_FF = 3 * N_EMBD
        key = jax.random.key(seed)
        k1, k2, k3, k4 = jax.random.split(key, 4)
        x = jax.random.normal(k1, (8, 256, N_EMBD), dtype=jnp.float32)
        w_gate = jax.random.normal(k2, (N_EMBD, N_EXP), dtype=jnp.float32) * 0.02
        c_fc = jax.random.normal(k3, (N_EXP, N_EMBD, D_FF), dtype=jnp.float32) * 0.02
        c_proj = jax.random.normal(k4, (N_EXP, D_FF // 2, N_EMBD), dtype=jnp.float32) * 0.02
        return {'x': x, 'w_gate': w_gate, 'c_fc': c_fc, 'c_proj': c_proj}
    _L3_ffn_all = _L3_ffn_setup()
    _L3_ffn_in = {k: v for k, v in _L3_ffn_all.items() if k in ('w_gate', 'c_fc', 'c_proj')}
    del _L3_ffn_all
    return {'x': x, 'ctx_1024': ctx_1024, 'mask_BxS2_bk0': mask_BxS2_bk0, 'mask_BxSxS2_if1': mask_BxSxS2_if1, 'L0_xattn_Wq': _L0_xattn_in['Wq'], 'L0_xattn_bq': _L0_xattn_in['bq'], 'L0_xattn_Wkv': _L0_xattn_in['Wkv'], 'L0_xattn_bkv': _L0_xattn_in['bkv'], 'L0_xattn_gq': _L0_xattn_in['gq'], 'L0_xattn_gk': _L0_xattn_in['gk'], 'L0_xattn_Wo': _L0_xattn_in['Wo'], 'L0_xattn_bo': _L0_xattn_in['bo'], 'L0_ffn_gate_w': _L0_ffn_in['gate_w'], 'L0_ffn_w13_weight': _L0_ffn_in['w13_weight'], 'L0_ffn_w2_weight': _L0_ffn_in['w2_weight'], 'L1_xattn_Wq': _L1_xattn_in['Wq'], 'L1_xattn_Wk': _L1_xattn_in['Wk'], 'L1_xattn_Wv': _L1_xattn_in['Wv'], 'L1_xattn_Wo': _L1_xattn_in['Wo'], 'L1_ffn_Wq': _L1_ffn_in['Wq'], 'L1_ffn_Wkv': _L1_ffn_in['Wkv'], 'L1_ffn_Ws': _L1_ffn_in['Ws'], 'L1_ffn_Wd': _L1_ffn_in['Wd'], 'L1_ffn_Wo': _L1_ffn_in['Wo'], 'L2_xattn_Wq': _L2_xattn_in['Wq'], 'L2_xattn_bq': _L2_xattn_in['bq'], 'L2_xattn_Wk': _L2_xattn_in['Wk'], 'L2_xattn_bk': _L2_xattn_in['bk'], 'L2_xattn_Wv': _L2_xattn_in['Wv'], 'L2_xattn_bv': _L2_xattn_in['bv'], 'L2_xattn_Wo': _L2_xattn_in['Wo'], 'L2_xattn_bo': _L2_xattn_in['bo'], 'L2_ffn_gate_w': _L2_ffn_in['gate_w'], 'L2_ffn_w1': _L2_ffn_in['w1'], 'L2_ffn_w3': _L2_ffn_in['w3'], 'L2_ffn_w2': _L2_ffn_in['w2'], 'L3_xattn_Wq': _L3_xattn_in['Wq'], 'L3_xattn_bq': _L3_xattn_in['bq'], 'L3_xattn_Wk': _L3_xattn_in['Wk'], 'L3_xattn_bk': _L3_xattn_in['bk'], 'L3_xattn_Wv': _L3_xattn_in['Wv'], 'L3_xattn_bv': _L3_xattn_in['bv'], 'L3_xattn_Wo': _L3_xattn_in['Wo'], 'L3_xattn_bo': _L3_xattn_in['bo'], 'L3_ffn_w_gate': _L3_ffn_in['w_gate'], 'L3_ffn_c_fc': _L3_ffn_in['c_fc'], 'L3_ffn_c_proj': _L3_ffn_in['c_proj']}

def reference(x, ctx_1024, mask_BxS2_bk0, mask_BxSxS2_if1, L0_xattn_Wq, L0_xattn_bq, L0_xattn_Wkv, L0_xattn_bkv, L0_xattn_gq, L0_xattn_gk, L0_xattn_Wo, L0_xattn_bo, L0_ffn_gate_w, L0_ffn_w13_weight, L0_ffn_w2_weight, L1_xattn_Wq, L1_xattn_Wk, L1_xattn_Wv, L1_xattn_Wo, L1_ffn_Wq, L1_ffn_Wkv, L1_ffn_Ws, L1_ffn_Wd, L1_ffn_Wo, L2_xattn_Wq, L2_xattn_bq, L2_xattn_Wk, L2_xattn_bk, L2_xattn_Wv, L2_xattn_bv, L2_xattn_Wo, L2_xattn_bo, L2_ffn_gate_w, L2_ffn_w1, L2_ffn_w3, L2_ffn_w2, L3_xattn_Wq, L3_xattn_bq, L3_xattn_Wk, L3_xattn_bk, L3_xattn_Wv, L3_xattn_bv, L3_xattn_Wo, L3_xattn_bo, L3_ffn_w_gate, L3_ffn_c_fc, L3_ffn_c_proj):
    import jax
    import jax.numpy as jnp

    def _L0_xattn_ref(x, context, context_mask, Wq, bq, Wkv, bkv, gq, gk, Wo, bo):
        import jax, jax.numpy as jnp
        import numpy as np
        DIM = 128
        COND_DIM = 128
        H = 16
        D = DIM // H
        EPS = 1e-06

        def rms_norm(x, gamma):
            xf = x.astype(jnp.float32)
            rms = jax.lax.rsqrt(jnp.mean(xf * xf, axis=-1, keepdims=True) + EPS)
            return (xf * rms * gamma[None, :, None, :]).astype(x.dtype)
        B, N, _ = x.shape
        M = context.shape[1]
        q = (x @ Wq.T + bq).reshape(B, N, H, D).transpose(0, 2, 1, 3)
        kv = (context @ Wkv.T + bkv).reshape(B, M, 2, H, D)
        k = kv[:, :, 0].transpose(0, 2, 1, 3)
        v = kv[:, :, 1].transpose(0, 2, 1, 3)
        q = rms_norm(q, gq)
        k = rms_norm(k, gk)
        scale = 1.0 / np.sqrt(D)
        scores = jnp.einsum('bhnd,bhmd->bhnm', q, k) * scale
        bias = jnp.where(context_mask[:, None, None, :], 0.0, -jnp.inf).astype(scores.dtype)
        attn = jax.nn.softmax(scores + bias, axis=-1)
        out = jnp.einsum('bhnm,bhmd->bhnd', attn, v)
        out = out.transpose(0, 2, 1, 3).reshape(B, N, DIM)
        return out @ Wo.T + bo

    def _L0_ffn_ref(hidden_states, gate_w, w13_weight, w2_weight):
        import jax, jax.numpy as jnp
        import numpy as np
        N_EXPERTS = 8
        N_GROUP = 4
        TOPK_GROUP = 2
        TOP_K = 2
        HIDDEN = 128
        INTER = 256
        B, S = (1, 128)

        def _grouped_topk(scores):
            T, E = scores.shape
            per_group = E // N_GROUP
            group_scores = scores.reshape(T, N_GROUP, per_group).max(-1)
            _, gidx = jax.lax.top_k(group_scores, TOPK_GROUP)
            gmask = jnp.zeros((T, N_GROUP), scores.dtype).at[jnp.arange(T)[:, None], gidx].set(1.0)
            smask = jnp.repeat(gmask, per_group, axis=1)
            masked = jnp.where(smask > 0, scores, 0.0)
            topk_w, topk_ids = jax.lax.top_k(masked, TOP_K)
            topk_w = topk_w / topk_w.sum(-1, keepdims=True)
            return (topk_ids, topk_w)
        Bm, Sm, H = hidden_states.shape
        x = hidden_states.reshape(-1, H)
        T = x.shape[0]
        scores = jax.nn.softmax(x @ gate_w.T, axis=-1)
        topk_ids, topk_w = _grouped_topk(scores)
        combine = jnp.zeros((T, N_EXPERTS), x.dtype).at[jnp.arange(T)[:, None], topk_ids].add(topk_w)
        gu = jnp.einsum('th,eih->tei', x, w13_weight)
        gate, up = (gu[..., :INTER], gu[..., INTER:])
        act = jax.nn.silu(gate) * up
        act = act * combine[:, :, None]
        out = jnp.einsum('tei,ehi->th', act, w2_weight)
        return out.reshape(Bm, Sm, H)

    def _L1_xattn_ref(x, context, Wq, Wk, Wv, Wo):
        import jax, jax.numpy as jnp
        import numpy as np
        DIM = 128
        H = 16
        DH = 64
        INNER = H * DH
        SCALE = DH ** (-0.5)
        B, L, _ = x.shape
        R = context.shape[1]
        q = (x @ Wq).reshape(B, L, H, DH).transpose(0, 2, 1, 3)
        k = (context @ Wk).reshape(B, R, H, DH).transpose(0, 2, 1, 3)
        v = (context @ Wv).reshape(B, R, H, DH).transpose(0, 2, 1, 3)
        scores = jnp.einsum('bhld,bhrd->bhlr', q, k) * SCALE
        attn = jax.nn.softmax(scores, axis=-1)
        out = jnp.einsum('bhlr,bhrd->bhld', attn, v)
        out = out.transpose(0, 2, 1, 3).reshape(B, L, INNER)
        return out @ Wo

    def _L1_ffn_ref(x, Wq, Wkv, Ws, Wd, Wo):
        import jax, jax.numpy as jnp
        import numpy as np
        B, T, DIM = (4, 128, 128)
        H, E, DH, K = (8, 5, 64, 3)

        def _topk_mask(s, k):
            idx = jax.lax.top_k(s, k)[1]
            return jnp.sum(jax.nn.one_hot(idx, s.shape[-1], dtype=s.dtype), axis=-2)
        b, t, _ = x.shape
        scale = DH ** (-0.5)
        ss = jax.nn.sigmoid(x @ Ws).reshape(b, t, H, E)
        sd = jax.nn.sigmoid(x @ Wd).reshape(b, t, H, E)
        ms = _topk_mask(ss, K)
        md = _topk_mask(sd, K)
        ss_g = ss * ms
        sd_g = sd * md
        q5 = (x @ Wq).reshape(b, t, H, E, DH)
        kv = (x @ Wkv).reshape(b, t, 2, H, E, DH)
        k5, v5 = (kv[:, :, 0], kv[:, :, 1])
        q = jnp.einsum('bthed,bthe->bhtd', q5, sd_g)
        k = jnp.einsum('bthed,bthe->bhtd', k5, ss_g)
        v = jnp.einsum('bthed,bthe->bhtd', v5, ss_g)
        attn = jax.nn.softmax(jnp.einsum('bhid,bhjd->bhij', q * scale, k), axis=-1)
        out = jnp.einsum('bhij,bhjd->bihd', attn, v)
        o5 = jnp.einsum('bthd,dm->bthm', out, Wo).reshape(b, t, H, E, DIM)
        return jnp.einsum('bthem,bthe->btm', o5, md)

    def _L2_xattn_ref(queries, keys, values, Wq, bq, Wk, bk, Wv, bv, Wo, bo):
        import jax, jax.numpy as jnp
        import numpy as np
        HIDDEN = 128
        HEADS = 16
        HEAD_DIM = HIDDEN // HEADS
        B, Sq, _ = queries.shape
        Skv = keys.shape[1]
        q = (queries @ Wq + bq).reshape(B, Sq, HEADS, HEAD_DIM)
        k = (keys @ Wk + bk).reshape(B, Skv, HEADS, HEAD_DIM)
        v = (values @ Wv + bv).reshape(B, Skv, HEADS, HEAD_DIM)
        logits = jnp.einsum('bqhd,bkhd->bhqk', q, k) / jnp.sqrt(jnp.float32(HEAD_DIM))
        weights = jax.nn.softmax(logits, axis=-1)
        attn = jnp.einsum('bhqk,bkhd->bqhd', weights, v).reshape(B, Sq, HIDDEN)
        return attn @ Wo + bo

    def _L2_ffn_ref(hidden_states, gate_w, w1, w3, w2):
        import jax, jax.numpy as jnp
        import numpy as np
        N_EXPERTS = 16
        TOP_K = 4
        HIDDEN = 128
        INTER = 64
        B, S = (2, 128)
        'DeepseekV3 MoE adapter forward: router -> sparse scores -> expert GLU MLP -> combine.'
        b, s, h = hidden_states.shape
        x = hidden_states.reshape(-1, h)
        logits = jnp.einsum('th,eh->te', x, gate_w)
        probs = jax.nn.softmax(logits, axis=-1)
        topk_w, topk_idx = jax.lax.top_k(probs, TOP_K)
        topk_w = topk_w / jnp.sum(topk_w, axis=-1, keepdims=True)
        one_hot = (topk_idx[..., None] == jnp.arange(N_EXPERTS)).astype(topk_w.dtype)
        scores = jnp.einsum('tk,tke->te', topk_w, one_hot)
        g = jnp.einsum('th,ehi->tei', x, w1)
        u = jnp.einsum('th,ehi->tei', x, w3)
        act = jax.nn.silu(g) * u
        expert_out = jnp.einsum('tei,eih->teh', act, w2)
        out = jnp.einsum('teh,te->th', expert_out, scores)
        return out.reshape(b, s, h)

    def _L3_xattn_ref(q, k, v, mask, Wq, bq, Wk, bk, Wv, bv, Wo, bo):
        import jax, jax.numpy as jnp
        import numpy as np
        import math
        D_MODEL = 128
        N_HEAD = 16
        D_K = D_MODEL // N_HEAD
        B, S, _ = q.shape

        def proj(x, W, b):
            y = x @ W.T + b
            return y.reshape(B, -1, N_HEAD, D_K).transpose(0, 2, 1, 3)
        qh = proj(q, Wq, bq)
        kh = proj(k, Wk, bk)
        vh = proj(v, Wv, bv)
        scores = jnp.einsum('bhqd,bhkd->bhqk', qh, kh) / math.sqrt(D_K)
        scores = jnp.where(mask[:, None, :, :] == 0, -1000000000.0, scores)
        attn = jax.nn.softmax(scores, axis=-1)
        out = jnp.einsum('bhqk,bhkd->bhqd', attn, vh)
        concat = out.transpose(0, 2, 1, 3).reshape(B, -1, D_MODEL)
        return concat @ Wo.T + bo

    def _L3_ffn_ref(x, w_gate, c_fc, c_proj):
        import jax, jax.numpy as jnp
        import numpy as np
        N_EMBD = 128
        N_EXP = 8
        TOP_K = 2
        CAPACITY = 512
        D_FF = 3 * N_EMBD
        B, T, d = x.shape
        N = B * T
        xf = x.reshape(N, d)
        scores = jax.nn.softmax(xf @ w_gate, axis=-1)
        weights, idx = jax.lax.top_k(scores, TOP_K)
        flat_e = idx.reshape(-1)
        tok = jnp.repeat(jnp.arange(N), TOP_K)
        oh = jax.nn.one_hot(flat_e, N_EXP, dtype=jnp.int32)
        pos = (jnp.cumsum(oh, axis=0) * oh).sum(-1) - 1
        valid = pos < CAPACITY
        pos_c = jnp.where(valid, pos, 0)
        vmask = valid.astype(x.dtype)[:, None]
        exp_x = jnp.zeros((N_EXP, CAPACITY, d), x.dtype)
        exp_x = exp_x.at[flat_e, pos_c].add(xf[tok] * vmask)
        h = jnp.einsum('ecd,edf->ecf', exp_x, c_fc)
        a, g = jnp.split(h, 2, axis=-1)
        h = jax.nn.silu(a) * g
        exp_out = jnp.einsum('ecf,efd->ecd', h, c_proj)
        gathered = exp_out[flat_e, pos_c]
        w = weights.reshape(-1)[:, None] * vmask
        out = (gathered * w).reshape(N, TOP_K, d).sum(axis=1)
        return out.reshape(B, T, d)
    x = x + _L0_xattn_ref(_layernorm(x, axis=-1), ctx_1024, mask_BxS2_bk0, L0_xattn_Wq, L0_xattn_bq, L0_xattn_Wkv, L0_xattn_bkv, L0_xattn_gq, L0_xattn_gk, L0_xattn_Wo, L0_xattn_bo)
    x = x + _L0_ffn_ref(_layernorm(x, axis=-1), L0_ffn_gate_w, L0_ffn_w13_weight, L0_ffn_w2_weight)
    x = x + _L1_xattn_ref(_layernorm(x, axis=-1), ctx_1024, L1_xattn_Wq, L1_xattn_Wk, L1_xattn_Wv, L1_xattn_Wo)
    x = x + _L1_ffn_ref(_layernorm(x, axis=-1), L1_ffn_Wq, L1_ffn_Wkv, L1_ffn_Ws, L1_ffn_Wd, L1_ffn_Wo)
    x = x + _L2_xattn_ref(_layernorm(x, axis=-1), ctx_1024, ctx_1024, L2_xattn_Wq, L2_xattn_bq, L2_xattn_Wk, L2_xattn_bk, L2_xattn_Wv, L2_xattn_bv, L2_xattn_Wo, L2_xattn_bo)
    x = x + _L2_ffn_ref(_layernorm(x, axis=-1), L2_ffn_gate_w, L2_ffn_w1, L2_ffn_w3, L2_ffn_w2)
    x = x + _L3_xattn_ref(_layernorm(x, axis=-1), ctx_1024, ctx_1024, mask_BxSxS2_if1, L3_xattn_Wq, L3_xattn_bq, L3_xattn_Wk, L3_xattn_bk, L3_xattn_Wv, L3_xattn_bv, L3_xattn_Wo, L3_xattn_bo)
    x = x + _L3_ffn_ref(_layernorm(x, axis=-1), L3_ffn_w_gate, L3_ffn_c_fc, L3_ffn_c_proj)
    return x

_drawn_inputs = setup_inputs


def setup_inputs(seed=0):
    import zlib

    import numpy as np

    out = dict(_drawn_inputs(seed))
    spreads = {'L0_xattn_bq': (0.0, 0.413),
     'L0_xattn_bkv': (0.0, 0.1),
     'L0_xattn_gq': (1.0, 0.2),
     'L0_xattn_gk': (1.0, 0.2),
     'L0_xattn_bo': (0.0, 0.1),
     'L2_xattn_bq': (0.0, 0.575),
     'L2_xattn_bk': (0.0, 2.0),
     'L2_xattn_bv': (0.0, 0.1),
     'L2_xattn_bo': (0.0, 0.1),
     'L3_xattn_bq': (0.0, 0.517),
     'L3_xattn_bk': (0.0, 2.0),
     'L3_xattn_bv': (0.0, 0.27),
     'L3_xattn_bo': (0.0, 0.1)}
    factors = {'L0_ffn_gate_w': 8.0,
     'L0_ffn_w13_weight': 8.0,
     'L0_ffn_w2_weight': 8.0,
     'L1_ffn_Wq': 45.787,
     'L1_ffn_Ws': 8.672,
     'L2_ffn_gate_w': 8.0,
     'L2_ffn_w1': 8.0,
     'L2_ffn_w3': 8.0,
     'L2_ffn_w2': 8.0,
     'L3_ffn_w_gate': 8.0,
     'L3_ffn_c_fc': 8.0,
     'L3_ffn_c_proj': 8.0}
    for name, (base, spread) in spreads.items():
        noise = np.random.default_rng([zlib.crc32(name.encode()), seed]).standard_normal(out[name].shape)
        drawn = base * np.exp(spread * noise) if base else spread * noise
        out[name] = jnp.asarray(drawn.astype(out[name].dtype))
    for name, factor in factors.items():
        out[name] = (out[name] * factor).astype(out[name].dtype)
    return out
```

```python
from contextlib import ExitStack

import concourse.bass as bass
from concourse import mybir

F32 = mybir.dt.float32
BF16 = mybir.dt.bfloat16
I32 = mybir.dt.int32
U8 = mybir.dt.uint8
ALU = mybir.AluOpType
ACT = mybir.ActivationFunctionType
AX = mybir.AxisListType.X

B = 8
T = 100
D = 128
S = 1444
H = 16
CT = 12
CW = 121
SP_ = CT * CW
NCH = 3
CH = SP_ // NCH
PAIRS = H // 2
DH = 8
GROUPS = 4
GH = H // GROUPS
GW = GH * T
VW = DH + 1
PARTS = 3
K_SEQ = (0, 1, 0, 2, 0, 1)
Q_SEQ = (0, 0, 1, 0, 2, 1)
STACK = 6 * 16
BIAS_ROW = STACK
SHIFT_ROW = STACK + 1
ROWS = STACK + 3
NEG = -float(2 ** 30)
P_SLOTS = 8
SMALL = (0, 2, 3)
MOE = {
    0: (8, 16, lambda half: half // 4),
    2: (16, 8, lambda half: half),
    3: (8, 12, lambda half: half // 3),
}
CAPACITY = 512
SH, SE, SD, SK = 8, 5, 64, 3
SQ = SH * SE * SD


class Steps:

    def __init__(self, nc, ctx, known):
        self.nc, self.ctx, self.known = nc, ctx, known
        self.sems, self.count, self.mark = {}, {}, {}

    def sem(self, name):
        if name not in self.sems:
            self.sems[name] = self.ctx.enter_context(self.nc.semaphore(name))
        return self.sems[name]

    def did(self, name, *key, by=1):
        self.count[name] = self.count.get(name, 0) + by
        self.mark[(name,) + key] = self.count[name]
        return self.sem(name), by

    def seen(self, turn, name, *key):
        totals, marks = self.known if self.known else ({}, {})
        if not self.known:
            return self.sem(name), turn * 2 + 1
        return self.sem(name), turn * totals[name] + marks[(name,) + key]

    def once(self, name, *key):
        return self.sem(name), self.known[1][(name,) + key] if self.known else 1


def build(nc, a, known):
    with ExitStack() as ctx:
        st = Steps(nc, ctx, known)
        did, seen, once = st.did, st.seen, st.once

        def sb(name, shape, dt=F32):
            return ctx.enter_context(nc.sbuf_tensor(name, shape, dt))

        ident = sb("ident", [128, 128])
        identb = sb("identb", [128, 128], BF16)
        headsum = sb("headsum", [128, 128])
        picks = sb("picks", [128, GH, VW])
        eps6 = sb("eps6", [128, 1])
        parity = sb("parity", [128, 2])
        before = sb("before", [128, 128])
        earlier = sb("earlier", [128, 16, 16])
        ones = sb("ones", [128, 128])
        half_power = sb("half_power", [128, 16])
        neg_eye = sb("neg_eye", [128, GH, T], BF16)
        w = {}
        for l in SMALL:
            for n, c in (("wq", 128), ("wk", 128), ("wv", H * VW), ("wo", 128),
                         ("bq", 128), ("bk", 1), ("bv", H * VW), ("bo", 128)):
                w[n, l] = sb(f"{n}{l}", [128, c])
            e, ni, _ = MOE[l]
            w["gw", l] = sb(f"gw{l}", [128, e])
            w["wa", l] = sb(f"wa{l}", [128, ni * 128])
            w["wb", l] = sb(f"wb{l}", [128, ni * 128])
            w["w2", l] = sb(f"w2{l}", [128, ni, 128])
        for n in ("wq", "wk", "wv", "wo"):
            w[n, 1] = sb(f"{n}1", [128, 1024])
        gqk = sb("gqk", [128, 2, 128])
        swd = sb("swd", [128, 2 * SH * SE])
        swqv = sb("swqv", [128, SQ])
        swk = sb("swk", [128, SQ])
        swo = sb("swo", [128, 3, 128])

        x = sb("x", [T, D])
        xn = sb("xn", [T, D])
        xnT = sb("xnT", [128, T])
        bn = sb("bn", [T, 6])
        mv = sb("mv", [T, 2])
        rstd = sb("rstd", [T, 1])
        ctxT = sb("ctxT", [128, SP_])
        ctxN = sb("ctxN", [CW, CT, D])
        ctxTb = sb("ctxTb", [128, SP_], BF16)
        absent = sb("absent", [T, SP_], BF16)
        Kf = sb("Kf", [128, SP_])
        mask_in = Kf[0:T, :].bitcast(I32)
        Kp = sb("Kp", [128, PARTS, SP_], BF16)
        ktmp = Kp[:, :, :].rearrange("p a n -> p (a n)").bitcast(F32)[:, 0:SP_]
        KS = sb("KS", [128, PAIRS, SP_], BF16)
        QS = sb("QS", [128, PAIRS, 2 * T], BF16)
        V = sb("V", [CW, CT, 168])
        qn = sb("qn", [T, D])
        qss = sb("qss", [T, H])
        qTf = sb("qTf", [128, T])
        Qp = sb("Qp", [128, PARTS, 2 * T], BF16)
        mxp = sb("mxp", [T, H, NCH])
        MZ = sb("MZ", [T, PAIRS, 2, 3], BF16)
        rsum = sb("rsum", [T, H])
        attn = sb("attn", [T, D])
        q2 = attn
        attnT = sb("attnT", [128, T])
        yb = sb("yb", [T, D])
        acnt = sb("acnt", [T, 8])
        lg = sb("lg", [T, 80])
        ex = sb("ex", [T, 80])
        gsc = sb("gsc", [T, 16])
        small = sb("small", [T, 4])
        msk = sb("msk", [T, 80])
        comb = sb("comb", [T, 80])
        rank = sb("rank", [T, 80])
        ARENA = 6800
        arena = sb("arena", [128, ARENA])
        P = arena[:, 0:P_SLOTS * GW].rearrange("p (s n) -> p s n", s=P_SLOTS)
        qt = arena[:, 3200:4800]
        qtb = arena[:, 4800:5600].bitcast(BF16)
        accP = arena[:, 5600:6400].rearrange("p (s n) -> p s n", s=2)
        Osb = arena[:, 6400:6800]
        qm = arena[:, 6400:6400 + 2 * T]
        cmp = arena[0:T, 5696:6496].rearrange("t (a n) -> t a n", a=2)
        mrow_in = arena[0:1, 0:SP_ // 4].bitcast(U8)
        mrow = arena[0:1, 400:400 + SP_ // 2].bitcast(BF16)
        qTh = Kf[:, 0:800]
        oT = Kf[:, 0:800]
        Un = Osb
        prod = arena[0:T, 0:SQ]
        sq = arena[0:T, 2560:3072]
        sk = arena[0:T, 3072:3584]
        sv = arena[0:T, 3584:4096]
        sqT = arena[:, 4096:4496]
        skT = arena[:, 4496:4896]
        sc = arena[0:T, 4896:5696]
        pT = arena[0:T, 5696:6496]
        so = sq
        sz = arena[0:T, 3072:3392]
        szT = arena[:, 6496:6796]
        th = [arena[:, 400 * i:400 * i + 400] for i in (0, 1)]
        hm = [arena[:, 400 * i:400 * i + 400] for i in (2, 3)]
        combT = None

        bank = [ctx.enter_context(nc.psum_tensor(f"bank{i}", [128, 512], F32)) for i in range(8)]
        b7b = bank[7][:, :].bitcast(BF16)
        scratch_k, scratch_q = a["scratch_k"], a["scratch_q"]

        def once_now(name):
            return st.sem(name), st.count[name]

        block = ctx.enter_context(nc.Block())

        @block.sync
        def _(sp):
            for t, n in ((ident, "ident"), (headsum, "headsum"), (picks, "picks"), (parity, "parity"),
                         (before, "before"), (earlier, "earlier"), (gqk, "gqk")):
                sp.dma_start(t[...], a[n]).then_inc(*did("const_in", by=16))

            def load(n, l):
                sp.dma_start(w[n, l][...], a[f"{n}{l}"]).then_inc(*did(f"weights_in{l}", by=16))
            for n in ("wq", "wk", "wv", "wo", "bq", "bk", "bv", "bo", "gw", "wa", "wb", "w2"):
                load(n, 0)
            for n in ("wq", "wk", "wv", "wo"):
                load(n, 1)
            for t, n in ((swd, "swd"), (swk, "swk"), (swo, "swo")):
                sp.dma_start(t[...], a[n]).then_inc(*did("weights_in1", by=16))
            for l in (2, 3):
                for n in ("wq", "wk", "wv", "wo", "bq", "bk", "bv", "bo", "gw", "wa", "wb", "w2"):
                    load(n, l)
            with sp.Fori(0, B) as b:
                sp.wait_ge(st.sem("turn_open"), b + 1)
                sp.sem_inc(st.sem("sync_passed"), 1)
                sp.dma_start(x[:, :], a["x"][b]).then_inc(*did("x_in", by=16))
                sp.dma_start(ctxT[:, :], a["ctxT"][b]).then_inc(*did("ctxT_in", by=16))
                sp.dma_start(arena[0:1, 0:SP_ // 4].bitcast(I32), a["mrow"][b]).then_inc(*did("mrow_in", by=16))
                sp.dma_start(ctxN[:, :, :], a["ctxN"][b]).then_inc(*did("ctxN_in", by=16))
                sp.dma_start(mask_in, a["mask"][b]).then_inc(*did("mask_in", by=16))
                sp.dma_start(swqv[:, :], a["swq"]).then_inc(*did("swqv_in", "q", by=16))

                def k_stack(l):
                    sp.wait_ge(*seen(b, "k_parts", l))
                    sp.dma_start(scratch_k, Kp[:, :, :]).then_inc(*did("k_out", l, by=16))
                    if l == 0:
                        sp.wait_ge(*seen(b, "mrow_ready"))
                    else:
                        sp.wait_ge(*seen(b, "scores", "end", l - 1))
                        sp.sem_inc(st.sem("sync_passed"), 1)
                    if l == 0:
                        sp.dma_start(KS[BIAS_ROW:BIAS_ROW + 1, :, :],
                                     mrow[:, :].unsqueeze(1).to_broadcast([1, PAIRS, SP_])
                                     ).then_inc(*did("k_stacked", l, by=16))
                    sp.wait_ge(*seen(b, "k_out", l))
                    for s, part in enumerate(K_SEQ):
                        sp.dma_start(KS[16 * s:16 * s + 16, :, :],
                                     scratch_k[:, part, :].rearrange("(p r) n -> r p n", r=16)
                                     ).then_inc(*did("k_stacked", l, by=16))

                def bias_row(l):
                    sp.wait_ge(*seen(b, "scores", "end", l - 1))
                    sp.dma_start(KS[BIAS_ROW:BIAS_ROW + 1, :, :],
                                 a["padrow"].unsqueeze(1).to_broadcast([1, PAIRS, SP_])
                                 ).then_inc(*did("k_stacked", l, by=16))

                def q_stack(l):
                    sp.wait_ge(*seen(b, "q_parts", l))
                    sp.dma_start(scratch_q, Qp[:, :, :]).then_inc(*did("q_out", l, by=16))
                    sp.wait_ge(*seen(b, "q_out", l))
                    for s, part in enumerate(Q_SEQ):
                        sp.dma_start(QS[16 * s:16 * s + 16, :, :],
                                     scratch_q[:, part, :].rearrange("(p r) n -> r p n", r=16)
                                     ).then_inc(*did("q_stacked", l, by=16))

                k_stack(0)
                q_stack(0)
                bias_row(1)
                sp.wait_ge(*seen(b, "switch_ps", 4))
                sp.dma_start(swqv[:, :], a["swv"]).then_inc(*did("swqv_in", "v", by=16))
                for l in (2, 3):
                    k_stack(l)
                    q_stack(l)
                sp.wait_ge(*seen(b, "x_out", 7))
                sp.sem_inc(st.sem("sync_passed"), 1)
                sp.dma_start(a["out"][b], x[:, :]).then_inc(*did("out_stored", by=16))
                sp.wait_ge(*seen(b, "out_stored"))
                sp.sem_inc(st.sem("turn_open"), 1)

        @block.gpsimd
        def _(pool):
            for n, (ap, value) in enumerate((
                    (ones[:, :], 1.0), (half_power[:, :], -0.5), (KS[STACK:ROWS, :, :], 1.0),
                    (QS[STACK:ROWS, :, :], 1.0), (MZ[:, :, :, :], 0.0), (V[:, :, :], 0.0),
                    (acnt[:, :], 0.0), (MZ[:, :, :, 0:1], 1.0))):
                pool.memset(ap, value).then_inc(*did("pool_setup"))
                pool.wait_ge(*once_now("pool_setup"))
            with pool.Fori(0, B) as b:
                pool.wait_ge(st.sem("turn_open"), b + 1)

                def power(name, ap, n):
                    pool.tensor_tensor(ap, ap, half_power[0:T, 0:n], ALU.pow).then_inc(*did(*name))

                def norm(k):
                    pool.wait_ge(*seen(b, "ln_var", k))
                    power(("ln_rstd", k), rstd[:, :], 1)

                norm(0)
                pool.wait_ge(*seen(b, "q_ms"))
                power(("q_rms",), qss[:, :], H)
                norm(1)
                norm(2)
                for g in range(GROUPS):
                    for c in range(CT):
                        pool.wait_ge(*seen(b, "exp", 1, g, c))
                        t = g * CT + c
                        dst = accP[0:CW, g % 2, :]
                        if c == 0:
                            if g >= 2:
                                pool.wait_ge(*seen(b, "p_sums", g - 2))
                            pool.sem_inc(st.sem("pool_passed"), 1)
                            pool.tensor_copy(dst, P[0:CW, t % P_SLOTS, :]).then_inc(*did("p_added", g, c))
                        else:
                            pool.wait_ge(*seen(b, "p_added", g, c - 1))
                            pool.tensor_tensor(dst, dst, P[0:CW, t % P_SLOTS, :], ALU.add).then_inc(*did("p_added", g, c))
                for k in range(3, 8):
                    norm(k)

        @block.tensor
        def _(pe):
            pe.wait_ge(*once("pool_setup"))
            pe.wait_ge(*once("const_in"))
            pe.wait_ge(*once("setup_bf16"))
            with pe.Fori(0, B) as b:
                pe.wait_ge(st.sem("turn_open"), b + 1)

                def norm_T(k):
                    pe.wait_ge(*seen(b, "xn", k))
                    pe.transpose(bank[7][:, 0:T], xn[:, :], ident[0:T, 0:T]).then_inc(*did("xnT_ps", k))
                    pe.wait_ge(*seen(b, "xnT", k))

                def prep(l):
                    if l == 0:
                        pe.wait_ge(*seen(b, "ctxT_in"))
                    else:
                        pe.wait_ge(*seen(b, "x_out", 2 * l - 1))
                    for ch in range(NCH):
                        pe.matmul(bank[ch][:, 0:CH], w["wk", l][:, :], ctxT[:, ch * CH:(ch + 1) * CH],
                                  start=True, stop=True).then_inc(*did("k_ps", l, ch))
                    for c in range(CT):
                        mm = pe.matmul(bank[3 + c // 3][0:CW, (c % 3) * 144:(c % 3) * 144 + 144],
                                       ctxT[:, c * CW:(c + 1) * CW], w["wv", l][:, :], start=True, stop=True)
                        if c % 3 == 2:
                            mm.then_inc(*did("v_ps", l, c // 3))
                    if l == 0:
                        for ch in range(NCH):
                            pe.wait_ge(*seen(b, "k_squared", ch))
                            pe.matmul(bank[ch][:, 0:CH], headsum[:, :], ktmp[:, ch * CH:(ch + 1) * CH],
                                      start=True, stop=True).then_inc(*did("k_ss", ch))

                def q_small(l):
                    pe.matmul(bank[6][0:T, 0:D], xnT[:, :], w["wq", l][:, :], start=True, stop=True
                              ).then_inc(*did("q_ps", l))
                    pe.wait_ge(*seen(b, "q_ready", l))
                    pe.transpose(bank[7][:, 0:T], qn[:, :], ident[0:T, 0:T]).then_inc(*did("qT_ps", l))

                def q_wide():
                    for p in range(8):
                        mm = pe.matmul(bank[p // 4][:, (p % 4) * T:(p % 4 + 1) * T],
                                       w["wq", 1][:, p * 128:(p + 1) * 128], xnT[:, :], start=True, stop=True)
                        if p % 4 == 3:
                            mm.then_inc(*did("qh_ps", p // 4))
                    for h in range(H):
                        if h % 8 == 0:
                            pe.wait_ge(*seen(b, "qh", h // 8))
                        r, j = 64 * (h % 2), h // 2
                        mm = pe.matmul(bank[2 + 2 * (h % 2) + j // 4][:, (j % 4) * T:(j % 4 + 1) * T],
                                       w["wk", 1][r:r + 64, (h // 2) * 128:(h // 2 + 1) * 128],
                                       qTh[r:r + 64, (h // 2) * T:(h // 2 + 1) * T], start=True, stop=True)
                        if h % 8 >= 6:
                            mm.then_inc(*did("qt_ps", h // 8, h % 2))

                def max_scores(l, g, k):
                    i, ch = divmod(k, NCH)
                    h = GH * g + i
                    n = g * 12 + k
                    if n >= 2:
                        pe.wait_ge(*seen(b, "max_chunk", l, n - 2))
                    dst = bank[3 + n % 2][0:T, 0:CH]
                    cols = slice(ch * CH, (ch + 1) * CH)
                    if l == 1:
                        pe.matmul(dst, qtb[:, h * T:(h + 1) * T], ctxTb[:, cols], start=True, stop=True
                                  ).then_inc(*did("max_scores", l, n))
                        return
                    p, e = h // 2, h % 2
                    if l == 3:
                        pe.matmul(dst, neg_eye[0:T, 0, :], absent[:, cols], start=True, stop=False)
                    pe.matmul(dst, QS[0:BIAS_ROW + 1, p, e * T:(e + 1) * T], KS[0:BIAS_ROW + 1, p, cols],
                              start=(l != 3), stop=True).then_inc(*did("max_scores", l, n))

                def shift_T(l, g):
                    pe.wait_ge(*seen(b, "maxima", l, g))
                    for n in range(4):
                        mm = pe.transpose(b7b[STACK:ROWS, n * T:(n + 1) * T], MZ[:, 2 * g + n // 2, n % 2, :],
                                          identb[0:T, 0:T])
                    mm.then_inc(*did("shift_ps", l, g))

                def scores(l, g, c):
                    t = g * CT + c
                    if c == 0:
                        pe.wait_ge(*seen(b, "shift", l, g))
                    if t >= 3:
                        pe.wait_ge(*seen(b, "exp", l, (t - 3) // CT, (t - 3) % CT))
                    bk = bank[t % 3]
                    cols = slice(c * CW, (c + 1) * CW)
                    if l == 1:
                        pe.matmul(bk[0:CW, 0:GW], ctxT[:, cols], qt[:, g * GW:(g + 1) * GW], start=True, stop=False)
                        mm = pe.matmul(bk[0:CW, 0:GW], KS[STACK:ROWS, 0, cols], QS[STACK:ROWS, 2 * g:2 * g + 2, :],
                                       start=False, stop=True)
                    else:
                        if l == 3:
                            pe.matmul(bk[0:CW, 0:GW], absent[:, cols], neg_eye[0:T, :, :], start=True, stop=False)
                        for p in (0, 1):
                            mm = pe.matmul(bk[0:CW, 2 * T * p:2 * T * (p + 1)], KS[0:ROWS, 2 * g + p, cols],
                                           QS[0:ROWS, 2 * g + p, :], start=(l != 3), stop=(l != 3 or p == 1))
                    mm.then_inc(*did("scores", l, g, c))
                    if t == GROUPS * CT - 1:
                        st.mark["scores", "end", l] = st.count["scores"]

                def values(l, g, u):
                    pe.wait_ge(*seen(b, "exp", l, g, 4 * u + 3))
                    if u == 0 and g > 0:
                        pe.wait_ge(*(seen(b, "u_ready", g - 1) if l == 1 else seen(b, "o_copied", l, g - 1)))
                    if l == 1:
                        for r in range(4):
                            c = 4 * u + r
                            mm = pe.matmul(bank[5][:, 0:GW], ctxN[:, c, :], P[0:CW, (g * CT + c) % P_SLOTS, :],
                                           start=(c == 0), stop=(c == CT - 1))
                            mm.then_inc(*did("values", l, g, c))
                        return
                    for lo, hi, v0 in ((0, 3 * T, 0), (3 * T, GW, 3 * VW)):
                        for r in range(4):
                            c = 4 * u + r
                            v = GH * VW * g + v0
                            mm = pe.matmul(bank[5][32 * r:32 * r + 32, lo:hi], V[:, c, v:v + 32],
                                           P[0:CW, (g * CT + c) % P_SLOTS, lo:hi],
                                           start=(u == 0 and lo == 0), stop=(u == 2), skip_group_check=True)
                    mm.then_inc(*did("values", l, g, 4 * u + 3))

                def p_sums(g):
                    pe.wait_ge(*seen(b, "p_added", g, CT - 1))
                    pe.matmul(bank[6][:, 0:GW], ones[0:CW, :], accP[0:CW, g % 2, :], start=True, stop=True
                              ).then_inc(*did("p_sums", g))

                def heads_out(l, g):
                    if l == 1:
                        pe.wait_ge(*seen(b, "u_ready", g))
                        for i in range(GH):
                            h = GH * g + i
                            mm = pe.matmul(bank[7][64 * (h % 2):64 * (h % 2) + 64, (i // 2) * T:(i // 2 + 1) * T],
                                           w["wv", 1][:, h * 64:(h + 1) * 64], Un[:, i * T:(i + 1) * T],
                                           start=True, stop=True, skip_group_check=True)
                        mm.then_inc(*did("heads", l, g))
                        return
                    pe.wait_ge(*seen(b, "o_copied", l, g))
                    for i in range(GH):
                        h = GH * g + i
                        mm = pe.matmul(bank[6][0:T, h * VW:(h + 1) * VW], Osb[:, i * T:(i + 1) * T],
                                       picks[:, i, :], start=True, stop=True, skip_group_check=True)
                    mm.then_inc(*did("heads", l, g))

                def cross(l):
                    pe.wait_ge(*once(f"weights_in{l}"))
                    if l != 1:
                        prep(l)
                    norm_T(2 * l)
                    if l == 1:
                        q_wide()
                        pe.wait_ge(*seen(b, "qt"))
                        pe.wait_ge(*seen(b, "ctxTb"))
                        pe.wait_ge(*seen(b, "ctxN_in"))
                        pe.wait_ge(*seen(b, "k_stacked", 1))
                    else:
                        q_small(l)
                        pe.wait_ge(*seen(b, "k_stacked", l))
                        pe.wait_ge(*seen(b, "q_stacked", l))
                        pe.wait_ge(*seen(b, "v_ready", l, 3))
                    if l == 3:
                        pe.wait_ge(*seen(b, "absent"))
                    for k in range(12):
                        max_scores(l, 0, k)
                    for g in range(GROUPS):
                        if l == 1 and g > 1:
                            pe.wait_ge(*seen(b, "oT", g - 2))
                        shift_T(l, g)
                        for u in range(3):
                            for c in range(4 * u, 4 * u + 4):
                                scores(l, g, c)
                                if g + 1 < GROUPS:
                                    max_scores(l, g + 1, c)
                            if l == 1 and g and u == 0:
                                p_sums(g - 1)
                            if u:
                                values(l, g, u - 1)
                            if l == 1 and g and u == 1:
                                heads_out(l, g - 1)
                        values(l, g, 2)
                        if l != 1:
                            heads_out(l, g)
                    if l == 1:
                        p_sums(GROUPS - 1)
                        pe.wait_ge(*seen(b, "oT", GROUPS - 2))
                        heads_out(l, GROUPS - 1)
                    if l == 1:
                        pe.wait_ge(*seen(b, "oT", GROUPS - 1))
                        for p in range(8):
                            mm = pe.matmul(bank[6][0:T, 0:D], oT[:, p * T:(p + 1) * T],
                                           w["wo", 1][:, p * 128:(p + 1) * 128], start=(p == 0), stop=(p == 7))
                        mm.then_inc(*did("y_ps", 2 * l))
                        return
                    pe.wait_ge(*seen(b, "attn", l))
                    pe.transpose(bank[7][:, 0:T], attn[:, :], ident[0:T, 0:T]).then_inc(*did("attnT_ps", l))
                    pe.wait_ge(*seen(b, "attnT", l))
                    pe.matmul(bank[6][0:T, 0:D], attnT[:, :], w["wo", l][:, :], start=True, stop=True
                              ).then_inc(*did("y_ps", 2 * l))

                def experts(l):
                    e, ni, of_half = MOE[l]
                    norm_T(2 * l + 1)
                    pe.matmul(bank[6][0:T, 0:e], xnT[:, :], w["gw", l][:, :], start=True, stop=True
                              ).then_inc(*did("logits", l))

                    def up(ck):
                        base = 3 * (ck % 2)
                        if ck >= 2:
                            pe.wait_ge(*seen(b, "hidden", l, ck - 2))
                        for n, wn in ((0, "wa"), (1, "wb")):
                            for t in range(4):
                                m = 4 * ck + t
                                mm = pe.matmul(bank[base + n][:, t * T:(t + 1) * T], w[wn, l][:, m * 128:(m + 1) * 128],
                                               xnT[:, :], start=True, stop=True)
                            mm.then_inc(*did("gate_up", l, ck, n))

                    def weigh(ck):
                        base = 3 * (ck % 2)
                        for t in range(4):
                            for s in (0, 1):
                                ex_ = of_half(2 * (4 * ck + t) + s)
                                mm = pe.matmul(bank[base + 2][64 * s:64 * s + 64, t * T:(t + 1) * T],
                                               comb[:, ex_:ex_ + 1].to_broadcast([T, 64]), ident[0:T, 0:T],
                                               start=True, stop=True, skip_group_check=True)
                        mm.then_inc(*did("weighed", l, ck))

                    def down(ck):
                        pe.wait_ge(*seen(b, "hidden", l, ck))
                        for t in range(4):
                            m = 4 * ck + t
                            mm = pe.matmul(bank[7][0:T, 0:D], hm[ck % 2][:, t * T:(t + 1) * T], w["w2", l][:, m, :],
                                           start=(m == 0), stop=(m == ni - 1))
                        mm.then_inc(*did("down", l, ck))

                    up(0)
                    up(1)
                    if l == 3:
                        pe.wait_ge(*seen(b, "kept"))
                        pe.matmul(bank[6][0:T, 16:24], before[0:T, 0:T], msk[:, 0:8], start=True, stop=False)
                        pe.matmul(bank[6][0:T, 16:24], ones[0:T, 0:T], acnt[:, :], start=False, stop=True
                                  ).then_inc(*did("position"))
                    pe.wait_ge(*seen(b, "comb", l))
                    for ck in range(ni // 4):
                        if ck >= 2:
                            up(ck)
                        weigh(ck)
                        if ck:
                            down(ck - 1)
                    down(ni // 4 - 1)

                def switch():
                    norm_T(3)
                    pe.matmul(bank[6][0:T, 0:2 * SH * SE], xnT[:, :], swd[:, :], start=True, stop=True
                              ).then_inc(*did("gates_ps"))
                    n = 0
                    for which in range(3):
                        if which == 0:
                            pe.wait_ge(*seen(b, "swqv_in", "q"))
                        if which == 2:
                            pe.wait_ge(*seen(b, "swqv_in", "v"))
                        src = swk if which == 1 else swqv
                        for k in range(5):
                            if n >= 5:
                                pe.wait_ge(*seen(b, "gated", n - 5))
                            mm = pe.matmul(bank[n % 5][0:T, :], xnT[:, :], src[:, k * 512:(k + 1) * 512],
                                           start=True, stop=True)
                            mm.then_inc(*did("switch_ps", n))
                            n += 1
                    for which, src, bk in ((0, sq, 5), (1, sk, 6)):
                        pe.wait_ge(*seen(b, "switch_sum", which))
                        for c in range(4):
                            mm = pe.transpose(bank[bk][:, c * T:(c + 1) * T], src[:, c * 128:(c + 1) * 128], ident[0:T, 0:T])
                        mm.then_inc(*did("switch_T_ps", which))
                    pe.wait_ge(*seen(b, "switch_T", 1))
                    pe.wait_ge(*seen(b, "gated", 14))
                    for h in range(SH):
                        r = 64 * (h % 2)
                        c = slice((h // 2) * T, (h // 2 + 1) * T)
                        mm = pe.matmul(bank[h % 2][0:T, (h // 2) * T:(h // 2 + 1) * T], sqT[r:r + 64, c], skT[r:r + 64, c],
                                       start=True, stop=True)
                        if h >= 6:
                            mm.then_inc(*did("self_scores", h % 2))
                    pe.wait_ge(*seen(b, "self_exp"))
                    for h in range(SH):
                        mm = pe.transpose(bank[2 + h // 4][0:T, (h % 4) * T:(h % 4 + 1) * T],
                                          sc[:, h * T:(h + 1) * T], ident[0:T, 0:T])
                        if h % 4 == 3:
                            mm.then_inc(*did("self_pT_ps", h // 4))
                    pe.wait_ge(*seen(b, "self_pT", 1))
                    pe.wait_ge(*seen(b, "switch_sum", 2))
                    for h in range(SH):
                        mm = pe.matmul(bank[4][0:T, h * SD:(h + 1) * SD], pT[:, h * T:(h + 1) * T],
                                       sv[:, h * SD:(h + 1) * SD], start=True, stop=True)
                    mm.then_inc(*did("self_out"))
                    pe.wait_ge(*seen(b, "switch_z"))
                    for c in range(3):
                        n = 128 if c < 2 else 64
                        mm = pe.transpose(bank[5][0:n, c * T:(c + 1) * T], sz[:, c * 128:c * 128 + n], ident[0:T, 0:T])
                    mm.then_inc(*did("switch_zT_ps"))
                    pe.wait_ge(*seen(b, "switch_zT"))
                    for c in range(3):
                        n = 128 if c < 2 else 64
                        mm = pe.matmul(bank[7][0:T, 0:D], szT[0:n, c * T:(c + 1) * T], swo[0:n, c, :],
                                       start=(c == 0), stop=(c == 2))
                    mm.then_inc(*did("y_ps", 3))

                for l in range(4):
                    cross(l)
                    if l == 1:
                        switch()
                    else:
                        experts(l)

        @block.scalar
        def _(act):
            act.wait_ge(*once("pool_setup"))
            act.wait_ge(*once("setup_bf16"))
            with act.Fori(0, B) as b:
                act.wait_ge(st.sem("turn_open"), b + 1)

                def prep(l):
                    act.wait_ge(*once(f"weights_in{l}"))
                    if l == 0:
                        act.wait_ge(*seen(b, "absent"))
                        act.wait_ge(*seen(b, "ctxT_in"))
                        act.activation(ctxTb[:, :], ctxT[:, :], ACT.Copy).then_inc(*did("ctxTb"))
                    for ch in range(NCH):
                        act.wait_ge(*seen(b, "k_ps", l, ch))
                        cols = slice(ch * CH, (ch + 1) * CH)
                        act.activation(Kf[:, cols], bank[ch][:, 0:CH], ACT.Identity, bias=w["bk", l][:, 0:1]
                                       ).then_inc(*did("k_biased", l, ch))
                    if l == 0:
                        for ch in range(NCH):
                            cols = slice(ch * CH, (ch + 1) * CH)
                            act.wait_ge(*seen(b, "k_biased", l, ch))
                            act.activation(ktmp[:, cols], Kf[:, cols], ACT.Square).then_inc(*did("k_squared", ch))
                        for ch in range(NCH):
                            cols = slice(ch * CH, (ch + 1) * CH)
                            act.wait_ge(*seen(b, "k_ss", ch))
                            act.activation(ktmp[:, cols], bank[ch][:, 0:CH], ACT.Ln, bias=eps6[:, 0:1], scale=1.0 / DH
                                           ).then_inc(*did("k_log", ch))
                        act.wait_ge(*seen(b, "k_log", NCH - 1))
                        act.activation(ktmp[:, :], ktmp[:, :], ACT.Exp, scale=-0.5).then_inc(*did("k_rms"))
                        act.wait_ge(*seen(b, "k_normed"))
                    else:
                        act.wait_ge(*seen(b, "k_biased", l, NCH - 1))
                    act.activation(Kp[:, 0, :], Kf[:, :], ACT.Copy).then_inc(*did("k_high", l))
                    act.wait_ge(*seen(b, "k_rest", l))
                    act.activation(Kp[:, 1, :], Kf[:, :], ACT.Copy).then_inc(*did("k_middle", l))

                def exps(l):
                    for g in range(GROUPS):
                        act.wait_ge(*seen(b, "shift_ps", l, g))
                        act.activation(QS[STACK:ROWS, 2 * g:2 * g + 2, :].rearrange("p a n -> p (a n)"),
                                       b7b[STACK:ROWS, 0:GW], ACT.Copy).then_inc(*did("shift", l, g))
                        for c in range(CT):
                            t = g * CT + c
                            act.wait_ge(*seen(b, "scores", l, g, c))
                            if t >= P_SLOTS:
                                o = t - P_SLOTS
                                u = (o % CT) if l == 1 else 4 * ((o % CT) // 4) + 3
                                act.wait_ge(*seen(b, "values", l, o // CT, u))
                                if l == 1:
                                    act.wait_ge(*seen(b, "p_added", o // CT, o % CT))
                            act.activation(P[0:CW, t % P_SLOTS, :], bank[t % 3][0:CW, 0:GW], ACT.Exp
                                           ).then_inc(*did("exp", l, g, c))
                            if l == 1 and c == 10 and g > 0:
                                heads_T(g - 1)
                        if l != 1:
                            act.wait_ge(*seen(b, "values", l, g, CT - 1))
                            if g > 0:
                                act.wait_ge(*seen(b, "heads", l, g - 1))
                            act.activation(Osb, bank[5][:, 0:GW], ACT.Copy).then_inc(*did("o_copied", l, g))
                    if l == 1:
                        heads_T(GROUPS - 1)

                def heads_T(g):
                    act.wait_ge(*seen(b, "heads", 1, g))
                    act.activation(oT[:, 2 * g * T:(2 * g + 2) * T], bank[7][:, 0:2 * T], ACT.Copy
                                   ).then_inc(*did("oT", g))

                def q_path(l):
                    act.wait_ge(*seen(b, "qT_ps", l))
                    act.activation(qTf[:, :], bank[7][:, 0:T], ACT.Copy, scale=float(DH) ** -0.5
                                   ).then_inc(*did("qT", l))

                def q_wide():
                    for n in range(2):
                        act.wait_ge(*seen(b, "qh_ps", n))
                        act.activation(qTh[:, n * 400:(n + 1) * 400], bank[n][:, 0:400], ACT.Copy, scale=0.125
                                       ).then_inc(*did("qh", n))
                    for n in range(4):
                        half, e = n // 2, n % 2
                        act.wait_ge(*seen(b, "qt_ps", half, e))
                        act.activation(qt[:, :].rearrange("p (j e q) -> p j e q", j=8, e=2)[:, 4 * half:4 * half + 4, e, :],
                                       bank[2 + 2 * e + half][:, 0:400].rearrange("p (j q) -> p j q", j=4), ACT.Copy
                                       ).then_inc(*did("qt_f", n))
                    act.wait_ge(*seen(b, "qt_f", 3))
                    act.activation(qtb[:, :], qt[:, :], ACT.Copy).then_inc(*did("qt"))

                def experts(l):
                    e, ni, _ = MOE[l]
                    act.wait_ge(*seen(b, "top", l))
                    act.activation(ex[:, 0:e], lg[:, 0:e], ACT.Exp, bias=small[:, 0:1]).then_inc(*did("route_exp", l))
                    for ck in range(ni // 4):
                        act.wait_ge(*seen(b, "gate_up", l, ck, 1))
                        if ck >= 2:
                            act.wait_ge(*seen(b, "hidden", l, ck - 2))
                        act.activation(th[ck % 2], bank[3 * (ck % 2)][:, 0:GW], ACT.Tanh, scale=0.5
                                       ).then_inc(*did("tanh", l, ck))

                def switch():
                    act.wait_ge(*seen(b, "gates_z"))
                    act.activation(ex[:, 0:80], lg[:, 0:80], ACT.Exp, scale=-1.0).then_inc(*did("gates_exp"))
                    for which, dst, bk in ((0, sqT, 5), (1, skT, 6)):
                        act.wait_ge(*seen(b, "switch_T_ps", which))
                        act.activation(dst, bank[bk][:, 0:400], ACT.Copy).then_inc(*did("switch_T", which))
                    act.wait_ge(*seen(b, "self_shifted", 1))
                    act.activation(sc, sc, ACT.Exp, scale=float(SD) ** -0.5).then_inc(*did("self_exp"))
                    for n in (0, 1):
                        act.wait_ge(*seen(b, "self_pT_ps", n))
                        act.activation(pT[:, n * 400:(n + 1) * 400], bank[2 + n][0:T, 0:400], ACT.Copy
                                       ).then_inc(*did("self_pT", n))
                    act.wait_ge(*seen(b, "switch_zT_ps"))
                    act.activation(szT[:, 0:2 * T], bank[5][:, 0:2 * T], ACT.Copy).then_inc(*did("switch_zT"))
                    act.activation(szT[0:64, 2 * T:3 * T], bank[5][0:64, 2 * T:3 * T], ACT.Copy
                                   ).then_inc(*did("switch_zT"))

                for l in range(4):
                    if l != 1:
                        prep(l)
                        q_path(l)
                    else:
                        q_wide()
                    exps(l)
                    if l == 1:
                        switch()
                    else:
                        experts(l)

        @block.vector
        def _(dve):
            V_ = nc.vector

            dve.wait_ge(*once("pool_setup"))
            dve.wait_ge(*once("const_in"))
            V_.tensor_copy(identb[:, :], ident[:, :]).then_inc(*did("setup_bf16"))
            V_.memset(eps6[:, :], 1e-6).then_inc(*did("setup_bf16"))
            V_.tensor_scalar(neg_eye[0:T, :, :], ident[0:T, 0:T].unsqueeze(1).to_broadcast([T, GH, T]), NEG, None, ALU.mult
                             ).then_inc(*did("setup_bf16"))
            V_.tensor_tensor(gqk[:, 0, :], gqk[:, 0, :], gqk[:, 1, :], ALU.mult).then_inc(*did("setup_bf16"))
            dve.sem_inc(st.sem("turn_open"), 1)
            with dve.Fori(0, B) as b:
                dve.wait_ge(st.sem("turn_open"), b + 1)

                def link(ins):
                    s, n = did("vector_order", st.count.get("vector_order", 0))
                    ins.then_inc(s, n)
                    dve.wait_ge(*seen(b, "vector_order", st.count["vector_order"] - 1))

                def norm(k):
                    link(V_.bn_stats(bn[:, :], x[:, :]))
                    dve.sem_inc(st.sem("vector_passed"), 1)
                    link(V_.bn_aggr(mv[:, :], bn[:, :]))
                    V_.tensor_scalar(rstd[:, :], mv[:, 1:2], 1e-5, None, ALU.add).then_inc(*did("ln_var", k))
                    dve.wait_ge(*seen(b, "ln_rstd", k))
                    V_.tensor_scalar(xn[:, :], x[:, :], mv[:, 0:1], rstd[:, 0:1], ALU.subtract, ALU.mult
                                     ).then_inc(*did("xn", k))
                    dve.wait_ge(*seen(b, "xnT_ps", k))
                    V_.tensor_copy(xnT[:, :], bank[7][:, 0:T]).then_inc(*did("xnT", k))

                def add_y(k, ps, bias=None):
                    dve.wait_ge(*seen(b, "y_ps", k))
                    if bias is not None:
                        link(V_.tensor_tensor(yb[:, :], ps, bias, ALU.add))
                        V_.tensor_tensor(x[:, :], x[:, :], yb[:, :], ALU.add).then_inc(*did("x_out", k))
                    else:
                        V_.tensor_tensor(x[:, :], x[:, :], ps, ALU.add).then_inc(*did("x_out", k))
                    dve.wait_ge(*seen(b, "x_out", k))

                def prep(l):
                    if l == 0:
                        dve.wait_ge(*seen(b, "k_rms"))
                        V_.tensor_tensor(Kf[:, :], Kf[:, :], ktmp, ALU.mult).then_inc(*did("k_normed"))
                    dve.wait_ge(*seen(b, "k_high", l))
                    V_.tensor_tensor(Kf[:, :], Kf[:, :], Kp[:, 0, :], ALU.subtract).then_inc(*did("k_rest", l))
                    dve.wait_ge(*seen(b, "k_middle", l))
                    V_.tensor_tensor(Kp[:, 2, :], Kf[:, :], Kp[:, 1, :], ALU.subtract).then_inc(*did("k_parts", l))

                def v_bias(l):
                    for u in range(4):
                        dve.wait_ge(*seen(b, "v_ps", l, u))
                        V_.tensor_tensor(V[:, 3 * u:3 * u + 3, 0:144],
                                         bank[3 + u][0:CW, 0:432].rearrange("p (a n) -> p a n", a=3),
                                         w["bv", l][0:CW, :].unsqueeze(1).to_broadcast([CW, 3, 144]), ALU.add
                                         ).then_inc(*did("v_ready", l, u))

                def q_path(l):
                    dve.wait_ge(*seen(b, "q_ps", l))
                    if l == 0:
                        link(V_.tensor_tensor(qn[:, :], bank[6][0:T, 0:D], w["bq", l][0:T, :], ALU.add))
                        link(V_.tensor_tensor(q2[:, :], qn[:, :], qn[:, :], ALU.mult))
                        link(V_.reduce_sum(qss[:, :], q2[:, :].rearrange("p (h d) -> p h d", h=H), AX))
                        V_.tensor_scalar(qss[:, :], qss[:, :], 1.0 / DH, 1e-6, ALU.mult, ALU.add).then_inc(*did("q_ms"))
                        dve.wait_ge(*seen(b, "q_rms"))
                        link(V_.tensor_tensor(q2[:, :].rearrange("p (h d) -> p h d", h=H),
                                              qn[:, :].rearrange("p (h d) -> p h d", h=H),
                                              qss[:, :].unsqueeze(2).to_broadcast([T, H, DH]), ALU.mult))
                        V_.tensor_tensor(qn[:, :], q2[:, :], gqk[0:T, 0, :], ALU.mult).then_inc(*did("q_ready", l))
                    else:
                        V_.tensor_tensor(qn[:, :], bank[6][0:T, 0:D], w["bq", l][0:T, :], ALU.add
                                         ).then_inc(*did("q_ready", l))
                    dve.wait_ge(*seen(b, "qT", l))
                    for e in (0, 1):
                        link(V_.tensor_scalar(qm[:, e * T:(e + 1) * T], qTf[:, :], parity[:, e:e + 1], None, ALU.mult))
                    link(V_.tensor_copy(Qp[:, 0, :], qm[:, :]))
                    link(V_.tensor_tensor(qm[:, :], qm[:, :], Qp[:, 0, :], ALU.subtract))
                    link(V_.tensor_copy(Qp[:, 1, :], qm[:, :]))
                    V_.tensor_tensor(Qp[:, 2, :], qm[:, :], Qp[:, 1, :], ALU.subtract).then_inc(*did("q_parts", l))

                def maxima(l, g):
                    for k in range(12):
                        i, ch = divmod(k, NCH)
                        n = g * 12 + k
                        dve.wait_ge(*seen(b, "max_scores", l, n))
                        V_.reduce_max(mxp[:, GH * g + i, ch:ch + 1], bank[3 + n % 2][0:T, 0:CH], AX
                                      ).then_inc(*did("max_chunk", l, n))
                        if l == 1 and g >= 2 and k == 3:
                            sums_out(g - 2)
                    dve.wait_ge(*seen(b, "max_chunk", l, g * 12 + 11))
                    flat = MZ[:, :, :, :].rearrange("t p e k -> t (p e k)")
                    for p in (2 * g, 2 * g + 1):
                        V_.tensor_reduce(flat[:, 6 * p + 1:6 * p + 6:4],
                                         mxp[:, 2 * p:2 * p + 2, :], AX, ALU.max, negate=True
                                         ).then_inc(*did("maxima", l, g))

                def sums_out(g):
                    dve.wait_ge(*seen(b, "p_sums", g))
                    if g > 0:
                        dve.wait_ge(*seen(b, "heads", 1, g - 1))
                    link(V_.reciprocal(Un, bank[6][:, 0:GW]))
                    dve.wait_ge(*seen(b, "values", 1, g, CT - 1))
                    V_.tensor_tensor(Un, bank[5][:, 0:GW], Un, ALU.mult).then_inc(*did("u_ready", g))

                def ranks(src, groups, n, keep, dst):
                    m = groups * n * n
                    gt = cmp[:, 0, 0:m].rearrange("t (g i j) -> t g i j", g=groups, i=n)
                    eq = cmp[:, 1, 0:m].rearrange("t (g i j) -> t g i j", g=groups, i=n)
                    s3 = src.rearrange("t (g n) -> t g n", g=groups)
                    other = s3.unsqueeze(2).to_broadcast([T, groups, n, n])
                    own = s3.unsqueeze(3).to_broadcast([T, groups, n, n])
                    V_.tensor_tensor(gt, other, own, ALU.is_gt)
                    link(V_.tensor_tensor(eq, other, own, ALU.is_equal))
                    link(V_.tensor_tensor(eq, eq, earlier[0:T, 0:n, 0:n].unsqueeze(1).to_broadcast([T, groups, n, n]),
                                          ALU.mult))
                    link(V_.tensor_tensor(cmp[:, 0, 0:m], cmp[:, 0, 0:m], cmp[:, 1, 0:m], ALU.add))
                    link(V_.reduce_sum(rank[:, 0:groups * n],
                                       cmp[:, 0, 0:m].rearrange("t (g j) -> t g j", j=n), AX))
                    link(V_.tensor_scalar(dst, rank[:, 0:groups * n], float(keep) - 0.5, None, ALU.is_lt))

                def experts(l):
                    e, ni, _ = MOE[l]
                    norm(2 * l + 1)
                    dve.wait_ge(*seen(b, "logits", l))
                    link(V_.tensor_copy(lg[:, 0:e], bank[6][0:T, 0:e]))
                    V_.tensor_reduce(small[:, 0:1], lg[:, 0:e], AX, ALU.max, negate=True).then_inc(*did("top", l))
                    dve.wait_ge(*seen(b, "route_exp", l))
                    link(V_.reduce_sum(small[:, 1:2], ex[:, 0:e], AX))
                    link(V_.reciprocal(small[:, 2:3], small[:, 1:2]))
                    link(V_.tensor_scalar(ex[:, 0:e], ex[:, 0:e], small[:, 2:3], None, ALU.mult))
                    if l == 0:
                        link(V_.reduce_max(gsc[:, 0:4], ex[:, 0:8].rearrange("t (g n) -> t g n", g=4), AX))
                        ranks(gsc[:, 0:4], 1, 4, 2, gsc[:, 8:12])
                        link(V_.tensor_tensor(ex[:, 0:8].rearrange("t (g n) -> t g n", g=4),
                                              ex[:, 0:8].rearrange("t (g n) -> t g n", g=4),
                                              gsc[:, 8:12].unsqueeze(2).to_broadcast([T, 4, 2]), ALU.mult))
                    ranks(ex[:, 0:e], 1, e, 4 if l == 2 else 2, msk[:, 0:e])
                    link(V_.tensor_tensor(ex[:, 0:e], ex[:, 0:e], msk[:, 0:e], ALU.mult))
                    if l == 3:
                        dve.sem_inc(*did("kept"))
                        dve.wait_ge(*seen(b, "position"))
                        link(V_.tensor_scalar(rank[:, 0:8], bank[6][0:T, 16:24], CAPACITY - 0.5, 0.5, ALU.is_lt, ALU.mult))
                        link(V_.tensor_tensor(acnt[:, :], acnt[:, :], msk[:, 0:8], ALU.add))
                        V_.tensor_tensor(comb[:, 0:e], ex[:, 0:e], rank[:, 0:e], ALU.mult).then_inc(*did("comb", l))
                    else:
                        link(V_.reduce_sum(small[:, 1:2], ex[:, 0:e], AX))
                        link(V_.reciprocal(small[:, 2:3], small[:, 1:2]))
                        V_.tensor_scalar(comb[:, 0:e], ex[:, 0:e], small[:, 2:3], 0.5, ALU.mult, ALU.mult
                                         ).then_inc(*did("comb", l))
                    for ck in range(ni // 4):
                        base = 3 * (ck % 2)
                        h_ = hm[ck % 2]
                        dve.wait_ge(*seen(b, "tanh", l, ck))
                        if ck >= 2:
                            dve.wait_ge(*seen(b, "down", l, ck - 2))
                        link(V_.scalar_tensor_tensor(h_, th[ck % 2], 1.0, bank[base + 1][:, 0:GW], ALU.add, ALU.mult))
                        link(V_.tensor_tensor(h_, h_, bank[base][:, 0:GW], ALU.mult))
                        dve.wait_ge(*seen(b, "weighed", l, ck))
                        V_.tensor_tensor(h_, h_, bank[base + 2][:, 0:GW], ALU.mult).then_inc(*did("hidden", l, ck))
                    dve.wait_ge(*seen(b, "down", l, ni // 4 - 1))
                    V_.tensor_tensor(x[:, :], x[:, :], bank[7][0:T, 0:D], ALU.add).then_inc(*did("x_out", 2 * l + 1))
                    dve.wait_ge(*seen(b, "x_out", 2 * l + 1))

                def switch():
                    norm(3)
                    dve.wait_ge(*seen(b, "gates_ps"))
                    V_.tensor_scalar(lg[:, 0:80], bank[6][0:T, 0:80], 17.0, None, ALU.min).then_inc(*did("gates_z"))
                    dve.wait_ge(*seen(b, "gates_z"))
                    ranks(lg[:, 0:80], 16, 5, SK, msk[:, 0:80])
                    dve.wait_ge(*seen(b, "gates_exp"))
                    link(V_.tensor_scalar(ex[:, 0:80], ex[:, 0:80], 1.0, None, ALU.add))
                    link(V_.reciprocal(ex[:, 0:80], ex[:, 0:80]))
                    link(V_.tensor_tensor(comb[:, 0:80], ex[:, 0:80], msk[:, 0:80], ALU.mult))
                    n = 0
                    for which, dst in ((0, sq), (1, sk), (2, sv)):
                        off = 40 if which == 0 else 0
                        for k in range(5):
                            dve.wait_ge(*seen(b, "switch_ps", n))
                            V_.tensor_tensor(prod[:, k * 512:(k + 1) * 512].rearrange("t (a d) -> t a d", a=8),
                                             bank[n % 5][0:T, :].rearrange("t (a d) -> t a d", a=8),
                                             comb[:, off + 8 * k:off + 8 * k + 8].unsqueeze(2).to_broadcast([T, 8, SD]),
                                             ALU.mult).then_inc(*did("gated", n))
                            n += 1
                        dve.wait_ge(*seen(b, "gated", n - 1))
                        V_.reduce_sum(dst.rearrange("t (h d) -> t h d", h=SH),
                                      prod.rearrange("t (h e d) -> t h d e", h=SH, e=SE), AX
                                      ).then_inc(*did("switch_sum", which))
                        dve.wait_ge(*seen(b, "switch_sum", which))
                    for n in (0, 1):
                        dve.wait_ge(*seen(b, "self_scores", n))
                        s3 = bank[n][0:T, 0:400].rearrange("t (h k) -> t h k", h=4)
                        link(V_.reduce_max(small[:, 0:4], s3, AX))
                        V_.tensor_tensor(sc.rearrange("t (j e k) -> t j e k", j=4, e=2)[:, :, n, :], s3,
                                         small[:, 0:4].unsqueeze(2).to_broadcast([T, 4, T]), ALU.subtract
                                         ).then_inc(*did("self_shifted", n))
                        dve.wait_ge(*seen(b, "self_shifted", n))
                    dve.wait_ge(*seen(b, "self_exp"))
                    link(V_.reduce_sum(rsum[:, 0:8], sc.rearrange("t (h k) -> t h k", h=SH), AX))
                    link(V_.reciprocal(rsum[:, 0:8], rsum[:, 0:8]))
                    dve.wait_ge(*seen(b, "self_out"))
                    link(V_.tensor_tensor(so.rearrange("t (h d) -> t h d", h=SH),
                                          bank[4][0:T, :].rearrange("t (h d) -> t h d", h=SH),
                                          rsum[:, 0:8].unsqueeze(2).to_broadcast([T, SH, SD]), ALU.mult))
                    for h in range(SH):
                        ins = V_.tensor_tensor(prod[:, h * 320:(h + 1) * 320].rearrange("t (e d) -> t e d", e=SE),
                                               so[:, h * SD:(h + 1) * SD].unsqueeze(1).to_broadcast([T, SE, SD]),
                                               msk[:, 40 + 5 * h:45 + 5 * h].unsqueeze(2).to_broadcast([T, SE, SD]),
                                               ALU.mult)
                    link(ins)
                    V_.reduce_sum(sz, prod.rearrange("t (h n) -> t n h", h=SH), AX).then_inc(*did("switch_z"))
                    add_y(3, bank[7][0:T, 0:D])

                for l in range(4):
                    if l == 0:
                        dve.wait_ge(*seen(b, "mask_in"))
                        V_.tensor_scalar(absent[:, :], mask_in, 0.0, None, ALU.is_equal).then_inc(*did("absent"))
                        dve.wait_ge(*seen(b, "mrow_in"))
                        V_.tensor_scalar(mrow[:, :], mrow_in[:, :], 0.0, NEG, ALU.is_equal, ALU.mult
                                         ).then_inc(*did("mrow_ready"))
                        dve.wait_ge(*seen(b, "x_in"))
                    if l != 1:
                        dve.wait_ge(*once(f"weights_in{l}"))
                        prep(l)
                        v_bias(l)
                    norm(2 * l)
                    if l != 1:
                        q_path(l)
                    maxima(l, 0)
                    for g in range(GROUPS):
                        if g + 1 < GROUPS:
                            maxima(l, g + 1)
                    if l == 1:
                        sums_out(GROUPS - 2)
                        sums_out(GROUPS - 1)
                    if l != 1:
                        dve.wait_ge(*seen(b, "heads", l, GROUPS - 1))
                        o3 = bank[6][0:T, 0:H * VW].rearrange("t (h d) -> t h d", h=H)
                        link(V_.reciprocal(rsum[:, :], o3[:, :, DH:VW].rearrange("t h d -> t (h d)")))
                        V_.tensor_tensor(attn[:, :].rearrange("t (h d) -> t h d", h=H), o3[:, :, 0:DH],
                                         rsum[:, :].unsqueeze(2).to_broadcast([T, H, DH]), ALU.mult
                                         ).then_inc(*did("attn", l))
                        dve.wait_ge(*seen(b, "attnT_ps", l))
                        V_.tensor_copy(attnT[:, :], bank[7][:, 0:T]).then_inc(*did("attnT", l))
                        add_y(2 * l, bank[6][0:T, 0:D], w["bo", l][0:T, :])
                        experts(l)
                    else:
                        add_y(2, bank[6][0:T, 0:D])
                        switch()
        return st.count, st.mark


def layout(i):
    import numpy as np
    f = np.float32
    r = lambda v: np.ascontiguousarray(v)
    wide = lambda v: r(np.broadcast_to(np.asarray(v)[None, :], (128, v.shape[0])))
    rows = np.minimum(np.arange(SP_), S - 1)
    ctx = np.asarray(i["ctx_1024"])[:, rows]
    a = {
        "x": r(i["x"]),
        "ctxT": r(ctx.transpose(0, 2, 1)),
        "ctxN": r(ctx.reshape(B, CT, CW, D).transpose(0, 2, 1, 3)),
        "mask": r(np.asarray(i["mask_BxSxS2_if1"])[:, :, rows]),
        "ident": np.eye(128, dtype=f),
        "ones_": None,
    }
    del a["ones_"]
    m = np.zeros((B, 1, SP_), np.uint8)
    m[:, 0, :S] = np.asarray(i["mask_BxS2_bk0"]).view(np.uint8)
    a["mrow"] = m.view(np.int32)
    p = np.arange(128)
    a["headsum"] = (p[:, None] // DH == p[None, :] // DH).astype(f)
    picks = np.zeros((128, GH, VW), f)
    for k in range(GH):
        for d in range(VW):
            picks[p % 32 == (VW * k if k < 3 else 0) + d, k, d] = 1
    a["picks"] = picks
    a["parity"] = np.stack([(p // DH) % 2 == 0, (p // DH) % 2 == 1], 1).astype(f)
    a["before"] = (p[:, None] < p[None, :]).astype(f)
    q = np.arange(16)
    a["earlier"] = r(np.broadcast_to((q[None, :] < q[:, None]).astype(f)[None], (128, 16, 16)))
    pad = np.zeros((1, SP_), f)
    pad[:, S:] = NEG
    a["padrow_f"] = pad

    def values(v):
        v = v.reshape(v.shape[0], H, DH)
        return r(np.concatenate([v, np.zeros((v.shape[0], H, 1), f)], 2).reshape(v.shape[0], H * VW))

    def value_bias(v):
        v = v.reshape(1, H, DH)
        v = np.concatenate([v, np.ones((1, H, 1), f)], 2).reshape(H * VW)
        return wide(v)

    for l, wq, bq, wk, bk, wv, bv, wo in (
        (0, i["L0_xattn_Wq"].T, i["L0_xattn_bq"], i["L0_xattn_Wkv"][:128].T, i["L0_xattn_bkv"][:128],
         i["L0_xattn_Wkv"][128:].T, i["L0_xattn_bkv"][128:], i["L0_xattn_Wo"].T),
        (2, i["L2_xattn_Wq"], i["L2_xattn_bq"], i["L2_xattn_Wk"], i["L2_xattn_bk"],
         i["L2_xattn_Wv"], i["L2_xattn_bv"], i["L2_xattn_Wo"]),
        (3, i["L3_xattn_Wq"].T, i["L3_xattn_bq"], i["L3_xattn_Wk"].T, i["L3_xattn_bk"],
         i["L3_xattn_Wv"].T, i["L3_xattn_bv"], i["L3_xattn_Wo"].T),
    ):
        a[f"wq{l}"], a[f"wk{l}"], a[f"wo{l}"] = r(wq), r(wk), r(wo)
        a[f"wv{l}"] = values(np.asarray(wv))
        a[f"bq{l}"], a[f"bo{l}"] = wide(bq), wide(i[f"L{l}_xattn_bo"])
        a[f"bk{l}"] = r(np.asarray(bk)[:, None])
        a[f"bv{l}"] = value_bias(np.asarray(bv))
    a["gqk"] = r(np.stack([wide(i["L0_xattn_gq"].reshape(128)), wide(i["L0_xattn_gk"].reshape(128))], 1))

    def in_rows(v):
        return r(v.reshape(-1, 128, v.shape[1]).transpose(1, 0, 2))

    w13 = i["L0_ffn_w13_weight"]
    a["gw0"] = r(i["L0_ffn_gate_w"].T)
    a["wa0"] = r(w13[:, :256].reshape(-1, 128).T)
    a["wb0"] = r(w13[:, 256:].reshape(-1, 128).T)
    a["w20"] = in_rows(i["L0_ffn_w2_weight"].transpose(0, 2, 1).reshape(-1, 128))
    a["gw2"] = r(i["L2_ffn_gate_w"].T)
    a["wa2"] = r(i["L2_ffn_w1"].transpose(1, 0, 2).reshape(128, -1))
    a["wb2"] = r(i["L2_ffn_w3"].transpose(1, 0, 2).reshape(128, -1))
    a["w22"] = in_rows(i["L2_ffn_w2"].reshape(-1, 128))
    fc = i["L3_ffn_c_fc"]
    a["gw3"] = r(i["L3_ffn_w_gate"])
    a["wa3"] = r(fc[:, :, :192].transpose(1, 0, 2).reshape(128, -1))
    a["wb3"] = r(fc[:, :, 192:].transpose(1, 0, 2).reshape(128, -1))
    a["w23"] = in_rows(i["L3_ffn_c_proj"].reshape(-1, 128))
    a["wq1"] = r(i["L1_xattn_Wq"])
    a["wk1"] = r(i["L1_xattn_Wk"].T.reshape(8, 128, 128).transpose(1, 0, 2).reshape(128, 1024))
    a["wv1"] = r(i["L1_xattn_Wv"])
    a["wo1"] = r(i["L1_xattn_Wo"].reshape(8, 128, 128).transpose(1, 0, 2).reshape(128, 1024))
    a["swd"] = r(np.concatenate([i["L1_ffn_Ws"], i["L1_ffn_Wd"]], 1))
    a["swq"] = r(i["L1_ffn_Wq"])
    a["swk"] = r(i["L1_ffn_Wkv"][:, :SQ])
    a["swv"] = r(i["L1_ffn_Wkv"][:, SQ:])
    wo = i["L1_ffn_Wo"].reshape(64, SE, 128).transpose(1, 0, 2).reshape(320, 128)
    wo = np.concatenate([wo, np.zeros((64, 128), f)], 0)
    a["swo"] = in_rows(wo)
    return a


def kernel(**inputs):
    import ml_dtypes
    import numpy as np
    import concourse.bacc as bacc
    from concourse.bass_utils import run_bass_kernel_spmd

    arrays = layout({k: np.asarray(v) for k, v in inputs.items()})
    arrays["padrow"] = arrays.pop("padrow_f").astype(ml_dtypes.bfloat16)
    known = None
    for _ in range(2):
        nc = bacc.Bacc("TRN2", target_bir_lowering=False, num_devices=1)
        a = {n: nc.dram_tensor(f"in_{n}", v.shape, mybir.dt.from_np(v.dtype), kind="ExternalInput").ap()
             for n, v in arrays.items()}
        a["scratch_k"] = nc.dram_tensor("scratch_k", (128, PARTS, SP_), BF16, kind="Internal").ap()
        a["scratch_q"] = nc.dram_tensor("scratch_q", (128, PARTS, 2 * T), BF16, kind="Internal").ap()
        a["out"] = nc.dram_tensor("out_x", (B, T, D), F32, kind="ExternalOutput").ap()
        known = build(nc, a, known)
    r = run_bass_kernel_spmd(nc, [{f"in_{n}": v for n, v in arrays.items()}], core_ids=[0])
    return r.results[0]["out_x"]
```

```python
from contextlib import ExitStack

import concourse.bass as bass
from concourse import mybir

F32 = mybir.dt.float32
BF16 = mybir.dt.bfloat16
I32 = mybir.dt.int32
U8 = mybir.dt.uint8
ALU = mybir.AluOpType
ACT = mybir.ActivationFunctionType
AX = mybir.AxisListType.X

B = 8
T = 100
D = 128
S = 1444
H = 16
CT = 12
CW = 121
SP_ = CT * CW
NCH = 3
CH = SP_ // NCH
PAIRS = H // 2
DH = 8
GROUPS = 4
GH = H // GROUPS
GW = GH * T
VW = DH + 1
PARTS = 3
K_SEQ = (0, 1, 2, 0, 1, 0)
Q_SEQ = (0, 0, 0, 1, 1, 2)
STACK = 6 * 16
BIAS_ROW = STACK
SHIFT_ROW = STACK + 1
ROWS = STACK + 3
NEG = -float(2 ** 30)
P_SLOTS = 8
SMALL = (0, 2, 3)
NEXT_SMALL = {0: 2, 2: 3, 3: 0}
V_BANKS = (3, 4, 0, 1)
LEAD = 4


def max_bank(n):
    return (3, 4, 0, 1, 2)[n % 5] if n < GH * NCH else 3 + n % 2


MOE = {
    0: (8, 16, lambda half: half // 4),
    2: (16, 8, lambda half: half),
    3: (8, 12, lambda half: half // 3),
}
CAPACITY = 512
SH, SE, SD, SK = 8, 5, 64, 3
SQ = SH * SE * SD


class Steps:

    def __init__(self, nc, ctx, known):
        self.nc, self.ctx, self.known = nc, ctx, known
        self.sems, self.count, self.mark = {}, {}, {}
        self.before_loop, self.others, self.first = {}, set(), {}

    def sem(self, name):
        if name not in self.sems:
            self.sems[name] = self.ctx.enter_context(self.nc.semaphore(name))
        return self.sems[name]

    def engine(self):
        self.others = set(self.count)

    def loop(self):
        for name, n in self.count.items():
            if name not in self.others:
                self.before_loop[name] = n
        self.first.update({k: v for k, v in self.mark.items() if k[0] not in self.others})

    def result(self):
        return ({n: c - self.before_loop.get(n, 0) for n, c in self.count.items()},
                dict(self.mark), dict(self.first))

    def did(self, name, *key, by=1):
        self.count[name] = self.count.get(name, 0) + by
        self.mark[(name,) + key] = self.count[name]
        return self.sem(name), by

    def seen(self, turn, name, *key):
        if turn is None:
            return self.once(name, *key)
        if not self.known:
            return self.sem(name), turn * 2 + 1
        return self.sem(name), turn * self.known[0][name] + self.known[1][(name,) + key]

    def ahead(self, turn, name, *key):
        if not self.known:
            return self.sem(name), turn * 2 + 1
        totals, marks, first = self.known
        assert marks[(name,) + key] == first[(name,) + key] + totals[name]
        return self.sem(name), turn * totals[name] + first[(name,) + key]

    def once(self, name, *key):
        return self.sem(name), self.known[2][(name,) + key] if self.known else 1


def build(nc, a, known):
    with ExitStack() as ctx:
        st = Steps(nc, ctx, known)
        did, seen, ahead, once = st.did, st.seen, st.ahead, st.once

        def sb(name, shape, dt=F32):
            return ctx.enter_context(nc.sbuf_tensor(name, shape, dt))

        ident = sb("ident", [128, 128])
        identb = sb("identb", [128, 128], BF16)
        headsum = sb("headsum", [128, 128])
        picks = sb("picks", [128, GH, VW])
        eps6 = sb("eps6", [128, 1])
        own_dims = sb("own_dims", [128, 2, 16])
        before = sb("before", [128, 128])
        earlier = sb("earlier", [128, 16, 16])
        ones = sb("ones", [128, 128])
        half_power = sb("half_power", [128, 16])
        neg_eye = sb("neg_eye", [128, GH, T], BF16)
        w = {}
        for l in SMALL:
            for n, c in (("wq", 128), ("wk", 128), ("wv", H * VW), ("wo", 128),
                         ("bq", 128), ("bk", 1), ("bv", H * VW), ("bo", 128)):
                w[n, l] = sb(f"{n}{l}", [128, c])
            e, ni, _ = MOE[l]
            w["gw", l] = sb(f"gw{l}", [128, e])
            w["wa", l] = sb(f"wa{l}", [128, ni * 128])
            w["wb", l] = sb(f"wb{l}", [128, ni * 128])
            w["w2", l] = sb(f"w2{l}", [128, ni, 128])
        for n in ("wq", "wk", "wv", "wo"):
            w[n, 1] = sb(f"{n}1", [128, 1024])
        gqk = sb("gqk", [128, 2, 128])
        swd = sb("swd", [128, 2 * SH * SE])
        swqv = sb("swqv", [128, SQ])
        swk = sb("swk", [128, SQ])
        swo = sb("swo", [128, 3, 128])

        x = sb("x", [T, D])
        x_next = sb("x_next", [T, D])

        xn = sb("xn", [T, D])
        xnT = sb("xnT", [128, T])
        bn = sb("bn", [T, 6])
        mv = sb("mv", [T, 2])
        rstd = sb("rstd", [T, 1])
        ctxT = sb("ctxT", [128, SP_])
        ctxN = sb("ctxN", [CW, CT, D])
        ctxTb = sb("ctxTb", [128, SP_], BF16)
        absent = sb("absent", [T, SP_], BF16)
        Kf = sb("Kf", [128, SP_])
        Kp = sb("Kp", [128, PARTS, SP_], BF16)
        ktmp = Kp[:, :, :].rearrange("p a n -> p (a n)").bitcast(F32)[:, 0:SP_]
        KS = sb("KS", [128, PAIRS, SP_], BF16)
        QS = sb("QS", [128, PAIRS, 2 * T], BF16)
        V = sb("V", [CW, CT, 168])
        qn = sb("qn", [T, D])
        qss = sb("qss", [T, H])
        Qz = Kf[0:T, 0:768].bitcast(BF16).rearrange("t (h s r) -> t h s r", h=H, s=6)
        qm = Kf[0:T, 768:1024].rearrange("t (h r) -> t h r", h=H)
        mxp = sb("mxp", [T, H, NCH])
        MZ = sb("MZ", [T, PAIRS, 2, 3], BF16)
        rsum = sb("rsum", [T, H])
        attn = sb("attn", [T, D])
        q2 = attn
        attnT = sb("attnT", [128, T])
        yb = sb("yb", [T, D])
        x_last = yb
        acnt = sb("acnt", [T, 8])
        lg = sb("lg", [T, 80])
        ex = sb("ex", [T, 80])
        gsc = sb("gsc", [T, 16])
        small = sb("small", [T, 4])
        msk = sb("msk", [T, 80])
        comb = sb("comb", [T, 80])
        rank = sb("rank", [T, 80])
        ARENA = 6800
        arena = sb("arena", [128, ARENA])
        P = arena[:, 0:P_SLOTS * GW].rearrange("p (s n) -> p s n", s=P_SLOTS)
        qt = arena[:, 3200:4800]
        qtb = arena[:, 4800:5600].bitcast(BF16)
        accP = arena[:, 5600:6400].rearrange("p (s n) -> p s n", s=2)
        Osb = arena[:, 6400:6800]
        cmp = arena[0:T, 5696:6496].rearrange("t (a n) -> t a n", a=2)
        mrow_in = arena[0:1, 3200:3200 + SP_ // 4]
        mrow = arena[0:1, 4672:4672 + SP_ // 2].bitcast(BF16)
        mask_in = arena[0:T, 3200:3200 + SP_].bitcast(I32)
        qTh = Kf[:, 0:800]
        oT = Kf[:, 0:800]
        Un = Osb
        prod = arena[0:T, 0:SQ]
        sq = arena[0:T, 2560:3072]
        sk = arena[0:T, 3072:3584]
        sv = arena[0:T, 3584:4096]
        sqT = arena[:, 4096:4496]
        skT = arena[:, 4496:4896]
        sc = arena[0:T, 4896:5696]
        pT = arena[0:T, 5696:6496]
        so = sq
        sz = arena[0:T, 3072:3392]
        szT = arena[:, 6496:6796]
        th = [arena[:, 400 * i:400 * i + 400] for i in (0, 1)]
        hm = [arena[:, 400 * i:400 * i + 400] for i in (2, 3)]

        bank = [ctx.enter_context(nc.psum_tensor(f"bank{i}", [128, 512], F32)) for i in range(8)]
        as_bf16 = [bank[i][:, :].bitcast(BF16) for i in range(8)]
        b7b = as_bf16[7]
        scratch_k = a["scratch_k"]

        def once_now(name):
            return st.sem(name), st.count[name]

        block = ctx.enter_context(nc.Block())

        @block.sync
        def _(sp):
            st.engine()
            for t, n in ((ctxT[:, :], "ctxT"),):
                sp.dma_start(t, a[n][0]).then_inc(*did(f"{n}_in", by=16))
            sp.dma_start(mrow_in.bitcast(I32), a["mrow"][0]).then_inc(*did("mrow_in", by=16))
            sp.dma_start(x_next[:, :], a["x"][0]).then_inc(*did("x_in", by=16))
            for t, n in ((ident, "ident"), (headsum, "headsum"), (picks, "picks"), (own_dims, "own_dims"),
                         (before, "before"), (earlier, "earlier"), (gqk, "gqk")):
                sp.dma_start(t[...], a[n]).then_inc(*did("const_in", by=16))

            def load(n, l):
                sp.dma_start(w[n, l][...], a[f"{n}{l}"]).then_inc(*did(f"weights_in{l}", by=16))
            for n in ("wq", "wk", "wv", "wo", "bq", "bk", "bv", "bo", "gw", "wa", "wb", "w2"):
                load(n, 0)
            b = None

            def inputs(src):
                sp.dma_start(ctxT[:, :], src("ctxT")).then_inc(*did("ctxT_in", by=16))
                sp.dma_start(mrow_in.bitcast(I32), src("mrow")).then_inc(*did("mrow_in", by=16))
                sp.dma_start(x_next[:, :], src("x")).then_inc(*did("x_in", by=16))

            def k_stack(l, prev):
                sp.wait_ge(*seen(b, "k_parts", l))
                sp.dma_start(scratch_k, Kp[:, :, :]).then_inc(*did("k_out", l, by=16))
                if prev is not None:
                    sp.wait_ge(*seen(b, "scores", "end", prev))
                    sp.sem_inc(st.sem("sync_passed"), 1)
                if l == 0:
                    sp.wait_ge(*seen(b, "mrow_ready"))
                    sp.dma_start(KS[BIAS_ROW:BIAS_ROW + 1, :, :],
                                 mrow[:, :].unsqueeze(1).to_broadcast([1, PAIRS, SP_])
                                 ).then_inc(*did(f"k_stacked{l}", by=16))
                sp.wait_ge(*seen(b, "k_out", l))
                for s, part in enumerate(K_SEQ):
                    sp.dma_start(KS[16 * s:16 * s + 16, :, :],
                                 scratch_k[:, part, :].rearrange("(p r) n -> r p n", r=16)
                                 ).then_inc(*did(f"k_stacked{l}", by=16))

            k_stack(0, None)
            for n in ("wq", "wk", "wv", "wo"):
                load(n, 1)
            for t, n in ((swd, "swd"), (swk, "swk"), (swo, "swo")):
                sp.dma_start(t[...], a[n]).then_inc(*did("weights_in1", by=16))
            for l in (2, 3):
                for n in ("wq", "wk", "wv", "wo", "bq", "bk", "bv", "bo", "gw", "wa", "wb", "w2"):
                    load(n, l)

            st.loop()
            with sp.Fori(0, B) as b:
                sp.wait_ge(st.sem("turn_open"), b + 1)

                sp.sem_inc(st.sem("sync_passed"), 1)
                sp.dma_start(mask_in, a["mask"][b]).then_inc(*did("mask_in", by=16))
                sp.dma_start(ctxN[:, :, :], a["ctxN"][b]).then_inc(*did("ctxN_in", by=16))
                sp.dma_start(swqv[:, :], a["swq"]).then_inc(*did("swqv_in", "q", by=16))
                sp.wait_ge(*seen(b, "scores", "end", 0))
                sp.dma_start(KS[BIAS_ROW:BIAS_ROW + 1, :, :],
                             a["padrow"].unsqueeze(1).to_broadcast([1, PAIRS, SP_])
                             ).then_inc(*did("bias_row_in", by=16))
                k_stack(2, 0)
                sp.wait_ge(*seen(b, "switch_ps", 4))
                sp.dma_start(swqv[:, :], a["swv"]).then_inc(*did("swqv_in", "v", by=16))
                k_stack(3, 2)
                sp.wait_ge(*seen(b, "v_ps", 3, 3))
                sp.sem_inc(st.sem("sync_passed"), 1)
                inputs(lambda n: a[n][1:][b])
                k_stack(0, 3)
                sp.wait_ge(*seen(b, "x_out", 7))
                sp.sem_inc(st.sem("sync_passed"), 1)
                sp.dma_start(a["out"][b], x_last[:, :]).then_inc(*did("out_stored", by=16))
                sp.wait_ge(*seen(b, "out_stored"))
                sp.sem_inc(st.sem("sync_passed"), 1)
            for name in ("k_stacked0", "x_in", "ctxT_in", "mrow_in"):
                sp.wait_ge(*ahead(B, name))

        @block.gpsimd
        def _(pool):
            st.engine()
            for n, (ap, value) in enumerate((
                    (ones[:, :], 1.0), (half_power[:, :], -0.5), (KS[STACK:ROWS, :, :], 1.0),
                    (QS[STACK:ROWS, :, :], 1.0), (MZ[:, :, :, :], 0.0), (V[:, :, :], 0.0),
                    (acnt[:, :], 0.0), (MZ[:, :, :, 0:1], 1.0))):
                pool.memset(ap, value).then_inc(*did("pool_setup"))
                pool.wait_ge(*once_now("pool_setup"))
            b = None

            def context_bf16():
                pool.wait_ge(*seen(b, "ctxT_in"))
                pool.sem_inc(st.sem("pool_passed"), 1)
                pool.tensor_copy(ctxTb[:, :], ctxT[:, :]).then_inc(*did("ctxTb"))

            context_bf16()
            st.loop()
            with pool.Fori(0, B) as b:
                pool.wait_ge(st.sem("turn_open"), b + 1)

                def power(name, ap, n):
                    pool.tensor_tensor(ap, ap, half_power[0:T, 0:n], ALU.pow).then_inc(*did(*name))

                def norm(k):
                    pool.wait_ge(*seen(b, "ln_var", k))
                    power(("ln_rstd", k), rstd[:, :], 1)

                norm(0)
                pool.wait_ge(*seen(b, "q_ms"))
                power(("q_rms",), qss[:, :], H)
                norm(1)
                norm(2)
                for g in range(GROUPS):
                    for c in range(CT):
                        pool.wait_ge(*seen(b, "exp", 1, g, c))
                        t = g * CT + c
                        dst = accP[0:CW, g % 2, :]
                        if c == 0:
                            if g >= 2:
                                pool.wait_ge(*seen(b, "p_sums", g - 2))
                            pool.sem_inc(st.sem("pool_passed"), 1)
                            pool.tensor_copy(dst, P[0:CW, t % P_SLOTS, :]).then_inc(*did("p_added", g, c))
                        else:
                            pool.wait_ge(*seen(b, "p_added", g, c - 1))
                            pool.tensor_tensor(dst, dst, P[0:CW, t % P_SLOTS, :], ALU.add).then_inc(*did("p_added", g, c))
                for k in range(3, 8):
                    if k == 7:
                        context_bf16()
                    norm(k)

        @block.tensor
        def _(pe):
            st.engine()
            pe.wait_ge(*once("pool_setup"))
            pe.wait_ge(*once("const_in"))
            pe.wait_ge(*once("setup_bf16"))
            b = None

            def k_chunk(l, ch):
                pe.matmul(bank[5 + ch][:, 0:CH], w["wk", l][:, :], ctxT[:, ch * CH:(ch + 1) * CH],
                          start=True, stop=True).then_inc(*did("k_ps", l, ch))

            def k_squares(ch):
                pe.wait_ge(*seen(b, "k_squared", ch))
                pe.matmul(bank[5 + ch][:, 0:CH], headsum[:, :], ktmp[:, ch * CH:(ch + 1) * CH],
                          start=True, stop=True).then_inc(*did("k_ss", ch))

            def v_proj(l):
                for c in range(CT):
                    mm = pe.matmul(bank[V_BANKS[c // 3]][0:CW, (c % 3) * 144:(c % 3) * 144 + 144],
                                   ctxT[:, c * CW:(c + 1) * CW], w["wv", l][:, :], start=True, stop=True)
                    if c % 3 == 2:
                        mm.then_inc(*did("v_ps", l, c // 3))

            pe.wait_ge(*once("weights_in0"))
            pe.wait_ge(*once("ctxT_in"))
            for ch in range(NCH):
                k_chunk(0, ch)
            for ch in range(NCH):
                k_squares(ch)
            v_proj(0)
            st.loop()
            with pe.Fori(0, B) as b:
                pe.wait_ge(st.sem("turn_open"), b + 1)

                def norm_T(k):
                    pe.wait_ge(*seen(b, "xn", k))
                    pe.transpose(bank[7][:, 0:T], xn[:, :], ident[0:T, 0:T]).then_inc(*did("xnT_ps", k))
                    pe.wait_ge(*seen(b, "xnT", k))

                def q_small(l):
                    pe.matmul(bank[6][0:T, 0:D], xnT[:, :], w["wq", l][:, :], start=True, stop=True
                              ).then_inc(*did("q_ps", l))
                    pe.wait_ge(*seen(b, "q_parts", l))
                    pe.wait_ge(*seen(b, "q_copied", l))
                    for h in range(H):
                        mm = pe.transpose(as_bf16[h // 8][0:STACK, (h % 8) * T:(h % 8 + 1) * T], Qz[:, h, :, :].rearrange("t s r -> t (s r)"),
                                          identb[0:T, 0:T])
                        if h % 8 == 7:
                            mm.then_inc(*did("qs_ps", l, h // 8))

                def q_wide():
                    for p in range(8):
                        mm = pe.matmul(bank[p // 4][:, (p % 4) * T:(p % 4 + 1) * T],
                                       w["wq", 1][:, p * 128:(p + 1) * 128], xnT[:, :], start=True, stop=True)
                        if p % 4 == 3:
                            mm.then_inc(*did("qh_ps", p // 4))
                    for h in range(H):
                        if h % 8 == 0:
                            pe.wait_ge(*seen(b, "qh", h // 8))
                        r, j = 64 * (h % 2), h // 2
                        mm = pe.matmul(bank[2 + 2 * (h % 2) + j // 4][:, (j % 4) * T:(j % 4 + 1) * T],
                                       w["wk", 1][r:r + 64, (h // 2) * 128:(h // 2 + 1) * 128],
                                       qTh[r:r + 64, (h // 2) * T:(h // 2 + 1) * T], start=True, stop=True)
                        if h % 8 >= 6:
                            mm.then_inc(*did("qt_ps", h // 8, h % 2))

                def max_scores(l, g, k):
                    i, ch = divmod(k, NCH)
                    h = GH * g + i
                    n = g * 12 + k
                    before_ = [m for m in range(n) if max_bank(m) == max_bank(n)]
                    if before_:
                        pe.wait_ge(*seen(b, "max_chunk", l, before_[-1]))
                    dst = bank[max_bank(n)][0:T, 0:CH]
                    cols = slice(ch * CH, (ch + 1) * CH)
                    if l == 1:
                        pe.matmul(dst, qtb[:, h * T:(h + 1) * T], ctxTb[:, cols], start=True, stop=True
                                  ).then_inc(*did("max_scores", l, n))
                        return
                    p, e = h // 2, h % 2
                    if l == 3:
                        pe.matmul(dst, neg_eye[0:T, 0, :], absent[:, cols], start=True, stop=False)
                    pe.matmul(dst, QS[0:BIAS_ROW + 1, p, e * T:(e + 1) * T], KS[0:BIAS_ROW + 1, p, cols],
                              start=(l != 3), stop=True).then_inc(*did("max_scores", l, n))

                def shift_T(l, g):
                    pe.wait_ge(*seen(b, "maxima", l, g))
                    for n in range(4):
                        mm = pe.transpose(b7b[STACK:ROWS, n * T:(n + 1) * T], MZ[:, 2 * g + n // 2, n % 2, :],
                                          identb[0:T, 0:T])
                    mm.then_inc(*did("shift_ps", l, g))

                def scores(l, g, c):
                    t = g * CT + c
                    if c == 0:
                        pe.wait_ge(*seen(b, "shift", l, g))
                    if t >= 3:
                        pe.wait_ge(*seen(b, "exp", l, (t - 3) // CT, (t - 3) % CT))
                    bk = bank[t % 3]
                    cols = slice(c * CW, (c + 1) * CW)
                    if l == 1:
                        pe.matmul(bk[0:CW, 0:GW], ctxT[:, cols], qt[:, g * GW:(g + 1) * GW], start=True, stop=False)
                        mm = pe.matmul(bk[0:CW, 0:GW], KS[STACK:ROWS, 0, cols], QS[STACK:ROWS, 2 * g:2 * g + 2, :],
                                       start=False, stop=True)
                    else:
                        if l == 3:
                            pe.matmul(bk[0:CW, 0:GW], absent[:, cols], neg_eye[0:T, :, :], start=True, stop=False)
                        for p in (0, 1):
                            mm = pe.matmul(bk[0:CW, 2 * T * p:2 * T * (p + 1)], KS[0:ROWS, 2 * g + p, cols],
                                           QS[0:ROWS, 2 * g + p, :], start=(l != 3), stop=(l != 3 or p == 1))
                    mm.then_inc(*did("scores", l, g, c))
                    if t == GROUPS * CT - 1:
                        st.mark["scores", "end", l] = st.count["scores"]

                def values(l, g, u):
                    pe.wait_ge(*seen(b, "exp", l, g, 4 * u + 3))
                    if u == 0 and g > 0:
                        pe.wait_ge(*(seen(b, "u_ready", g - 1) if l == 1 else seen(b, "o_copied", l, g - 1)))
                    if l == 1:
                        for r in range(4):
                            c = 4 * u + r
                            mm = pe.matmul(bank[5][:, 0:GW], ctxN[:, c, :], P[0:CW, (g * CT + c) % P_SLOTS, :],
                                           start=(c == 0), stop=(c == CT - 1))
                            mm.then_inc(*did("values", l, g, c))
                        return
                    for lo, hi, v0 in ((0, 3 * T, 0), (3 * T, GW, 3 * VW)):
                        for r in range(4):
                            c = 4 * u + r
                            v = GH * VW * g + v0
                            mm = pe.matmul(bank[5][32 * r:32 * r + 32, lo:hi], V[:, c, v:v + 32],
                                           P[0:CW, (g * CT + c) % P_SLOTS, lo:hi],
                                           start=(u == 0 and lo == 0), stop=(u == 2), skip_group_check=True)
                    mm.then_inc(*did("values", l, g, 4 * u + 3))

                def p_sums(g):
                    pe.wait_ge(*seen(b, "p_added", g, CT - 1))
                    pe.matmul(bank[6][:, 0:GW], ones[0:CW, :], accP[0:CW, g % 2, :], start=True, stop=True
                              ).then_inc(*did("p_sums", g))

                def heads_out(l, g):
                    if l == 1:
                        pe.wait_ge(*seen(b, "u_ready", g))
                        for i in range(GH):
                            h = GH * g + i
                            mm = pe.matmul(bank[7][64 * (h % 2):64 * (h % 2) + 64, (i // 2) * T:(i // 2 + 1) * T],
                                           w["wv", 1][:, h * 64:(h + 1) * 64], Un[:, i * T:(i + 1) * T],
                                           start=True, stop=True, skip_group_check=True)
                        mm.then_inc(*did("heads", l, g))
                        return
                    pe.wait_ge(*seen(b, "o_copied", l, g))
                    for i in range(GH):
                        h = GH * g + i
                        mm = pe.matmul(bank[6][0:T, h * VW:(h + 1) * VW], Osb[:, i * T:(i + 1) * T],
                                       picks[:, i, :], start=True, stop=True, skip_group_check=True)
                    mm.then_inc(*did("heads", l, g))

                def cross(l):
                    pe.wait_ge(*once(f"weights_in{l}"))
                    nl = NEXT_SMALL.get(l)
                    if nl is not None:
                        pe.wait_ge(*once(f"weights_in{nl}"))
                    norm_T(2 * l)
                    if l == 1:
                        q_wide()
                        pe.wait_ge(*seen(b, "qt"))
                        pe.wait_ge(*ahead(b, "ctxTb"))
                        pe.wait_ge(*seen(b, "ctxN_in"))
                        pe.wait_ge(*seen(b, "bias_row_in"))
                    else:
                        q_small(l)
                        of = ahead if l == 0 else seen
                        pe.wait_ge(*of(b, f"k_stacked{l}"))
                        pe.wait_ge(*seen(b, "q_stacked", l))
                        pe.wait_ge(*seen(b, "q_stacked_too", l))
                        pe.wait_ge(*of(b, "v_ready", l, 3))
                    if l == 3:
                        pe.wait_ge(*seen(b, "absent"))
                        pe.wait_ge(*seen(b, "ctxT_in"))
                    for n in range(12 + LEAD):
                        if l != 1 and n in (1, 2, 3):
                            k_chunk(nl, n - 1)
                        if l == 3 and n in (6, 7, 8):
                            k_squares(n - 6)
                        max_scores(l, n // 12, n % 12)
                    if l != 1:
                        pe.wait_ge(*seen(b, "k_read", nl))
                    shift_T(l, 0)
                    for g in range(GROUPS):
                        for u in range(3):
                            for c in range(4 * u, 4 * u + 4):
                                scores(l, g, c)
                                n = 12 * (g + 1) + c + LEAD
                                if n < 12 * GROUPS:
                                    max_scores(l, n // 12, n % 12)
                            if u == 2 and g + 1 < GROUPS:
                                if l == 1 and g:
                                    pe.wait_ge(*seen(b, "oT", g - 1))
                                else:
                                    pe.wait_ge(*seen(b, "shift", l, g))
                                shift_T(l, g + 1)
                            if l == 1 and g and u == 0:
                                p_sums(g - 1)
                            if u:
                                values(l, g, u - 1)
                            if g and u == 1:
                                heads_out(l, g - 1)
                        values(l, g, 2)
                    if l != 1:
                        heads_out(l, GROUPS - 1)
                    if l == 1:
                        p_sums(GROUPS - 1)
                        pe.wait_ge(*seen(b, "oT", GROUPS - 2))
                        heads_out(l, GROUPS - 1)
                    if l == 1:
                        pe.wait_ge(*seen(b, "oT", GROUPS - 1))
                        for p in range(8):
                            mm = pe.matmul(bank[6][0:T, 0:D], oT[:, p * T:(p + 1) * T],
                                           w["wo", 1][:, p * 128:(p + 1) * 128], start=(p == 0), stop=(p == 7))
                        mm.then_inc(*did("y_ps", 2 * l))
                        return
                    v_proj(nl)
                    pe.wait_ge(*seen(b, "attn", l))
                    pe.transpose(bank[7][:, 0:T], attn[:, :], ident[0:T, 0:T]).then_inc(*did("attnT_ps", l))
                    pe.wait_ge(*seen(b, "attnT", l))
                    pe.matmul(bank[6][0:T, 0:D], attnT[:, :], w["wo", l][:, :], start=True, stop=True
                              ).then_inc(*did("y_ps", 2 * l))

                def experts(l):
                    e, ni, of_half = MOE[l]
                    norm_T(2 * l + 1)
                    pe.wait_ge(*seen(b, "v_ready", NEXT_SMALL[l], 3))
                    pe.matmul(bank[6][0:T, 0:e], xnT[:, :], w["gw", l][:, :], start=True, stop=True
                              ).then_inc(*did("logits", l))

                    def up(ck):
                        base = 3 * (ck % 2)
                        if ck >= 2:
                            pe.wait_ge(*seen(b, "hidden", l, ck - 2))
                        for n, wn in ((0, "wa"), (1, "wb")):
                            for t in range(4):
                                m = 4 * ck + t
                                mm = pe.matmul(bank[base + n][:, t * T:(t + 1) * T], w[wn, l][:, m * 128:(m + 1) * 128],
                                               xnT[:, :], start=True, stop=True)
                            mm.then_inc(*did("gate_up", l, ck, n))

                    def weigh(ck):
                        base = 3 * (ck % 2)
                        for t in range(4):
                            for s in (0, 1):
                                ex_ = of_half(2 * (4 * ck + t) + s)
                                mm = pe.matmul(bank[base + 2][64 * s:64 * s + 64, t * T:(t + 1) * T],
                                               comb[:, ex_:ex_ + 1].to_broadcast([T, 64]), ident[0:T, 0:T],
                                               start=True, stop=True, skip_group_check=True)
                        mm.then_inc(*did("weighed", l, ck))

                    def down(ck):
                        pe.wait_ge(*seen(b, "hidden", l, ck))
                        for t in range(4):
                            m = 4 * ck + t
                            mm = pe.matmul(bank[7][0:T, 0:D], hm[ck % 2][:, t * T:(t + 1) * T], w["w2", l][:, m, :],
                                           start=(m == 0), stop=(m == ni - 1))
                        mm.then_inc(*did("down", l, ck))

                    up(0)
                    up(1)
                    if l == 3:
                        pe.wait_ge(*seen(b, "kept"))
                        pe.matmul(bank[6][0:T, 16:24], before[0:T, 0:T], msk[:, 0:8], start=True, stop=False)
                        pe.matmul(bank[6][0:T, 16:24], ones[0:T, 0:T], acnt[:, :], start=False, stop=True
                                  ).then_inc(*did("position"))
                    pe.wait_ge(*seen(b, "comb", l))
                    for ck in range(ni // 4):
                        if ck >= 2:
                            up(ck)
                        weigh(ck)
                        if ck:
                            down(ck - 1)
                    down(ni // 4 - 1)

                def switch():
                    norm_T(3)
                    pe.matmul(bank[6][0:T, 0:2 * SH * SE], xnT[:, :], swd[:, :], start=True, stop=True
                              ).then_inc(*did("gates_ps"))
                    n = 0
                    for which in range(3):
                        if which == 0:
                            pe.wait_ge(*seen(b, "swqv_in", "q"))
                        if which == 2:
                            pe.wait_ge(*seen(b, "swqv_in", "v"))
                        src = swk if which == 1 else swqv
                        for k in range(5):
                            if n >= 5:
                                pe.wait_ge(*seen(b, "gated", n - 5))
                            mm = pe.matmul(bank[n % 5][0:T, :], xnT[:, :], src[:, k * 512:(k + 1) * 512],
                                           start=True, stop=True)
                            mm.then_inc(*did("switch_ps", n))
                            n += 1
                    for which, src, bk in ((0, sq, 5), (1, sk, 6)):
                        pe.wait_ge(*seen(b, "switch_sum", which))
                        for c in range(4):
                            mm = pe.transpose(bank[bk][:, c * T:(c + 1) * T], src[:, c * 128:(c + 1) * 128], ident[0:T, 0:T])
                        mm.then_inc(*did("switch_T_ps", which))
                    pe.wait_ge(*seen(b, "switch_T", 1))
                    pe.wait_ge(*seen(b, "gated", 14))
                    for h in range(SH):
                        r = 64 * (h % 2)
                        c = slice((h // 2) * T, (h // 2 + 1) * T)
                        mm = pe.matmul(bank[h % 2][0:T, (h // 2) * T:(h // 2 + 1) * T], sqT[r:r + 64, c], skT[r:r + 64, c],
                                       start=True, stop=True)
                        if h >= 6:
                            mm.then_inc(*did("self_scores", h % 2))
                    pe.wait_ge(*seen(b, "self_exp"))
                    for h in range(SH):
                        mm = pe.transpose(bank[2 + h // 4][0:T, (h % 4) * T:(h % 4 + 1) * T],
                                          sc[:, h * T:(h + 1) * T], ident[0:T, 0:T])
                        if h % 4 == 3:
                            mm.then_inc(*did("self_pT_ps", h // 4))
                    pe.wait_ge(*seen(b, "self_pT", 1))
                    pe.wait_ge(*seen(b, "switch_sum", 2))
                    for h in range(SH):
                        mm = pe.matmul(bank[4][0:T, h * SD:(h + 1) * SD], pT[:, h * T:(h + 1) * T],
                                       sv[:, h * SD:(h + 1) * SD], start=True, stop=True)
                    mm.then_inc(*did("self_out"))
                    pe.wait_ge(*seen(b, "switch_z"))
                    for c in range(3):
                        n = 128 if c < 2 else 64
                        mm = pe.transpose(bank[5][0:n, c * T:(c + 1) * T], sz[:, c * 128:c * 128 + n], ident[0:T, 0:T])
                    mm.then_inc(*did("switch_zT_ps"))
                    pe.wait_ge(*seen(b, "switch_zT"))
                    for c in range(3):
                        n = 128 if c < 2 else 64
                        mm = pe.matmul(bank[7][0:T, 0:D], szT[0:n, c * T:(c + 1) * T], swo[0:n, c, :],
                                       start=(c == 0), stop=(c == 2))
                    mm.then_inc(*did("y_ps", 3))

                for l in range(4):
                    cross(l)
                    if l == 1:
                        switch()
                    else:
                        experts(l)

        @block.scalar
        def _(act):
            st.engine()
            act.wait_ge(*once("pool_setup"))
            act.wait_ge(*once("setup_bf16"))
            b = None

            def next_keys(l):
                if b is not None and l == 0:
                    act.wait_ge(*seen(b, "k_out", 3))
                for ch in range(NCH):
                    cols = slice(ch * CH, (ch + 1) * CH)
                    act.wait_ge(*seen(b, "k_ps", l, ch))
                    if l == 0:
                        act.activation(ktmp[:, cols], bank[5 + ch][:, 0:CH], ACT.Square, bias=w["bk", l][:, 0:1]
                                       ).then_inc(*did("k_squared_first", ch))
                    ins = act.activation(Kf[:, cols], bank[5 + ch][:, 0:CH], ACT.Identity, bias=w["bk", l][:, 0:1])
                    if l == 0:
                        ins.then_inc(*did("k_squared", ch))
                    else:
                        ins.then_inc(*did("k_read", l))
                if l != 0:
                    return
                for ch in range(NCH):
                    cols = slice(ch * CH, (ch + 1) * CH)
                    act.wait_ge(*seen(b, "k_ss", ch))
                    act.activation(ktmp[:, cols], bank[5 + ch][:, 0:CH], ACT.Ln, bias=eps6[:, 0:1], scale=1.0 / DH
                                   ).then_inc(*did("k_read", 0))
                act.wait_ge(*seen(b, "k_read", 0))
                act.activation(ktmp[:, :], ktmp[:, :], ACT.Exp, scale=-0.5).then_inc(*did("k_rms"))

            act.wait_ge(*once("weights_in0"))
            next_keys(0)
            st.loop()
            with act.Fori(0, B) as b:
                act.wait_ge(st.sem("turn_open"), b + 1)

                def shift(l, g):
                    act.wait_ge(*seen(b, "shift_ps", l, g))
                    act.activation(QS[STACK:ROWS, 2 * g:2 * g + 2, :].rearrange("p a n -> p (a n)"),
                                   b7b[STACK:ROWS, 0:GW], ACT.Copy).then_inc(*did("shift", l, g))

                def exps(l):
                    if l != 1:
                        next_keys(NEXT_SMALL[l])
                    shift(l, 0)
                    for g in range(GROUPS):
                        for c in range(CT):
                            t = g * CT + c
                            act.wait_ge(*seen(b, "scores", l, g, c))
                            if t >= P_SLOTS:
                                o = t - P_SLOTS
                                u = (o % CT) if l == 1 else 4 * ((o % CT) // 4) + 3
                                act.wait_ge(*seen(b, "values", l, o // CT, u))
                                if l == 1:
                                    act.wait_ge(*seen(b, "p_added", o // CT, o % CT))
                            act.activation(P[0:CW, t % P_SLOTS, :], bank[t % 3][0:CW, 0:GW], ACT.Exp
                                           ).then_inc(*did("exp", l, g, c))
                            if l == 1 and c == 10 and g > 0:
                                heads_T(g - 1)
                        if g + 1 < GROUPS:
                            shift(l, g + 1)
                        if l != 1:
                            act.wait_ge(*seen(b, "values", l, g, CT - 1))
                            if g > 0:
                                act.wait_ge(*seen(b, "heads", l, g - 1))
                            act.activation(Osb, bank[5][:, 0:GW], ACT.Copy).then_inc(*did("o_copied", l, g))
                    if l == 1:
                        heads_T(GROUPS - 1)
                        return
                    act.wait_ge(*seen(b, "attnT_ps", l))
                    act.activation(attnT[:, :], bank[7][:, 0:T], ACT.Copy).then_inc(*did("attnT", l))

                def heads_T(g):
                    act.wait_ge(*seen(b, "heads", 1, g))
                    act.activation(oT[:, 2 * g * T:(2 * g + 2) * T], bank[7][:, 0:2 * T], ACT.Copy
                                   ).then_inc(*did("oT", g))

                def q_path(l):
                    act.wait_ge(*seen(b, "q_high", l))
                    act.activation(Qz[:, :, 1:3, :], Qz[:, :, 0:1, :].to_broadcast([T, H, 2, 16]), ACT.Copy
                                   ).then_inc(*did("q_copied", l))
                    act.wait_ge(*seen(b, "q_middle", l))
                    act.activation(Qz[:, :, 4, :], Qz[:, :, 3, :], ACT.Copy).then_inc(*did("q_copied", l))
                    act.wait_ge(*seen(b, "qs_ps", l, 0))
                    act.activation(QS[0:STACK, 0:4, :].rearrange("p a n -> p (a n)"), as_bf16[0][0:STACK, 0:8 * T],
                                   ACT.Copy).then_inc(*did("q_stacked", l))

                def q_wide():
                    for n in range(2):
                        act.wait_ge(*seen(b, "qh_ps", n))
                        act.activation(qTh[:, n * 400:(n + 1) * 400], bank[n][:, 0:400], ACT.Copy, scale=0.125
                                       ).then_inc(*did("qh", n))
                    for n in range(4):
                        half, e = n // 2, n % 2
                        act.wait_ge(*seen(b, "qt_ps", half, e))
                        act.activation(qt[:, :].rearrange("p (j e q) -> p j e q", j=8, e=2)[:, 4 * half:4 * half + 4, e, :],
                                       bank[2 + 2 * e + half][:, 0:400].rearrange("p (j q) -> p j q", j=4), ACT.Copy
                                       ).then_inc(*did("qt_f", n))
                    act.wait_ge(*seen(b, "qt_f", 3))
                    act.activation(qtb[:, :], qt[:, :], ACT.Copy).then_inc(*did("qt"))

                def experts(l):
                    e, ni, _ = MOE[l]
                    act.wait_ge(*seen(b, "top", l))
                    act.activation(ex[:, 0:e], lg[:, 0:e], ACT.Exp, bias=small[:, 0:1]).then_inc(*did("route_exp", l))
                    for ck in range(ni // 4):
                        act.wait_ge(*seen(b, "gate_up", l, ck, 1))
                        if ck >= 2:
                            act.wait_ge(*seen(b, "hidden", l, ck - 2))
                        act.activation(th[ck % 2], bank[3 * (ck % 2)][:, 0:GW], ACT.Tanh, scale=0.5
                                       ).then_inc(*did("tanh", l, ck))

                def switch():
                    act.wait_ge(*seen(b, "gates_z"))
                    act.activation(ex[:, 0:80], lg[:, 0:80], ACT.Exp, scale=-1.0).then_inc(*did("gates_exp"))
                    for which, dst, bk in ((0, sqT, 5), (1, skT, 6)):
                        act.wait_ge(*seen(b, "switch_T_ps", which))
                        act.activation(dst, bank[bk][:, 0:400], ACT.Copy).then_inc(*did("switch_T", which))
                    act.wait_ge(*seen(b, "self_shifted", 1))
                    act.activation(sc, sc, ACT.Exp, scale=float(SD) ** -0.5).then_inc(*did("self_exp"))
                    for n in (0, 1):
                        act.wait_ge(*seen(b, "self_pT_ps", n))
                        act.activation(pT[:, n * 400:(n + 1) * 400], bank[2 + n][0:T, 0:400], ACT.Copy
                                       ).then_inc(*did("self_pT", n))
                    act.wait_ge(*seen(b, "switch_zT_ps"))
                    act.activation(szT[:, 0:2 * T], bank[5][:, 0:2 * T], ACT.Copy).then_inc(*did("switch_zT"))
                    act.activation(szT[0:64, 2 * T:3 * T], bank[5][0:64, 2 * T:3 * T], ACT.Copy
                                   ).then_inc(*did("switch_zT"))

                for l in range(4):
                    if l != 1:
                        q_path(l)
                    else:
                        q_wide()
                    exps(l)
                    if l == 1:
                        switch()
                    else:
                        experts(l)

        @block.vector
        def _(dve):
            V_ = nc.vector
            st.engine()
            dve.wait_ge(*once("pool_setup"))
            dve.wait_ge(*once("const_in"))
            V_.tensor_copy(identb[:, :], ident[:, :]).then_inc(*did("setup_bf16"))
            V_.memset(eps6[:, :], 1e-6).then_inc(*did("setup_bf16"))
            V_.tensor_scalar(neg_eye[0:T, :, :], ident[0:T, 0:T].unsqueeze(1).to_broadcast([T, GH, T]), NEG, None, ALU.mult
                             ).then_inc(*did("setup_bf16"))
            V_.tensor_tensor(gqk[:, 0, :], gqk[:, 0, :], gqk[:, 1, :], ALU.mult).then_inc(*did("setup_bf16"))
            b = None

            def link(ins):
                s, n = did("vector_order", st.count.get("vector_order", 0))
                ins.then_inc(s, n)
                dve.wait_ge(*seen(b, "vector_order", st.count["vector_order"] - 1))

            def k_split(l):
                if l == 0:
                    dve.wait_ge(*seen(b, "k_rms"))
                    link(V_.tensor_tensor(Kf[:, :], Kf[:, :], ktmp, ALU.mult))
                else:
                    dve.wait_ge(*seen(b, "k_read", l))
                link(V_.tensor_copy(Kp[:, 0, :], Kf[:, :]))
                link(V_.tensor_tensor(Kf[:, :], Kf[:, :], Kp[:, 0, :], ALU.subtract))
                link(V_.tensor_copy(Kp[:, 1, :], Kf[:, :]))
                V_.tensor_tensor(Kp[:, 2, :], Kf[:, :], Kp[:, 1, :], ALU.subtract).then_inc(*did("k_parts", l))

            def v_bias(l):
                for u in range(4):
                    dve.wait_ge(*seen(b, "v_ps", l, u))
                    V_.tensor_tensor(V[:, 3 * u:3 * u + 3, 0:144],
                                     bank[V_BANKS[u]][0:CW, 0:432].rearrange("p (a n) -> p a n", a=3),
                                     w["bv", l][0:CW, :].unsqueeze(1).to_broadcast([CW, 3, 144]), ALU.add
                                     ).then_inc(*did("v_ready", l, u))

            def mask_row():
                dve.wait_ge(*seen(b, "mrow_in"))
                V_.tensor_scalar(mrow[:, :], mrow_in.bitcast(U8), 0.0, NEG, ALU.is_equal, ALU.mult
                                 ).then_inc(*did("mrow_ready"))

            mask_row()
            dve.wait_ge(*once("weights_in0"))
            k_split(0)
            v_bias(0)
            dve.sem_inc(st.sem("turn_open"), 1)
            st.loop()
            with dve.Fori(0, B) as b:
                dve.wait_ge(*ahead(b, "x_in"))
                link(V_.tensor_copy(x[:, :], x_next[:, :]))

                def norm(k):
                    link(V_.bn_stats(bn[:, :], x[:, :]))
                    dve.sem_inc(st.sem("vector_passed"), 1)
                    link(V_.bn_aggr(mv[:, :], bn[:, :]))
                    V_.tensor_scalar(rstd[:, :], mv[:, 1:2], 1e-5, None, ALU.add).then_inc(*did("ln_var", k))
                    dve.wait_ge(*seen(b, "ln_rstd", k))
                    V_.tensor_scalar(xn[:, :], x[:, :], mv[:, 0:1], rstd[:, 0:1], ALU.subtract, ALU.mult
                                     ).then_inc(*did("xn", k))
                    dve.wait_ge(*seen(b, "xnT_ps", k))
                    V_.tensor_copy(xnT[:, :], bank[7][:, 0:T]).then_inc(*did("xnT", k))

                def add_y(k, ps, bias=None):
                    dve.wait_ge(*seen(b, "y_ps", k))
                    if bias is not None:
                        link(V_.tensor_tensor(yb[:, :], ps, bias, ALU.add))
                        V_.tensor_tensor(x[:, :], x[:, :], yb[:, :], ALU.add).then_inc(*did("x_out", k))
                    else:
                        V_.tensor_tensor(x[:, :], x[:, :], ps, ALU.add).then_inc(*did("x_out", k))
                    dve.wait_ge(*seen(b, "x_out", k))

                def q_path(l):
                    dve.wait_ge(*seen(b, "q_ps", l))
                    if l == 0:
                        link(V_.tensor_tensor(qn[:, :], bank[6][0:T, 0:D], w["bq", l][0:T, :], ALU.add))
                        link(V_.tensor_tensor(q2[:, :], qn[:, :], qn[:, :], ALU.mult))
                        link(V_.reduce_sum(qss[:, :], q2[:, :].rearrange("p (h d) -> p h d", h=H), AX))
                        V_.tensor_scalar(qss[:, :], qss[:, :], 1.0 / DH, 1e-6, ALU.mult, ALU.add).then_inc(*did("q_ms"))
                        dve.wait_ge(*seen(b, "q_rms"))
                        link(V_.tensor_tensor(q2[:, :].rearrange("p (h d) -> p h d", h=H),
                                              qn[:, :].rearrange("p (h d) -> p h d", h=H),
                                              qss[:, :].unsqueeze(2).to_broadcast([T, H, DH]), ALU.mult))
                        V_.tensor_tensor(qn[:, :], q2[:, :], gqk[0:T, 0, :], ALU.mult).then_inc(*did("q_ready", l))
                    else:
                        V_.tensor_tensor(qn[:, :], bank[6][0:T, 0:D], w["bq", l][0:T, :], ALU.add
                                         ).then_inc(*did("q_ready", l))
                    dve.wait_ge(*seen(b, "q_ready", l))
                    link(V_.tensor_tensor(qm.rearrange("t (p e) r -> t p e r", e=2),
                                          qn[:, :].rearrange("t (p r) -> t p r", p=PAIRS).unsqueeze(2
                                          ).to_broadcast([T, PAIRS, 2, 16]),
                                          own_dims[0:T, :, :].unsqueeze(1).to_broadcast([T, PAIRS, 2, 16]), ALU.mult))
                    V_.tensor_copy(Qz[:, :, 0, :], qm).then_inc(*did("q_high", l))
                    dve.wait_ge(*seen(b, "q_high", l))
                    link(V_.tensor_tensor(qm, qm, Qz[:, :, 0, :], ALU.subtract))
                    V_.tensor_copy(Qz[:, :, 3, :], qm).then_inc(*did("q_middle", l))
                    dve.wait_ge(*seen(b, "q_middle", l))
                    V_.tensor_tensor(Qz[:, :, 5, :], qm, Qz[:, :, 3, :], ALU.subtract).then_inc(*did("q_parts", l))
                    dve.wait_ge(*seen(b, "qs_ps", l, 1))
                    V_.tensor_copy(QS[0:STACK, 4:8, :].rearrange("p a n -> p (a n)"), as_bf16[1][0:STACK, 0:8 * T]
                                   ).then_inc(*did("q_stacked_too", l))

                def maxima(l, g):
                    for k in range(12):
                        i, ch = divmod(k, NCH)
                        n = g * 12 + k
                        dve.wait_ge(*seen(b, "max_scores", l, n))
                        V_.reduce_max(mxp[:, GH * g + i, ch:ch + 1], bank[max_bank(n)][0:T, 0:CH], AX
                                      ).then_inc(*did("max_chunk", l, n))
                        if l == 1 and g >= 2 and k == 8:
                            sums_out(g - 2)
                    dve.wait_ge(*seen(b, "max_chunk", l, g * 12 + 11))
                    flat = MZ[:, :, :, :].rearrange("t p e k -> t (p e k)")
                    for p in (2 * g, 2 * g + 1):
                        V_.tensor_reduce(flat[:, 6 * p + 1:6 * p + 6:4],
                                         mxp[:, 2 * p:2 * p + 2, :], AX, ALU.max, negate=True
                                         ).then_inc(*did("maxima", l, g))

                def sums_out(g):
                    dve.wait_ge(*seen(b, "p_sums", g))
                    if g > 0:
                        dve.wait_ge(*seen(b, "heads", 1, g - 1))
                    link(V_.reciprocal(Un, bank[6][:, 0:GW]))
                    dve.wait_ge(*seen(b, "values", 1, g, CT - 1))
                    V_.tensor_tensor(Un, bank[5][:, 0:GW], Un, ALU.mult).then_inc(*did("u_ready", g))

                def ranks(src, groups, n, keep, dst):
                    m = groups * n * n
                    gt = cmp[:, 0, 0:m].rearrange("t (g i j) -> t g i j", g=groups, i=n)
                    eq = cmp[:, 1, 0:m].rearrange("t (g i j) -> t g i j", g=groups, i=n)
                    s3 = src.rearrange("t (g n) -> t g n", g=groups)
                    other = s3.unsqueeze(2).to_broadcast([T, groups, n, n])
                    own = s3.unsqueeze(3).to_broadcast([T, groups, n, n])
                    V_.tensor_tensor(gt, other, own, ALU.is_gt)
                    link(V_.tensor_tensor(eq, other, own, ALU.is_equal))
                    link(V_.tensor_tensor(eq, eq, earlier[0:T, 0:n, 0:n].unsqueeze(1).to_broadcast([T, groups, n, n]),
                                          ALU.mult))
                    link(V_.tensor_tensor(cmp[:, 0, 0:m], cmp[:, 0, 0:m], cmp[:, 1, 0:m], ALU.add))
                    link(V_.reduce_sum(rank[:, 0:groups * n],
                                       cmp[:, 0, 0:m].rearrange("t (g j) -> t g j", j=n), AX))
                    link(V_.tensor_scalar(dst, rank[:, 0:groups * n], float(keep) - 0.5, None, ALU.is_lt))

                def experts(l):
                    e, ni, _ = MOE[l]
                    norm(2 * l + 1)
                    dve.wait_ge(*seen(b, "logits", l))
                    link(V_.tensor_copy(lg[:, 0:e], bank[6][0:T, 0:e]))
                    V_.tensor_reduce(small[:, 0:1], lg[:, 0:e], AX, ALU.max, negate=True).then_inc(*did("top", l))
                    dve.wait_ge(*seen(b, "route_exp", l))
                    link(V_.reduce_sum(small[:, 1:2], ex[:, 0:e], AX))
                    link(V_.reciprocal(small[:, 2:3], small[:, 1:2]))
                    link(V_.tensor_scalar(ex[:, 0:e], ex[:, 0:e], small[:, 2:3], None, ALU.mult))
                    if l == 0:
                        link(V_.reduce_max(gsc[:, 0:4], ex[:, 0:8].rearrange("t (g n) -> t g n", g=4), AX))
                        ranks(gsc[:, 0:4], 1, 4, 2, gsc[:, 8:12])
                        link(V_.tensor_tensor(ex[:, 0:8].rearrange("t (g n) -> t g n", g=4),
                                              ex[:, 0:8].rearrange("t (g n) -> t g n", g=4),
                                              gsc[:, 8:12].unsqueeze(2).to_broadcast([T, 4, 2]), ALU.mult))
                    ranks(ex[:, 0:e], 1, e, 4 if l == 2 else 2, msk[:, 0:e])
                    link(V_.tensor_tensor(ex[:, 0:e], ex[:, 0:e], msk[:, 0:e], ALU.mult))
                    if l == 3:
                        dve.sem_inc(*did("kept"))
                        dve.wait_ge(*seen(b, "position"))
                        link(V_.tensor_scalar(rank[:, 0:8], bank[6][0:T, 16:24], CAPACITY - 0.5, 0.5, ALU.is_lt, ALU.mult))
                        link(V_.tensor_tensor(acnt[:, :], acnt[:, :], msk[:, 0:8], ALU.add))
                        V_.tensor_tensor(comb[:, 0:e], ex[:, 0:e], rank[:, 0:e], ALU.mult).then_inc(*did("comb", l))
                    else:
                        link(V_.reduce_sum(small[:, 1:2], ex[:, 0:e], AX))
                        link(V_.reciprocal(small[:, 2:3], small[:, 1:2]))
                        V_.tensor_scalar(comb[:, 0:e], ex[:, 0:e], small[:, 2:3], 0.5, ALU.mult, ALU.mult
                                         ).then_inc(*did("comb", l))
                    for ck in range(ni // 4):
                        base = 3 * (ck % 2)
                        h_ = hm[ck % 2]
                        dve.wait_ge(*seen(b, "tanh", l, ck))
                        if ck >= 2:
                            dve.wait_ge(*seen(b, "down", l, ck - 2))
                        link(V_.scalar_tensor_tensor(h_, th[ck % 2], 1.0, bank[base + 1][:, 0:GW], ALU.add, ALU.mult))
                        link(V_.tensor_tensor(h_, h_, bank[base][:, 0:GW], ALU.mult))
                        dve.wait_ge(*seen(b, "weighed", l, ck))
                        V_.tensor_tensor(h_, h_, bank[base + 2][:, 0:GW], ALU.mult).then_inc(*did("hidden", l, ck))
                    dve.wait_ge(*seen(b, "down", l, ni // 4 - 1))
                    V_.tensor_tensor((x_last if l == 3 else x)[:, :], x[:, :], bank[7][0:T, 0:D], ALU.add
                                     ).then_inc(*did("x_out", 2 * l + 1))
                    dve.wait_ge(*seen(b, "x_out", 2 * l + 1))

                def switch():
                    norm(3)
                    dve.wait_ge(*seen(b, "gates_ps"))
                    V_.tensor_scalar(lg[:, 0:80], bank[6][0:T, 0:80], 17.0, None, ALU.min).then_inc(*did("gates_z"))
                    dve.wait_ge(*seen(b, "gates_z"))
                    ranks(lg[:, 0:80], 16, 5, SK, msk[:, 0:80])
                    dve.wait_ge(*seen(b, "gates_exp"))
                    link(V_.tensor_scalar(ex[:, 0:80], ex[:, 0:80], 1.0, None, ALU.add))
                    link(V_.reciprocal(ex[:, 0:80], ex[:, 0:80]))
                    link(V_.tensor_tensor(comb[:, 0:80], ex[:, 0:80], msk[:, 0:80], ALU.mult))
                    n = 0
                    for which, dst in ((0, sq), (1, sk), (2, sv)):
                        off = 40 if which == 0 else 0
                        for k in range(5):
                            dve.wait_ge(*seen(b, "switch_ps", n))
                            V_.tensor_tensor(prod[:, k * 512:(k + 1) * 512].rearrange("t (a d) -> t a d", a=8),
                                             bank[n % 5][0:T, :].rearrange("t (a d) -> t a d", a=8),
                                             comb[:, off + 8 * k:off + 8 * k + 8].unsqueeze(2).to_broadcast([T, 8, SD]),
                                             ALU.mult).then_inc(*did("gated", n))
                            n += 1
                        dve.wait_ge(*seen(b, "gated", n - 1))
                        V_.reduce_sum(dst.rearrange("t (h d) -> t h d", h=SH),
                                      prod.rearrange("t (h e d) -> t h d e", h=SH, e=SE), AX
                                      ).then_inc(*did("switch_sum", which))
                        dve.wait_ge(*seen(b, "switch_sum", which))
                    for n in (0, 1):
                        dve.wait_ge(*seen(b, "self_scores", n))
                        s3 = bank[n][0:T, 0:400].rearrange("t (h k) -> t h k", h=4)
                        link(V_.reduce_max(small[:, 0:4], s3, AX))
                        V_.tensor_tensor(sc.rearrange("t (j e k) -> t j e k", j=4, e=2)[:, :, n, :], s3,
                                         small[:, 0:4].unsqueeze(2).to_broadcast([T, 4, T]), ALU.subtract
                                         ).then_inc(*did("self_shifted", n))
                        dve.wait_ge(*seen(b, "self_shifted", n))
                    dve.wait_ge(*seen(b, "self_exp"))
                    link(V_.reduce_sum(rsum[:, 0:8], sc.rearrange("t (h k) -> t h k", h=SH), AX))
                    link(V_.reciprocal(rsum[:, 0:8], rsum[:, 0:8]))
                    dve.wait_ge(*seen(b, "self_out"))
                    link(V_.tensor_tensor(so.rearrange("t (h d) -> t h d", h=SH),
                                          bank[4][0:T, :].rearrange("t (h d) -> t h d", h=SH),
                                          rsum[:, 0:8].unsqueeze(2).to_broadcast([T, SH, SD]), ALU.mult))
                    for h in range(SH):
                        ins = V_.tensor_tensor(prod[:, h * 320:(h + 1) * 320].rearrange("t (e d) -> t e d", e=SE),
                                               so[:, h * SD:(h + 1) * SD].unsqueeze(1).to_broadcast([T, SE, SD]),
                                               msk[:, 40 + 5 * h:45 + 5 * h].unsqueeze(2).to_broadcast([T, SE, SD]),
                                               ALU.mult)
                    link(ins)
                    V_.reduce_sum(sz, prod.rearrange("t (h n) -> t n h", h=SH), AX).then_inc(*did("switch_z"))
                    add_y(3, bank[7][0:T, 0:D])

                for l in range(4):
                    norm(2 * l)
                    if l != 1:
                        q_path(l)
                    if l == 3:
                        mask_row()
                    maxima(l, 0)
                    if l == 0:
                        dve.wait_ge(*seen(b, "mask_in"))
                        V_.tensor_scalar(absent[:, :], mask_in, 0.0, None, ALU.is_equal).then_inc(*did("absent"))
                        dve.wait_ge(*seen(b, "absent"))
                    for g in range(GROUPS):
                        if g + 1 < GROUPS:
                            maxima(l, g + 1)
                    if l == 1:
                        sums_out(GROUPS - 2)
                        sums_out(GROUPS - 1)
                    if l != 1:
                        k_split(NEXT_SMALL[l])
                        dve.wait_ge(*seen(b, "heads", l, GROUPS - 1))
                        o3 = bank[6][0:T, 0:H * VW].rearrange("t (h d) -> t h d", h=H)
                        link(V_.reciprocal(rsum[:, :], o3[:, :, DH:VW].rearrange("t h d -> t (h d)")))
                        V_.tensor_tensor(attn[:, :].rearrange("t (h d) -> t h d", h=H), o3[:, :, 0:DH],
                                         rsum[:, :].unsqueeze(2).to_broadcast([T, H, DH]), ALU.mult
                                         ).then_inc(*did("attn", l))
                        v_bias(NEXT_SMALL[l])
                        add_y(2 * l, bank[6][0:T, 0:D], w["bo", l][0:T, :])
                        experts(l)
                    else:
                        add_y(2, bank[6][0:T, 0:D])
                        switch()
                dve.sem_inc(st.sem("turn_open"), 1)
        return st.result()


def layout(i):
    import numpy as np
    f = np.float32
    r = lambda v: np.ascontiguousarray(v)
    wide = lambda v: r(np.broadcast_to(np.asarray(v)[None, :], (128, v.shape[0])))
    once_more = lambda v: r(np.concatenate([v, v[-1:]], 0))
    rows = np.minimum(np.arange(SP_), S - 1)
    ctx = np.asarray(i["ctx_1024"])[:, rows]
    a = {
        "x": once_more(i["x"]),
        "ctxT": once_more(ctx.transpose(0, 2, 1)),
        "ctxN": r(ctx.reshape(B, CT, CW, D).transpose(0, 2, 1, 3)),
        "mask": r(np.asarray(i["mask_BxSxS2_if1"])[:, :, rows]),
        "ident": np.eye(128, dtype=f),
    }
    m = np.zeros((B, 1, SP_), np.uint8)
    m[:, 0, :S] = np.asarray(i["mask_BxS2_bk0"]).view(np.uint8)
    a["mrow"] = once_more(m.view(np.int32))
    p = np.arange(128)
    a["headsum"] = (p[:, None] // DH == p[None, :] // DH).astype(f)
    picks = np.zeros((128, GH, VW), f)
    for k in range(GH):
        for d in range(VW):
            picks[p % 32 == (VW * k if k < 3 else 0) + d, k, d] = 1
    a["picks"] = picks
    own = np.zeros((128, 2, 16), f)
    own[:, 0, :DH] = own[:, 1, DH:] = DH ** -0.5
    a["own_dims"] = own
    a["before"] = (p[:, None] < p[None, :]).astype(f)
    q = np.arange(16)
    a["earlier"] = r(np.broadcast_to((q[None, :] < q[:, None]).astype(f)[None], (128, 16, 16)))
    pad = np.zeros((1, SP_), f)
    pad[:, S:] = NEG
    a["padrow_f"] = pad

    def values(v):
        v = v.reshape(v.shape[0], H, DH)
        return r(np.concatenate([v, np.zeros((v.shape[0], H, 1), f)], 2).reshape(v.shape[0], H * VW))

    def value_bias(v):
        v = v.reshape(1, H, DH)
        v = np.concatenate([v, np.ones((1, H, 1), f)], 2).reshape(H * VW)
        return wide(v)

    for l, wq, bq, wk, bk, wv, bv, wo in (
        (0, i["L0_xattn_Wq"].T, i["L0_xattn_bq"], i["L0_xattn_Wkv"][:128].T, i["L0_xattn_bkv"][:128],
         i["L0_xattn_Wkv"][128:].T, i["L0_xattn_bkv"][128:], i["L0_xattn_Wo"].T),
        (2, i["L2_xattn_Wq"], i["L2_xattn_bq"], i["L2_xattn_Wk"], i["L2_xattn_bk"],
         i["L2_xattn_Wv"], i["L2_xattn_bv"], i["L2_xattn_Wo"]),
        (3, i["L3_xattn_Wq"].T, i["L3_xattn_bq"], i["L3_xattn_Wk"].T, i["L3_xattn_bk"],
         i["L3_xattn_Wv"].T, i["L3_xattn_bv"], i["L3_xattn_Wo"].T),
    ):
        a[f"wq{l}"], a[f"wk{l}"], a[f"wo{l}"] = r(wq), r(wk), r(wo)
        a[f"wv{l}"] = values(np.asarray(wv))
        a[f"bq{l}"], a[f"bo{l}"] = wide(bq), wide(i[f"L{l}_xattn_bo"])
        a[f"bk{l}"] = r(np.asarray(bk)[:, None])
        a[f"bv{l}"] = value_bias(np.asarray(bv))
    a["gqk"] = r(np.stack([wide(i["L0_xattn_gq"].reshape(128)), wide(i["L0_xattn_gk"].reshape(128))], 1))

    def in_rows(v):
        return r(v.reshape(-1, 128, v.shape[1]).transpose(1, 0, 2))

    w13 = i["L0_ffn_w13_weight"]
    a["gw0"] = r(i["L0_ffn_gate_w"].T)
    a["wa0"] = r(w13[:, :256].reshape(-1, 128).T)
    a["wb0"] = r(w13[:, 256:].reshape(-1, 128).T)
    a["w20"] = in_rows(i["L0_ffn_w2_weight"].transpose(0, 2, 1).reshape(-1, 128))
    a["gw2"] = r(i["L2_ffn_gate_w"].T)
    a["wa2"] = r(i["L2_ffn_w1"].transpose(1, 0, 2).reshape(128, -1))
    a["wb2"] = r(i["L2_ffn_w3"].transpose(1, 0, 2).reshape(128, -1))
    a["w22"] = in_rows(i["L2_ffn_w2"].reshape(-1, 128))
    fc = i["L3_ffn_c_fc"]
    a["gw3"] = r(i["L3_ffn_w_gate"])
    a["wa3"] = r(fc[:, :, :192].transpose(1, 0, 2).reshape(128, -1))
    a["wb3"] = r(fc[:, :, 192:].transpose(1, 0, 2).reshape(128, -1))
    a["w23"] = in_rows(i["L3_ffn_c_proj"].reshape(-1, 128))
    a["wq1"] = r(i["L1_xattn_Wq"])
    a["wk1"] = r(i["L1_xattn_Wk"].T.reshape(8, 128, 128).transpose(1, 0, 2).reshape(128, 1024))
    a["wv1"] = r(i["L1_xattn_Wv"])
    a["wo1"] = r(i["L1_xattn_Wo"].reshape(8, 128, 128).transpose(1, 0, 2).reshape(128, 1024))
    a["swd"] = r(np.concatenate([i["L1_ffn_Ws"], i["L1_ffn_Wd"]], 1))
    a["swq"] = r(i["L1_ffn_Wq"])
    a["swk"] = r(i["L1_ffn_Wkv"][:, :SQ])
    a["swv"] = r(i["L1_ffn_Wkv"][:, SQ:])
    wo = i["L1_ffn_Wo"].reshape(64, SE, 128).transpose(1, 0, 2).reshape(320, 128)
    wo = np.concatenate([wo, np.zeros((64, 128), f)], 0)
    a["swo"] = in_rows(wo)
    return a


def kernel(**inputs):
    import ml_dtypes
    import numpy as np
    import concourse.bacc as bacc
    from concourse.bass_utils import run_bass_kernel_spmd

    arrays = layout({k: np.asarray(v) for k, v in inputs.items()})
    arrays["padrow"] = arrays.pop("padrow_f").astype(ml_dtypes.bfloat16)
    known = None
    for _ in range(2):
        nc = bacc.Bacc("TRN2", target_bir_lowering=False, num_devices=1)
        a = {n: nc.dram_tensor(f"in_{n}", v.shape, mybir.dt.from_np(v.dtype), kind="ExternalInput").ap()
             for n, v in arrays.items()}
        a["scratch_k"] = nc.dram_tensor("scratch_k", (128, PARTS, SP_), BF16, kind="Internal").ap()
        a["out"] = nc.dram_tensor("out_x", (B, T, D), F32, kind="ExternalOutput").ap()
        known = build(nc, a, known)
    r = run_bass_kernel_spmd(nc, [{f"in_{n}": v for n, v in arrays.items()}], core_ids=[0])
    return r.results[0]["out_x"]
```

```python
from contextlib import ExitStack

import concourse.bass as bass
from concourse import mybir

F32 = mybir.dt.float32
BF16 = mybir.dt.bfloat16
I32 = mybir.dt.int32
U8 = mybir.dt.uint8
ALU = mybir.AluOpType
ACT = mybir.ActivationFunctionType
AX = mybir.AxisListType.X

B = 8
T = 100
D = 128
S = 1444
H = 16
CT = 12
CW = 121
SP_ = CT * CW
NCH = 3
CH = SP_ // NCH
PAIRS = H // 2
DH = 8
GROUPS = 4
GH = H // GROUPS
GW = GH * T
VW = DH + 1
PARTS = 3
K_SEQ = (0, 1, 2, 0, 1, 0)
Q_SEQ = (0, 0, 0, 1, 1, 2)
STACK = 6 * 16
BIAS_ROW = STACK
ROWS = BIAS_ROW + 3
NEG = -float(2 ** 30)
LOWEST = -3.0e38
P_SLOTS = 8
SMALL = (0, 2, 3)
NEXT_SMALL = {0: 2, 2: 3, 3: 0}
V_BANKS = (3, 4, 7, 2)
K_BANKS = (5, 7, 6)
LEAD = 2


MOE = {
    0: (8, 16, lambda half: half // 4),
    2: (16, 8, lambda half: half),
    3: (8, 12, lambda half: half // 3),
}
CAPACITY = 512
SH, SE, SD, SK = 8, 5, 64, 3
SQ = SH * SE * SD
Z_HEADS = 5


def max_bank(l, n):
    if n < GH * NCH:
        return (3, 4, 0, 1, 2)[n % 5]
    return 3 + n % 2 if l == 1 else (7, 3, 4)[n % 3]


def chunks_after(l, g, c):
    first = GH * NCH * (g + 1) + LEAD
    if l != 1:
        ns = (first + c,)
    elif c < 4:
        ns = (first + c,)
    elif c < 8:
        ns = ()
    else:
        ns = (first + 2 * c - 12, first + 2 * c - 11)
    return [n for n in ns if n < GH * NCH * GROUPS]


class Steps:

    def __init__(self, nc, ctx, known):
        self.nc, self.ctx, self.known = nc, ctx, known
        self.sems, self.count, self.mark = {}, {}, {}
        self.before_loop, self.others, self.first = {}, set(), {}

    def sem(self, name):
        if name not in self.sems:
            self.sems[name] = self.ctx.enter_context(self.nc.semaphore(name))
        return self.sems[name]

    def engine(self):
        self.others = set(self.count)

    def loop(self):
        for name, n in self.count.items():
            if name not in self.others:
                self.before_loop[name] = n
        self.first.update({k: v for k, v in self.mark.items() if k[0] not in self.others})

    def result(self):
        return ({n: c - self.before_loop.get(n, 0) for n, c in self.count.items()},
                dict(self.mark), dict(self.first))

    def did(self, name, *key, by=1):
        self.count[name] = self.count.get(name, 0) + by
        self.mark[(name,) + key] = self.count[name]
        return self.sem(name), by

    def seen(self, turn, name, *key):
        if turn is None:
            return self.once(name, *key)
        if not self.known:
            return self.sem(name), turn * 2 + 1
        return self.sem(name), turn * self.known[0][name] + self.known[1][(name,) + key]

    def ahead(self, turn, name, *key):
        if not self.known:
            return self.sem(name), turn * 2 + 1
        totals, marks, first = self.known
        assert marks[(name,) + key] == first[(name,) + key] + totals[name]
        return self.sem(name), turn * totals[name] + first[(name,) + key]

    def once(self, name, *key):
        return self.sem(name), self.known[2][(name,) + key] if self.known else 1


def build(nc, a, known):
    with ExitStack() as ctx:
        st = Steps(nc, ctx, known)
        did, seen, ahead, once = st.did, st.seen, st.ahead, st.once

        def sb(name, shape, dt=F32):
            return ctx.enter_context(nc.sbuf_tensor(name, shape, dt))

        ident = sb("ident", [128, 128])
        identb = sb("identb", [128, 128], BF16)
        headsum = sb("headsum", [128, 128])
        picks = sb("picks", [128, GH, VW])
        eps6 = sb("eps6", [128, 1])
        own_dims = sb("own_dims", [128, 2, 16])
        before = sb("before", [128, 128])
        earlier = sb("earlier", [128, 16, 16])
        ones = sb("ones", [128, 128])
        half_power = sb("half_power", [128, 16])
        eyes = sb("eyes", [128, GH, T], BF16)
        w = {}
        for l in SMALL:
            for n, c in (("wq", 128), ("wk", 128), ("wv", H * VW), ("wo", 128),
                         ("bq", 128), ("bk", 1), ("bv", H * VW), ("bo", 128)):
                w[n, l] = sb(f"{n}{l}", [128, c])
            e, ni, _ = MOE[l]
            w["gw", l] = sb(f"gw{l}", [128, e])
            w["wa", l] = sb(f"wa{l}", [128, ni * 128])
            w["wb", l] = sb(f"wb{l}", [128, ni * 128])
            w["w2", l] = sb(f"w2{l}", [128, ni, 128])
        for n in ("wq", "wk", "wv", "wo"):
            w[n, 1] = sb(f"{n}1", [128, 1024])
        gqk = sb("gqk", [128, 2, 128])
        swd = sb("swd", [128, 2 * SH * SE])
        swqv = sb("swqv", [128, SQ])
        swk = sb("swk", [128, SQ])
        swo = sb("swo", [128, 3, 128])

        x = sb("x", [T, D])
        x_next = sb("x_next", [T, D])
        xn = sb("xn", [T, D])
        xnT = sb("xnT", [128, T])
        bn = sb("bn", [T, 6])
        mv = sb("mv", [T, 2])
        rstd = sb("rstd", [T, 1])
        ctxT = sb("ctxT", [128, SP_])
        ctxN = sb("ctxN", [CW, CT, D])
        ctxTb = sb("ctxTb", [128, SP_], BF16)
        absent = sb("absent", [T, SP_], BF16)
        Kf = sb("Kf", [128, SP_])
        Kp = sb("Kp", [128, PARTS, SP_], BF16)
        ktmp = Kp[:, :, :].rearrange("p a n -> p (a n)").bitcast(F32)[:, 0:SP_]
        KS = sb("KS", [128, PAIRS, SP_], BF16)
        QS = sb("QS", [128, PAIRS, 2 * T], BF16)
        V = sb("V", [CW, CT, 168])
        qn = sb("qn", [T, D])
        qss = sb("qss", [T, H])
        mxp = sb("mxp", [T, H, NCH])
        MZ = sb("MZ", [T, PAIRS, 2, 3], BF16)
        rsum = sb("rsum", [T, H])
        attn = sb("attn", [T, D])
        q2 = attn
        attnT = sb("attnT", [128, T])
        yb = sb("yb", [T, D])
        x_last = yb
        acnt = sb("acnt", [T, 8])
        lg = sb("lg", [T, 80])
        ex = sb("ex", [T, 80])
        gsc = sb("gsc", [T, 16])
        small = sb("small", [T, 4])
        msk = sb("msk", [T, 80])
        comb = sb("comb", [T, 80])
        rank = sb("rank", [T, 80])
        arena = sb("arena", [128, 6800])
        P = arena[:, 0:P_SLOTS * GW].rearrange("p (s n) -> p s n", s=P_SLOTS)
        qt = arena[:, 3200:4800]
        qtb = arena[:, 4800:5600].bitcast(BF16)
        accP = arena[:, 5600:6400].rearrange("p (s n) -> p s n", s=2)
        Osb = arena[:, 6400:6800]
        cmp = arena[0:T, 5696:6496].rearrange("t (a n) -> t a n", a=2)
        mrow_in = arena[0:1, 3200:3200 + SP_ // 4]
        mrow = arena[0:1, 4672:4672 + SP_ // 2].bitcast(BF16)
        Qz = arena[0:T, 5400:6168].bitcast(BF16).rearrange("t (h s r) -> t h s r", h=H, s=6)
        qm = arena[0:T, 6400:6656].rearrange("t (h r) -> t h r", h=H)
        masked = arena[0:T, 5400:5400 + 2 * CH].rearrange("t (s n) -> t s n", s=2)
        mask_in = arena[0:T, 3200:3200 + SP_].bitcast(I32)
        qTh = Kf[:, 0:800]
        oT = Kf[:, 0:800]
        Un = Osb
        gated = [arena[0:T, SQ * i:SQ * (i + 1)] for i in (0, 1)]
        sq = sv = gated[0][:, 0:512]
        sk = arena[0:T, 5120:5632]
        sqT = arena[:, 5632:6032]
        skT = arena[:, 6032:6432]
        sc = arena[0:T, 2560:3360]
        pT = arena[0:T, 3360:4160]
        so = arena[0:T, 4160:4672]
        kept_heads = gated[0]
        sz = arena[0:T, 4672:4992]
        szT = arena[:, 4992:5292]
        sz_part = arena[0:T, 5300:5620]
        th = [arena[:, 400 * i:400 * i + 400] for i in (0, 1)]
        hm = [arena[:, 400 * i:400 * i + 400] for i in (2, 3)]

        bank = [ctx.enter_context(nc.psum_tensor(f"bank{i}", [128, 512], F32)) for i in range(8)]
        as_bf16 = [bank[i][:, :].bitcast(BF16) for i in range(8)]

        def of_parity(ap, half, e):
            return ap[:, :].rearrange("p (j e q) -> p j e q", j=8, e=2)[:, 4 * half:4 * half + 4, e, :]

        def shift_ps(l):
            return as_bf16[7][STACK:ROWS, 0:GW] if l == 1 else as_bf16[6][STACK:ROWS, 400:400 + GW]

        scratch_k = a["scratch_k"]

        def once_now(name):
            return st.sem(name), st.count[name]

        block = ctx.enter_context(nc.Block())

        @block.sync
        def _(sp):
            st.engine()
            def inputs(src):
                sp.dma_start(ctxT[:, :], src("ctxT")).then_inc(*did("ctxT_in", by=16))
                sp.dma_start(mrow_in.bitcast(I32), src("mrow")).then_inc(*did("mrow_in", by=16))
                sp.dma_start(x_next[:, :], src("x")).then_inc(*did("x_in", by=16))

            inputs(lambda n: a[n][0])
            for t, n in ((ident, "ident"), (headsum, "headsum"), (picks, "picks"), (own_dims, "own_dims"),
                         (before, "before"), (earlier, "earlier"), (gqk, "gqk")):
                sp.dma_start(t[...], a[n]).then_inc(*did("const_in", by=16))

            def load(n, l):
                sp.dma_start(w[n, l][...], a[f"{n}{l}"]).then_inc(*did(f"weights_in{l}", by=16))
            for n in ("wq", "wk", "wv", "wo", "bq", "bk", "bv", "bo", "gw", "wa", "wb", "w2"):
                load(n, 0)
            b = None

            def k_stack(l, prev):
                sp.wait_ge(*seen(b, "k_parts", l))
                sp.dma_start(scratch_k, Kp[:, :, :]).then_inc(*did("k_out", l, by=16))
                if prev is not None:
                    sp.wait_ge(*seen(b, "scores", "end", prev))
                    sp.sem_inc(st.sem("sync_passed"), 1)
                if l == 0:
                    sp.wait_ge(*seen(b, "mrow_ready"))
                    sp.dma_start(KS[BIAS_ROW:BIAS_ROW + 1, :, :],
                                 mrow[:, :].unsqueeze(1).to_broadcast([1, PAIRS, SP_])
                                 ).then_inc(*did(f"k_stacked{l}", by=16))
                sp.wait_ge(*seen(b, "k_out", l))
                for s, part in enumerate(K_SEQ):
                    sp.dma_start(KS[16 * s:16 * s + 16, :, :],
                                 scratch_k[:, part, :].rearrange("(p r) n -> r p n", r=16)
                                 ).then_inc(*did(f"k_stacked{l}", by=16))

            k_stack(0, None)
            for n in ("wq", "wk", "wv", "wo"):
                load(n, 1)
            for t, n in ((swd, "swd"), (swk, "swk"), (swo, "swo")):
                sp.dma_start(t[...], a[n]).then_inc(*did("weights_in1", by=16))
            for l in (2, 3):
                for n in ("wq", "wk", "wv", "wo", "bq", "bk", "bv", "bo", "gw", "wa", "wb", "w2"):
                    load(n, l)

            st.loop()
            with sp.Fori(0, B) as b:
                sp.wait_ge(st.sem("turn_open"), b + 1)
                sp.sem_inc(st.sem("sync_passed"), 1)
                sp.dma_start(mask_in, a["mask"][b]).then_inc(*did("mask_in", by=16))
                sp.dma_start(ctxN[:, :, :], a["ctxN"][b]).then_inc(*did("ctxN_in", by=16))
                sp.dma_start(swqv[:, :], a["swq"]).then_inc(*did("swqv_in", "q", by=16))
                sp.wait_ge(*seen(b, "scores", "end", 0))
                sp.dma_start(KS[BIAS_ROW:BIAS_ROW + 1, :, :],
                             a["padrow"].unsqueeze(1).to_broadcast([1, PAIRS, SP_])
                             ).then_inc(*did("bias_row_in", by=16))
                k_stack(2, 0)
                sp.wait_ge(*seen(b, "switch_ps", 4))
                sp.dma_start(swqv[:, :], a["swv"]).then_inc(*did("swqv_in", "v", by=16))
                k_stack(3, 2)
                sp.wait_ge(*seen(b, "v_ps", 3, 3))
                sp.sem_inc(st.sem("sync_passed"), 1)
                inputs(lambda n: a[n][1:][b])
                k_stack(0, 3)
                sp.wait_ge(*seen(b, "x_out", 7))
                sp.sem_inc(st.sem("sync_passed"), 1)
                sp.dma_start(a["out"][b], x_last[:, :]).then_inc(*did("out_stored", by=16))
                sp.wait_ge(*seen(b, "out_stored"))
                sp.sem_inc(st.sem("sync_passed"), 1)
            for name in ("k_stacked0", "x_in", "ctxT_in", "mrow_in"):
                sp.wait_ge(*ahead(B, name))

        @block.gpsimd
        def _(pool):
            st.engine()
            for n, (ap, value) in enumerate((
                    (ones[:, :], 1.0), (half_power[:, :], -0.5), (KS[STACK:ROWS, :, :], 1.0),
                    (QS[STACK:ROWS, :, :], 1.0), (MZ[:, :, :, :], 0.0), (V[:, :, :], 0.0),
                    (acnt[:, :], 0.0), (MZ[:, :, :, 0:1], 1.0))):
                pool.memset(ap, value).then_inc(*did("pool_setup"))
                pool.wait_ge(*once_now("pool_setup"))
            b = None

            def context_bf16():
                pool.wait_ge(*seen(b, "ctxT_in"))
                pool.sem_inc(st.sem("pool_passed"), 1)
                pool.tensor_copy(ctxTb[:, :], ctxT[:, :]).then_inc(*did("ctxTb"))

            context_bf16()
            st.loop()
            with pool.Fori(0, B) as b:
                pool.wait_ge(st.sem("turn_open"), b + 1)

                def power(name, ap, n):
                    pool.tensor_tensor(ap, ap, half_power[0:T, 0:n], ALU.pow).then_inc(*did(*name))

                def norm(k):
                    pool.wait_ge(*seen(b, "ln_var", k))
                    power(("ln_rstd", k), rstd[:, :], 1)

                norm(0)
                pool.wait_ge(*seen(b, "q_ms"))
                power(("q_rms",), qss[:, :], H)
                norm(1)
                norm(2)
                for g in range(GROUPS):
                    for c in range(CT):
                        pool.wait_ge(*seen(b, "exp", 1, g, c))
                        t = g * CT + c
                        dst = accP[0:CW, g % 2, :]
                        if c == 0:
                            if g >= 2:
                                pool.wait_ge(*seen(b, "p_sums", g - 2))
                            pool.sem_inc(st.sem("pool_passed"), 1)
                            pool.tensor_copy(dst, P[0:CW, t % P_SLOTS, :]).then_inc(*did("p_added", g, c))
                        else:
                            pool.wait_ge(*seen(b, "p_added", g, c - 1))
                            pool.tensor_tensor(dst, dst, P[0:CW, t % P_SLOTS, :], ALU.add).then_inc(*did("p_added", g, c))
                norm(3)
                for which in (0, 2):
                    for e in range(1, SE):
                        pool.wait_ge(*seen(b, "gated", 5 * which + e))
                        if e > 1:
                            pool.wait_ge(*seen(b, "expert_sum", which, e - 1))
                        pool.tensor_tensor(sq, sq, gated[0][:, 512 * e:512 * (e + 1)], ALU.add
                                           ).then_inc(*did("expert_sum", which, e))
                for h in range(Z_HEADS, SH):
                    if h == Z_HEADS:
                        pool.wait_ge(*seen(b, "self_normed"))
                    pool.tensor_tensor(kept_heads[:, h * 320:(h + 1) * 320].rearrange("t (e d) -> t e d", e=SE),
                                       so[:, h * SD:(h + 1) * SD].unsqueeze(1).to_broadcast([T, SE, SD]),
                                       msk[:, 40 + 5 * h:45 + 5 * h].unsqueeze(2).to_broadcast([T, SE, SD]),
                                       ALU.mult).then_inc(*did("pool_kept", h))
                for h in range(Z_HEADS + 1, SH):
                    pool.wait_ge(*seen(b, "pool_kept", SH - 1))
                    if h > Z_HEADS + 1:
                        pool.wait_ge(*seen(b, "z_part", h - 1))
                    pool.tensor_tensor(sz_part, kept_heads[:, Z_HEADS * 320:(Z_HEADS + 1) * 320] if h == Z_HEADS + 1 else sz_part,
                                       kept_heads[:, h * 320:(h + 1) * 320], ALU.add).then_inc(*did("z_part", h))
                for k in range(4, 8):
                    if k == 7:
                        context_bf16()
                    norm(k)

        @block.tensor
        def _(pe):
            st.engine()
            pe.wait_ge(*once("pool_setup"))
            pe.wait_ge(*once("const_in"))
            pe.wait_ge(*once("setup_bf16"))
            b = None

            def k_chunk(l, ch):
                pe.matmul(bank[K_BANKS[ch]][:, 0:CH], w["wk", l][:, :], ctxT[:, ch * CH:(ch + 1) * CH],
                          start=True, stop=True).then_inc(*did("k_ps", l, ch))

            def k_squares(ch):
                pe.wait_ge(*seen(b, "k_squared", ch))
                pe.matmul(bank[K_BANKS[ch]][:, 0:CH], headsum[:, :], ktmp[:, ch * CH:(ch + 1) * CH],
                          start=True, stop=True).then_inc(*did("k_ss", ch))

            def v_proj(l, u):
                for c in range(3 * u, 3 * u + 3):
                    mm = pe.matmul(bank[V_BANKS[u]][0:CW, (c % 3) * 144:(c % 3) * 144 + 144],
                                   ctxT[:, c * CW:(c + 1) * CW], w["wv", l][:, :], start=True, stop=True)
                mm.then_inc(*did("v_ps", l, u))

            pe.wait_ge(*once("weights_in0"))
            pe.wait_ge(*once("ctxT_in"))
            for ch in range(NCH):
                k_chunk(0, ch)
            for ch in range(NCH):
                k_squares(ch)
            pe.wait_ge(*once("k_log"))
            for u in range(4):
                v_proj(0, u)
            st.loop()
            with pe.Fori(0, B) as b:
                pe.wait_ge(st.sem("turn_open"), b + 1)

                def norm_T(k):
                    pe.wait_ge(*seen(b, "xn", k))
                    pe.transpose(bank[7][:, 0:T], xn[:, :], ident[0:T, 0:T]).then_inc(*did("xnT_ps", k))
                    pe.wait_ge(*seen(b, "xnT", k))

                def q_small(l):
                    pe.matmul(bank[6][0:T, 0:D], xnT[:, :], w["wq", l][:, :], start=True, stop=True
                              ).then_inc(*did("q_ps", l))
                    k_chunk(NEXT_SMALL[l], 1)
                    pe.wait_ge(*seen(b, "q_parts", l))
                    pe.wait_ge(*seen(b, "q_copied", l))
                    for h in range(H):
                        mm = pe.transpose(as_bf16[h // 8][0:STACK, (h % 8) * T:(h % 8 + 1) * T], Qz[:, h, :, :].rearrange("t s r -> t (s r)"),
                                          identb[0:T, 0:T])
                        if h % 8 == 7:
                            mm.then_inc(*did("qs_ps", l, h // 8))

                def q_wide():
                    for p in range(8):
                        mm = pe.matmul(bank[p // 4][:, (p % 4) * T:(p % 4 + 1) * T],
                                       w["wq", 1][:, p * 128:(p + 1) * 128], xnT[:, :], start=True, stop=True)
                        if p % 4 == 3:
                            mm.then_inc(*did("qh_ps", p // 4))
                    for h in range(H):
                        if h % 8 == 0:
                            pe.wait_ge(*(seen(b, "qh", 0) if h == 0 else seen(b, "qh_too")))
                        r, j = 64 * (h % 2), h // 2
                        mm = pe.matmul(bank[2 + 2 * (h % 2) + j // 4][:, (j % 4) * T:(j % 4 + 1) * T],
                                       w["wk", 1][r:r + 64, (h // 2) * 128:(h // 2 + 1) * 128],
                                       qTh[r:r + 64, (h // 2) * T:(h // 2 + 1) * T], start=True, stop=True)
                        if h % 8 >= 6:
                            mm.then_inc(*did("qt_ps", h // 8, h % 2))

                def max_scores(l, g, k):
                    i, ch = divmod(k, NCH)
                    h = GH * g + i
                    n = g * 12 + k
                    earlier_ns = [m for m in range(n) if max_bank(l, m) == max_bank(l, n)]
                    if earlier_ns:
                        pe.wait_ge(*seen(b, "max_chunk", l, earlier_ns[-1]))
                    dst = bank[max_bank(l, n)][0:T, 0:CH]
                    cols = slice(ch * CH, (ch + 1) * CH)
                    if l == 1:
                        pe.matmul(dst, qtb[:, h * T:(h + 1) * T], ctxTb[:, cols], start=True, stop=True
                                  ).then_inc(*did("max_scores", l, n))
                        return
                    p, e = h // 2, h % 2
                    pe.matmul(dst, QS[0:BIAS_ROW + 1, p, e * T:(e + 1) * T], KS[0:BIAS_ROW + 1, p, cols],
                              start=True, stop=True).then_inc(*did("max_scores", l, n))

                def shift_T(l, g):
                    pe.wait_ge(*seen(b, "maxima", l, g))
                    for n in range(4):
                        mm = pe.transpose(shift_ps(l)[:, n * T:(n + 1) * T], MZ[:, 2 * g + n // 2, n % 2, :],
                                          identb[0:T, 0:T])
                    mm.then_inc(*did("shift_ps", l, g))

                def scores(l, g, c):
                    t = g * CT + c
                    if c == 0:
                        pe.wait_ge(*seen(b, "shift", l, g))
                    if t >= 3:
                        pe.wait_ge(*seen(b, "exp", l, (t - 3) // CT, (t - 3) % CT))
                    bk = bank[t % 3]
                    cols = slice(c * CW, (c + 1) * CW)
                    if l == 1:
                        pe.matmul(bk[0:CW, 0:GW], ctxT[:, cols], qt[:, g * GW:(g + 1) * GW], start=True, stop=False)
                        mm = pe.matmul(bk[0:CW, 0:GW], KS[STACK:ROWS, 0, cols], QS[STACK:ROWS, 2 * g:2 * g + 2, :],
                                       start=False, stop=True)
                    else:
                        if l == 3:
                            pe.matmul(bk[0:CW, 0:GW], absent[:, cols], eyes[0:T, :, :], start=True, stop=False)
                        for p in (0, 1):
                            mm = pe.matmul(bk[0:CW, 2 * T * p:2 * T * (p + 1)], KS[0:ROWS, 2 * g + p, cols],
                                           QS[0:ROWS, 2 * g + p, :], start=(l != 3), stop=(l != 3 or p == 1))
                    mm.then_inc(*did("scores", l, g, c))
                    if t == GROUPS * CT - 1:
                        st.mark["scores", "end", l] = st.count["scores"]

                def values(l, g, u, part=None):
                    pe.wait_ge(*seen(b, "exp", l, g, 4 * u + 3))
                    if u == 0 and g > 0 and not part:
                        pe.wait_ge(*(seen(b, "u_ready", g - 1) if l == 1 else seen(b, "o_copied", l, g - 1)))
                    if l == 1:
                        for r in range(4):
                            c = 4 * u + r
                            if g == GROUPS - 1 and u == 2 and r == 0:
                                p_sums(g)
                            mm = pe.matmul(bank[5][:, 0:GW], ctxN[:, c, :], P[0:CW, (g * CT + c) % P_SLOTS, :],
                                           start=(c == 0), stop=(c == CT - 1))
                            mm.then_inc(*did("values", l, g, c))
                        return
                    lo, hi, v0 = ((0, 3 * T, 0), (3 * T, GW, 3 * VW))[part]
                    for r in range(4):
                        c = 4 * u + r
                        v = GH * VW * g + v0
                        mm = pe.matmul(bank[5][32 * r:32 * r + 32, lo:hi], V[:, c, v:v + 32],
                                       P[0:CW, (g * CT + c) % P_SLOTS, lo:hi],
                                       start=(u == 0 and lo == 0), stop=(u == 2), skip_group_check=True)
                    if part:
                        mm.then_inc(*did("values", l, g, 4 * u + 3))

                def p_sums(g):
                    pe.wait_ge(*seen(b, "p_added", g, CT - 1))
                    pe.matmul(bank[6][:, 0:GW], ones[0:CW, :], accP[0:CW, g % 2, :], start=True, stop=True
                              ).then_inc(*did("p_sums", g))

                def heads_out(l, g):
                    if l == 1:
                        pe.wait_ge(*seen(b, "u_ready", g))
                        for i in range(GH):
                            h = GH * g + i
                            mm = pe.matmul(bank[7][64 * (h % 2):64 * (h % 2) + 64, (i // 2) * T:(i // 2 + 1) * T],
                                           w["wv", 1][:, h * 64:(h + 1) * 64], Un[:, i * T:(i + 1) * T],
                                           start=True, stop=True, skip_group_check=True)
                        mm.then_inc(*did("heads", l, g))
                        return
                    pe.wait_ge(*seen(b, "o_copied", l, g))
                    for i in range(GH):
                        h = GH * g + i
                        mm = pe.matmul(bank[6][0:T, h * VW:(h + 1) * VW], Osb[:, i * T:(i + 1) * T],
                                       picks[:, i, :], start=True, stop=True, skip_group_check=True)
                    mm.then_inc(*did("heads", l, g))

                def cross(l):
                    pe.wait_ge(*once(f"weights_in{l}"))
                    nl = NEXT_SMALL.get(l)
                    if nl is not None:
                        pe.wait_ge(*once(f"weights_in{nl}"))
                    if l == 3:
                        pe.wait_ge(*seen(b, "ctxT_in"))
                    if l != 1:
                        k_chunk(nl, 0)
                    norm_T(2 * l)
                    if l == 1:
                        q_wide()
                        pe.wait_ge(*seen(b, "qtb", 0))
                        pe.wait_ge(*seen(b, "qt_odd", 1))
                        pe.wait_ge(*ahead(b, "ctxTb"))
                        pe.wait_ge(*seen(b, "ctxN_in"))
                        pe.wait_ge(*seen(b, "bias_row_in"))
                    else:
                        q_small(l)
                        of = ahead if l == 0 else seen
                        pe.wait_ge(*of(b, f"k_stacked{l}"))
                        pe.wait_ge(*seen(b, "q_stacked", l))
                        pe.wait_ge(*seen(b, "q_stacked_too", l))
                        pe.wait_ge(*of(b, "v_ready", l, 3))
                    if l == 3:
                        pe.wait_ge(*seen(b, "absent"))
                    for n in range(GH * NCH + LEAD):
                        if l == 1 and n == 0:
                            pe.wait_ge(*seen(b, "qt_even", 1))
                        if l != 1 and n == (4 if l == 3 else 7):
                            k_chunk(nl, 2)
                        if l == 3 and n in (2, 6, 9):
                            k_squares((2, 6, 9).index(n))
                        if l != 1 and n == 12:
                            pe.wait_ge(*(seen(b, "k_log") if l == 3 else seen(b, "k_biased", nl, 2)))
                        max_scores(l, n // 12, n % 12)
                    if l == 1:
                        pe.wait_ge(*seen(b, "qtb", 1))
                    shift_T(l, 0)
                    for g in range(GROUPS):
                        for u in range(3):
                            for c in range(4 * u, 4 * u + 4):
                                scores(l, g, c)
                                if l != 1 and (g or c > 3) and c % 4 > 1:
                                    before_g, before_u = divmod(3 * g + u - 1, 3)
                                    values(l, before_g, before_u, c % 4 - 2)
                                if l != 1 and g and c == 9:
                                    heads_out(l, g - 1)
                                if l != 1 and g == GROUPS - 1 and c in (4, 8, 11):
                                    v_proj(nl, (4, 8, 11).index(c))
                                for n in chunks_after(l, g, c):
                                    max_scores(l, n // 12, n % 12)
                            if u == 2 and g + 1 < GROUPS:
                                if l == 1 and g:
                                    pe.wait_ge(*seen(b, "oT", g - 1))
                                else:
                                    pe.wait_ge(*seen(b, "shift", l, g))
                                shift_T(l, g + 1)
                            if l == 1 and g and u == 0:
                                p_sums(g - 1)
                            if l == 1 and u:
                                values(l, g, u - 1)
                            if l == 1 and g and u == 1:
                                heads_out(l, g - 1)
                        if l == 1:
                            values(l, g, 2)
                    if l != 1:
                        values(l, GROUPS - 1, 2, 0)
                        values(l, GROUPS - 1, 2, 1)
                        heads_out(l, GROUPS - 1)
                    if l == 1:
                        pe.wait_ge(*seen(b, "oT", GROUPS - 2))
                        heads_out(l, GROUPS - 1)
                    if l == 1:
                        pe.wait_ge(*seen(b, "oT", GROUPS - 1))
                        for p in range(8):
                            mm = pe.matmul(bank[6][0:T, 0:D], oT[:, p * T:(p + 1) * T],
                                           w["wo", 1][:, p * 128:(p + 1) * 128], start=(p == 0), stop=(p == 7))
                        mm.then_inc(*did("y_ps", 2 * l))
                        return
                    pe.wait_ge(*seen(b, "attn", l))
                    pe.transpose(bank[7][:, 0:T], attn[:, :], ident[0:T, 0:T]).then_inc(*did("attnT_ps", l))
                    pe.wait_ge(*seen(b, "attnT", l))
                    pe.matmul(bank[6][0:T, 0:D], attnT[:, :], w["wo", l][:, :], start=True, stop=True
                              ).then_inc(*did("y_ps", 2 * l))
                    v_proj(nl, 3)

                def experts(l):
                    e, ni, of_half = MOE[l]
                    norm_T(2 * l + 1)
                    pe.matmul(bank[6][0:T, 0:e], xnT[:, :], w["gw", l][:, :], start=True, stop=True
                              ).then_inc(*did("logits", l))

                    def up(ck):
                        base = 3 * (ck % 2)
                        if ck >= 2:
                            pe.wait_ge(*seen(b, "hidden", l, ck - 2))
                        for n, wn in ((0, "wa"), (1, "wb")):
                            for t in range(4):
                                m = 4 * ck + t
                                mm = pe.matmul(bank[base + n][:, t * T:(t + 1) * T], w[wn, l][:, m * 128:(m + 1) * 128],
                                               xnT[:, :], start=True, stop=True)
                            mm.then_inc(*did("gate_up", l, ck, n))

                    def weigh(ck):
                        base = 3 * (ck % 2)
                        for t in range(4):
                            for s in (0, 1):
                                ex_ = of_half(2 * (4 * ck + t) + s)
                                mm = pe.matmul(bank[base + 2][64 * s:64 * s + 64, t * T:(t + 1) * T],
                                               comb[:, ex_:ex_ + 1].to_broadcast([T, 64]), ident[0:T, 0:T],
                                               start=True, stop=True, skip_group_check=True)
                        mm.then_inc(*did("weighed", l, ck))

                    def down(ck):
                        pe.wait_ge(*seen(b, "hidden", l, ck))
                        for t in range(4):
                            m = 4 * ck + t
                            mm = pe.matmul(bank[7][0:T, 0:D], hm[ck % 2][:, t * T:(t + 1) * T], w["w2", l][:, m, :],
                                           start=(m == 0), stop=(m == ni - 1))
                        mm.then_inc(*did("down", l, ck))

                    up(0)
                    up(1)
                    if l == 3:
                        pe.wait_ge(*seen(b, "kept"))
                        pe.matmul(bank[6][0:T, 16:24], before[0:T, 0:T], msk[:, 0:8], start=True, stop=False)
                        pe.matmul(bank[6][0:T, 16:24], ones[0:T, 0:T], acnt[:, :], start=False, stop=True
                                  ).then_inc(*did("position"))
                    pe.wait_ge(*seen(b, "comb", l))
                    for ck in range(ni // 4):
                        if ck >= 2:
                            up(ck)
                        weigh(ck)
                        if ck:
                            down(ck - 1)
                    down(ni // 4 - 1)

                def switch():
                    norm_T(3)
                    pe.matmul(bank[6][0:T, 0:2 * SH * SE], xnT[:, :], swd[:, :], start=True, stop=True
                              ).then_inc(*did("gates_ps"))

                    def transposed(which):
                        src, bk = (sq, 5) if which == 0 else (sk, 6)
                        pe.wait_ge(*(seen(b, "expert_sum", 0, SE - 1) if which == 0 else seen(b, "keys_sum")))
                        for c in range(4):
                            mm = pe.transpose(bank[bk][:, c * T:(c + 1) * T], src[:, c * 128:(c + 1) * 128], ident[0:T, 0:T])
                        mm.then_inc(*did("switch_T_ps", which))

                    for n in range(3 * SE):
                        which, k = divmod(n, SE)
                        if n == 0:
                            pe.wait_ge(*seen(b, "swqv_in", "q"))
                        if n == 2 * SE:
                            pe.wait_ge(*seen(b, "swqv_in", "v"))
                        if n == 2 * SE + 2:
                            transposed(0)
                        if n == 3 * SE - 1:
                            transposed(1)
                        src = swk if which == 1 else swqv
                        if n >= 5:
                            pe.wait_ge(*seen(b, "gated", n - 5))
                        pe.matmul(bank[n % 5][0:T, :], xnT[:, :], src[:, k * 512:(k + 1) * 512],
                                  start=True, stop=True).then_inc(*did("switch_ps", n))
                    pe.wait_ge(*seen(b, "switch_T", 1))
                    for h in range(SH):
                        r = 64 * (h % 2)
                        c = slice((h // 2) * T, (h // 2 + 1) * T)
                        mm = pe.matmul(bank[5 + h % 2][0:T, (h // 2) * T:(h // 2 + 1) * T], sqT[r:r + 64, c], skT[r:r + 64, c],
                                       start=True, stop=True)
                        if h >= 6:
                            mm.then_inc(*did("self_scores", h % 2))
                    pe.wait_ge(*seen(b, "self_exp"))
                    for h in range(SH):
                        mm = pe.transpose(bank[2 + h // 4][0:T, (h % 4) * T:(h % 4 + 1) * T],
                                          sc[:, h * T:(h + 1) * T], ident[0:T, 0:T])
                        if h % 4 == 3:
                            mm.then_inc(*did("self_pT_ps", h // 4))
                    pe.wait_ge(*seen(b, "expert_sum", 2, SE - 1))
                    for h in range(SH):
                        if h % 4 == 0:
                            pe.wait_ge(*seen(b, "self_pT", h // 4))
                        mm = pe.matmul(bank[4][0:T, h * SD:(h + 1) * SD], pT[:, h * T:(h + 1) * T],
                                       sv[:, h * SD:(h + 1) * SD], start=True, stop=True)
                    mm.then_inc(*did("self_out"))
                    pe.wait_ge(*seen(b, "switch_z"))
                    for c in range(3):
                        n = 128 if c < 2 else 64
                        mm = pe.transpose(bank[5][0:n, c * T:(c + 1) * T], sz[:, c * 128:c * 128 + n], ident[0:T, 0:T])
                    mm.then_inc(*did("switch_zT_ps"))
                    pe.wait_ge(*seen(b, "switch_zT"))
                    for c in range(3):
                        n = 128 if c < 2 else 64
                        mm = pe.matmul(bank[7][0:T, 0:D], szT[0:n, c * T:(c + 1) * T], swo[0:n, c, :],
                                       start=(c == 0), stop=(c == 2))
                    mm.then_inc(*did("y_ps", 3))

                for l in range(4):
                    cross(l)
                    if l == 1:
                        switch()
                    else:
                        experts(l)

        @block.scalar
        def _(act):
            st.engine()
            act.wait_ge(*once("pool_setup"))
            act.wait_ge(*once("setup_bf16"))
            b = None

            def keys_biased(l, ch):
                cols = slice(ch * CH, (ch + 1) * CH)
                act.wait_ge(*seen(b, "k_ps", l, ch))
                act.activation(Kf[:, cols], bank[K_BANKS[ch]][:, 0:CH], ACT.Identity, bias=w["bk", l][:, 0:1]
                               ).then_inc(*did("k_biased", l, ch))
                if l == 0:
                    if b is not None and ch == 0:
                        act.wait_ge(*seen(b, "k_out", 3))
                    act.activation(ktmp[:, cols], bank[K_BANKS[ch]][:, 0:CH], ACT.Square, bias=w["bk", l][:, 0:1]
                                   ).then_inc(*did("k_squared", ch))

            def key_norms():
                for ch in range(NCH):
                    cols = slice(ch * CH, (ch + 1) * CH)
                    act.wait_ge(*seen(b, "k_ss", ch))
                    act.activation(ktmp[:, cols], bank[K_BANKS[ch]][:, 0:CH], ACT.Ln, bias=eps6[:, 0:1],
                                   scale=1.0 / DH).then_inc(*did("k_log"))
                act.wait_ge(*seen(b, "k_log"))
                act.activation(ktmp[:, :], ktmp[:, :], ACT.Exp, scale=-0.5).then_inc(*did("k_rms"))

            act.wait_ge(*once("weights_in0"))
            for ch in range(NCH):
                keys_biased(0, ch)
            key_norms()
            st.loop()
            with act.Fori(0, B) as b:
                act.wait_ge(st.sem("turn_open"), b + 1)

                def shift(l, g):
                    act.wait_ge(*seen(b, "shift_ps", l, g))
                    act.activation(QS[STACK:ROWS, 2 * g:2 * g + 2, :].rearrange("p a n -> p (a n)"),
                                   shift_ps(l), ACT.Copy).then_inc(*did("shift", l, g))

                def values_out(l, g):
                    act.wait_ge(*seen(b, "values", l, g, CT - 1))
                    if g > 0:
                        act.wait_ge(*seen(b, "heads", l, g - 1))
                    act.activation(Osb, bank[5][:, 0:GW], ACT.Copy).then_inc(*did("o_copied", l, g))

                def exps(l):
                    shift(l, 0)
                    for g in range(GROUPS):
                        for c in range(CT):
                            t = g * CT + c
                            act.wait_ge(*seen(b, "scores", l, g, c))
                            if t >= P_SLOTS:
                                o = t - P_SLOTS
                                u = (o % CT) if l == 1 else 4 * ((o % CT) // 4) + 3
                                act.wait_ge(*seen(b, "values", l, o // CT, u))
                                if l == 1:
                                    act.wait_ge(*seen(b, "p_added", o // CT, o % CT))
                            act.activation(P[0:CW, t % P_SLOTS, :], bank[t % 3][0:CW, 0:GW], ACT.Exp
                                           ).then_inc(*did("exp", l, g, c))
                            if l == 1 and c == 10 and g > 0:
                                heads_T(g - 1)
                            if l != 1 and g and c == 4:
                                values_out(l, g - 1)
                        if g + 1 < GROUPS:
                            shift(l, g + 1)
                    if l != 1:
                        values_out(l, GROUPS - 1)
                    if l == 1:
                        heads_T(GROUPS - 1)
                        return
                    act.wait_ge(*seen(b, "attnT_ps", l))
                    act.activation(attnT[:, :], bank[7][:, 0:T], ACT.Copy).then_inc(*did("attnT", l))

                def heads_T(g):
                    act.wait_ge(*seen(b, "heads", 1, g))
                    act.activation(oT[:, 2 * g * T:(2 * g + 2) * T], bank[7][:, 0:2 * T], ACT.Copy
                                   ).then_inc(*did("oT", g))

                def q_path(l):
                    act.wait_ge(*seen(b, "q_high", l))
                    act.activation(Qz[:, :, 1:3, :], Qz[:, :, 0:1, :].to_broadcast([T, H, 2, 16]), ACT.Copy
                                   ).then_inc(*did("q_copied", l))
                    act.wait_ge(*seen(b, "q_middle", l))
                    act.activation(Qz[:, :, 4, :], Qz[:, :, 3, :], ACT.Copy).then_inc(*did("q_copied", l))
                    keys_biased(NEXT_SMALL[l], 1)
                    act.wait_ge(*seen(b, "qs_ps", l, 0))
                    act.activation(QS[0:STACK, 0:4, :].rearrange("p a n -> p (a n)"), as_bf16[0][0:STACK, 0:8 * T],
                                   ACT.Copy).then_inc(*did("q_stacked", l))

                def q_wide():
                    act.wait_ge(*seen(b, "qh_ps", 0))
                    act.activation(qTh[:, 0:400], bank[0][:, 0:400], ACT.Copy, scale=0.125).then_inc(*did("qh", 0))
                    for half in (0, 1):
                        act.wait_ge(*seen(b, "qt_ps", half, 0))
                        act.activation(of_parity(qt, half, 0), bank[2 + half][:, 0:400].rearrange("p (j q) -> p j q", j=4),
                                       ACT.Copy).then_inc(*did("qt_even", half))
                        act.wait_ge(*seen(b, "qt_even", half))
                        act.wait_ge(*seen(b, "qt_odd", half))
                        cols = slice(800 * half, 800 * half + 800)
                        act.activation(qtb[:, cols], qt[:, cols], ACT.Copy).then_inc(*did("qtb", half))

                def experts(l):
                    e, ni, _ = MOE[l]
                    act.wait_ge(*seen(b, "top", l))
                    act.activation(ex[:, 0:e], lg[:, 0:e], ACT.Exp, bias=small[:, 0:1]).then_inc(*did("route_exp", l))
                    for ck in range(ni // 4):
                        act.wait_ge(*seen(b, "gate_up", l, ck, 1))
                        if ck >= 2:
                            act.wait_ge(*seen(b, "hidden", l, ck - 2))
                        act.activation(th[ck % 2], bank[3 * (ck % 2)][:, 0:GW], ACT.Tanh, scale=0.5
                                       ).then_inc(*did("tanh", l, ck))

                def switch():
                    act.wait_ge(*seen(b, "gates_z"))
                    act.activation(ex[:, 0:80], lg[:, 0:80], ACT.Exp, scale=-1.0).then_inc(*did("gates_exp"))
                    for which, dst, bk in ((0, sqT, 5), (1, skT, 6)):
                        act.wait_ge(*seen(b, "switch_T_ps", which))
                        act.activation(dst, bank[bk][:, 0:400], ACT.Copy).then_inc(*did("switch_T", which))
                    act.wait_ge(*seen(b, "self_shifted", 1))
                    act.activation(sc, sc, ACT.Exp, scale=float(SD) ** -0.5).then_inc(*did("self_exp"))
                    for n in (0, 1):
                        act.wait_ge(*seen(b, "self_pT_ps", n))
                        act.activation(pT[:, n * 400:(n + 1) * 400], bank[2 + n][0:T, 0:400], ACT.Copy
                                       ).then_inc(*did("self_pT", n))
                    act.wait_ge(*seen(b, "switch_zT_ps"))
                    act.activation(szT[:, 0:2 * T], bank[5][:, 0:2 * T], ACT.Copy).then_inc(*did("switch_zT"))
                    act.activation(szT[0:64, 2 * T:3 * T], bank[5][0:64, 2 * T:3 * T], ACT.Copy
                                   ).then_inc(*did("switch_zT"))

                for l in range(4):
                    if l != 1:
                        keys_biased(NEXT_SMALL[l], 0)
                        q_path(l)
                        keys_biased(NEXT_SMALL[l], 2)
                        if l == 3:
                            key_norms()
                    else:
                        q_wide()
                    exps(l)
                    if l == 1:
                        switch()
                    else:
                        experts(l)

        @block.vector
        def _(dve):
            V_ = nc.vector
            st.engine()
            dve.wait_ge(*once("pool_setup"))
            dve.wait_ge(*once("const_in"))
            V_.tensor_copy(identb[:, :], ident[:, :]).then_inc(*did("setup_bf16"))
            V_.memset(eps6[:, :], 1e-6).then_inc(*did("setup_bf16"))
            V_.tensor_copy(eyes[0:T, :, :], ident[0:T, 0:T].unsqueeze(1).to_broadcast([T, GH, T])
                           ).then_inc(*did("setup_bf16"))
            V_.tensor_tensor(gqk[:, 0, :], gqk[:, 0, :], gqk[:, 1, :], ALU.mult).then_inc(*did("setup_bf16"))
            b = None

            def link(ins):
                s, n = did("vector_order", st.count.get("vector_order", 0))
                ins.then_inc(s, n)
                dve.wait_ge(*seen(b, "vector_order", st.count["vector_order"] - 1))

            def k_split(l):
                if l == 0:
                    dve.wait_ge(*seen(b, "k_rms"))
                    link(V_.tensor_tensor(Kf[:, :], Kf[:, :], ktmp, ALU.mult))
                else:
                    dve.wait_ge(*seen(b, "k_biased", l, NCH - 1))
                link(V_.tensor_copy(Kp[:, 0, :], Kf[:, :]))
                link(V_.tensor_tensor(Kf[:, :], Kf[:, :], Kp[:, 0, :], ALU.subtract))
                link(V_.tensor_copy(Kp[:, 1, :], Kf[:, :]))
                V_.tensor_tensor(Kp[:, 2, :], Kf[:, :], Kp[:, 1, :], ALU.subtract).then_inc(*did("k_parts", l))

            def v_bias(l, u):
                dve.wait_ge(*seen(b, "v_ps", l, u))
                V_.tensor_tensor(V[:, 3 * u:3 * u + 3, 0:144],
                                 bank[V_BANKS[u]][0:CW, 0:432].rearrange("p (a n) -> p a n", a=3),
                                 w["bv", l][0:CW, :].unsqueeze(1).to_broadcast([CW, 3, 144]), ALU.add
                                 ).then_inc(*did("v_ready", l, u))

            def mask_row():
                dve.wait_ge(*seen(b, "mrow_in"))
                V_.tensor_scalar(mrow[:, :], mrow_in.bitcast(U8), 0.0, NEG, ALU.is_equal, ALU.mult
                                 ).then_inc(*did("mrow_ready"))

            mask_row()
            dve.wait_ge(*once("weights_in0"))
            k_split(0)
            for u in range(4):
                v_bias(0, u)
            dve.wait_ge(*once_now("v_ready"))
            dve.sem_inc(st.sem("turn_open"), 1)
            st.loop()
            with dve.Fori(0, B) as b:
                dve.wait_ge(*ahead(b, "x_in"))
                link(V_.tensor_copy(x[:, :], x_next[:, :]))

                def norm(k):
                    link(V_.bn_stats(bn[:, :], x[:, :]))
                    dve.sem_inc(st.sem("vector_passed"), 1)
                    link(V_.bn_aggr(mv[:, :], bn[:, :]))
                    V_.tensor_scalar(rstd[:, :], mv[:, 1:2], 1e-5, None, ALU.add).then_inc(*did("ln_var", k))
                    dve.wait_ge(*seen(b, "ln_rstd", k))
                    V_.tensor_scalar(xn[:, :], x[:, :], mv[:, 0:1], rstd[:, 0:1], ALU.subtract, ALU.mult
                                     ).then_inc(*did("xn", k))
                    dve.wait_ge(*seen(b, "xnT_ps", k))
                    V_.tensor_copy(xnT[:, :], bank[7][:, 0:T]).then_inc(*did("xnT", k))

                def add_y(k, ps, bias=None):
                    dve.wait_ge(*seen(b, "y_ps", k))
                    if bias is not None:
                        link(V_.tensor_tensor(yb[:, :], ps, bias, ALU.add))
                        V_.tensor_tensor(x[:, :], x[:, :], yb[:, :], ALU.add).then_inc(*did("x_out", k))
                    else:
                        V_.tensor_tensor(x[:, :], x[:, :], ps, ALU.add).then_inc(*did("x_out", k))
                    dve.wait_ge(*seen(b, "x_out", k))

                def q_wide():
                    dve.wait_ge(*seen(b, "qh_ps", 1))
                    V_.tensor_scalar(qTh[:, 400:800], bank[1][:, 0:400], 0.125, None, ALU.mult).then_inc(*did("qh_too"))
                    for half in (0, 1):
                        dve.wait_ge(*seen(b, "qt_ps", half, 1))
                        V_.tensor_copy(of_parity(qt, half, 1), bank[4 + half][:, 0:400].rearrange("p (j q) -> p j q", j=4)
                                       ).then_inc(*did("qt_odd", half))

                def q_path(l):
                    dve.wait_ge(*seen(b, "q_ps", l))
                    if l == 0:
                        link(V_.tensor_tensor(qn[:, :], bank[6][0:T, 0:D], w["bq", l][0:T, :], ALU.add))
                        link(V_.tensor_tensor(q2[:, :], qn[:, :], qn[:, :], ALU.mult))
                        link(V_.reduce_sum(qss[:, :], q2[:, :].rearrange("p (h d) -> p h d", h=H), AX))
                        V_.tensor_scalar(qss[:, :], qss[:, :], 1.0 / DH, 1e-6, ALU.mult, ALU.add).then_inc(*did("q_ms"))
                        dve.wait_ge(*seen(b, "q_rms"))
                        link(V_.tensor_tensor(q2[:, :].rearrange("p (h d) -> p h d", h=H),
                                              qn[:, :].rearrange("p (h d) -> p h d", h=H),
                                              qss[:, :].unsqueeze(2).to_broadcast([T, H, DH]), ALU.mult))
                        V_.tensor_tensor(qn[:, :], q2[:, :], gqk[0:T, 0, :], ALU.mult).then_inc(*did("q_ready", l))
                    else:
                        V_.tensor_tensor(qn[:, :], bank[6][0:T, 0:D], w["bq", l][0:T, :], ALU.add
                                         ).then_inc(*did("q_ready", l))
                    dve.wait_ge(*seen(b, "q_ready", l))
                    link(V_.tensor_tensor(qm.rearrange("t (p e) r -> t p e r", e=2),
                                          qn[:, :].rearrange("t (p r) -> t p r", p=PAIRS).unsqueeze(2
                                          ).to_broadcast([T, PAIRS, 2, 16]),
                                          own_dims[0:T, :, :].unsqueeze(1).to_broadcast([T, PAIRS, 2, 16]), ALU.mult))
                    V_.tensor_copy(Qz[:, :, 0, :], qm).then_inc(*did("q_high", l))
                    dve.wait_ge(*seen(b, "q_high", l))
                    link(V_.tensor_tensor(qm, qm, Qz[:, :, 0, :], ALU.subtract))
                    V_.tensor_copy(Qz[:, :, 3, :], qm).then_inc(*did("q_middle", l))
                    dve.wait_ge(*seen(b, "q_middle", l))
                    V_.tensor_tensor(Qz[:, :, 5, :], qm, Qz[:, :, 3, :], ALU.subtract).then_inc(*did("q_parts", l))
                    dve.wait_ge(*seen(b, "qs_ps", l, 1))
                    V_.tensor_copy(QS[0:STACK, 4:8, :].rearrange("p a n -> p (a n)"), as_bf16[1][0:STACK, 0:8 * T]
                                   ).then_inc(*did("q_stacked_too", l))

                def maxima(l, g):
                    for k in range(12):
                        i, ch = divmod(k, NCH)
                        n = g * 12 + k
                        dve.wait_ge(*seen(b, "max_scores", l, n))
                        src = bank[max_bank(l, n)][0:T, 0:CH]
                        if l == 3:
                            if n >= 2:
                                dve.wait_ge(*seen(b, "max_chunk", l, n - 2))
                            dve.sem_inc(st.sem("vector_passed"), 1)
                            V_.tensor_tensor_reduce(masked[:, n % 2, :], src, absent[:, ch * CH:(ch + 1) * CH],
                                                    1.0, LOWEST, ALU.add, ALU.max, mxp[:, GH * g + i, ch:ch + 1]
                                                    ).then_inc(*did("max_chunk", l, n))
                        else:
                            V_.reduce_max(mxp[:, GH * g + i, ch:ch + 1], src, AX).then_inc(*did("max_chunk", l, n))
                        if l == 1 and g >= 2 and k == LEAD + 3:
                            sums_out(g - 2)
                    dve.wait_ge(*seen(b, "max_chunk", l, g * 12 + 11))
                    flat = MZ[:, :, :, :].rearrange("t p e k -> t (p e k)")
                    for p in (2 * g, 2 * g + 1):
                        V_.tensor_reduce(flat[:, 6 * p + 1:6 * p + 6:4],
                                         mxp[:, 2 * p:2 * p + 2, :], AX, ALU.max, negate=True
                                         ).then_inc(*did("maxima", l, g))

                def sums_out(g):
                    dve.wait_ge(*seen(b, "p_sums", g))
                    if g > 0:
                        dve.wait_ge(*seen(b, "heads", 1, g - 1))
                    link(V_.reciprocal(Un, bank[6][:, 0:GW]))
                    dve.wait_ge(*seen(b, "values", 1, g, CT - 1))
                    V_.tensor_tensor(Un, bank[5][:, 0:GW], Un, ALU.mult).then_inc(*did("u_ready", g))

                def ranks(src, groups, n, keep, dst):
                    m = groups * n * n
                    gt = cmp[:, 0, 0:m].rearrange("t (g i j) -> t g i j", g=groups, i=n)
                    eq = cmp[:, 1, 0:m].rearrange("t (g i j) -> t g i j", g=groups, i=n)
                    s3 = src.rearrange("t (g n) -> t g n", g=groups)
                    other = s3.unsqueeze(2).to_broadcast([T, groups, n, n])
                    own = s3.unsqueeze(3).to_broadcast([T, groups, n, n])
                    V_.tensor_tensor(gt, other, own, ALU.is_gt)
                    link(V_.tensor_tensor(eq, other, own, ALU.is_equal))
                    link(V_.tensor_tensor(eq, eq, earlier[0:T, 0:n, 0:n].unsqueeze(1).to_broadcast([T, groups, n, n]),
                                          ALU.mult))
                    link(V_.tensor_tensor(cmp[:, 0, 0:m], cmp[:, 0, 0:m], cmp[:, 1, 0:m], ALU.add))
                    link(V_.reduce_sum(rank[:, 0:groups * n],
                                       cmp[:, 0, 0:m].rearrange("t (g j) -> t g j", j=n), AX))
                    link(V_.tensor_scalar(dst, rank[:, 0:groups * n], float(keep) - 0.5, None, ALU.is_lt))

                def experts(l):
                    e, ni, _ = MOE[l]
                    norm(2 * l + 1)
                    v_bias(NEXT_SMALL[l], 3)
                    dve.wait_ge(*seen(b, "logits", l))
                    link(V_.tensor_copy(lg[:, 0:e], bank[6][0:T, 0:e]))
                    V_.tensor_reduce(small[:, 0:1], lg[:, 0:e], AX, ALU.max, negate=True).then_inc(*did("top", l))
                    dve.wait_ge(*seen(b, "route_exp", l))
                    link(V_.reduce_sum(small[:, 1:2], ex[:, 0:e], AX))
                    link(V_.reciprocal(small[:, 2:3], small[:, 1:2]))
                    link(V_.tensor_scalar(ex[:, 0:e], ex[:, 0:e], small[:, 2:3], None, ALU.mult))
                    if l == 0:
                        link(V_.reduce_max(gsc[:, 0:4], ex[:, 0:8].rearrange("t (g n) -> t g n", g=4), AX))
                        ranks(gsc[:, 0:4], 1, 4, 2, gsc[:, 8:12])
                        link(V_.tensor_tensor(ex[:, 0:8].rearrange("t (g n) -> t g n", g=4),
                                              ex[:, 0:8].rearrange("t (g n) -> t g n", g=4),
                                              gsc[:, 8:12].unsqueeze(2).to_broadcast([T, 4, 2]), ALU.mult))
                    ranks(ex[:, 0:e], 1, e, 4 if l == 2 else 2, msk[:, 0:e])
                    link(V_.tensor_tensor(ex[:, 0:e], ex[:, 0:e], msk[:, 0:e], ALU.mult))
                    if l == 3:
                        dve.sem_inc(*did("kept"))
                        dve.wait_ge(*seen(b, "position"))
                        link(V_.tensor_scalar(rank[:, 0:8], bank[6][0:T, 16:24], CAPACITY - 0.5, 0.5, ALU.is_lt, ALU.mult))
                        link(V_.tensor_tensor(acnt[:, :], acnt[:, :], msk[:, 0:8], ALU.add))
                        V_.tensor_tensor(comb[:, 0:e], ex[:, 0:e], rank[:, 0:e], ALU.mult).then_inc(*did("comb", l))
                    else:
                        link(V_.reduce_sum(small[:, 1:2], ex[:, 0:e], AX))
                        link(V_.reciprocal(small[:, 2:3], small[:, 1:2]))
                        V_.tensor_scalar(comb[:, 0:e], ex[:, 0:e], small[:, 2:3], 0.5, ALU.mult, ALU.mult
                                         ).then_inc(*did("comb", l))
                    for ck in range(ni // 4):
                        base = 3 * (ck % 2)
                        h_ = hm[ck % 2]
                        dve.wait_ge(*seen(b, "tanh", l, ck))
                        if ck >= 2:
                            dve.wait_ge(*seen(b, "down", l, ck - 2))
                        link(V_.scalar_tensor_tensor(h_, th[ck % 2], 1.0, bank[base + 1][:, 0:GW], ALU.add, ALU.mult))
                        link(V_.tensor_tensor(h_, h_, bank[base][:, 0:GW], ALU.mult))
                        dve.wait_ge(*seen(b, "weighed", l, ck))
                        V_.tensor_tensor(h_, h_, bank[base + 2][:, 0:GW], ALU.mult).then_inc(*did("hidden", l, ck))
                    dve.wait_ge(*seen(b, "down", l, ni // 4 - 1))
                    V_.tensor_tensor((x_last if l == 3 else x)[:, :], x[:, :], bank[7][0:T, 0:D], ALU.add
                                     ).then_inc(*did("x_out", 2 * l + 1))
                    dve.wait_ge(*seen(b, "x_out", 2 * l + 1))

                def switch():
                    norm(3)
                    dve.wait_ge(*seen(b, "gates_ps"))
                    V_.tensor_scalar(lg[:, 0:80], bank[6][0:T, 0:80], 17.0, None, ALU.min).then_inc(*did("gates_z"))
                    dve.wait_ge(*seen(b, "gates_z"))
                    ranks(lg[:, 0:80], 16, 5, SK, msk[:, 0:80])
                    dve.wait_ge(*seen(b, "gates_exp"))
                    link(V_.tensor_scalar(ex[:, 0:80], ex[:, 0:80], 1.0, None, ALU.add))
                    link(V_.reciprocal(ex[:, 0:80], ex[:, 0:80]))
                    link(V_.tensor_tensor(comb[:, 0:80], ex[:, 0:80], msk[:, 0:80], ALU.mult))
                    n = 0
                    for which in range(3):
                        off = 40 if which == 0 else 0
                        if which == 2:
                            dve.wait_ge(*seen(b, "switch_T_ps", 0))
                        for k in range(SE):
                            dve.wait_ge(*seen(b, "switch_ps", n))
                            V_.tensor_tensor(gated[which % 2][:, k * 512:(k + 1) * 512].rearrange("t (a d) -> t a d", a=SH),
                                             bank[n % 5][0:T, :].rearrange("t (a d) -> t a d", a=SH),
                                             comb[:, off + k:off + 40:SE].unsqueeze(2).to_broadcast([T, SH, SD]),
                                             ALU.mult).then_inc(*did("gated", n))
                            n += 1
                        if which == 1:
                            dve.wait_ge(*seen(b, "gated", n - 1))
                            V_.reduce_sum(sk, gated[1].rearrange("t (e n) -> t n e", e=SE), AX).then_inc(*did("keys_sum"))
                    for n in (0, 1):
                        dve.wait_ge(*seen(b, "self_scores", n))
                        s3 = bank[5 + n][0:T, 0:400].rearrange("t (h k) -> t h k", h=4)
                        link(V_.reduce_max(small[:, 0:4], s3, AX))
                        V_.tensor_tensor(sc.rearrange("t (j e k) -> t j e k", j=4, e=2)[:, :, n, :], s3,
                                         small[:, 0:4].unsqueeze(2).to_broadcast([T, 4, T]), ALU.subtract
                                         ).then_inc(*did("self_shifted", n))
                        dve.wait_ge(*seen(b, "self_shifted", n))
                    dve.wait_ge(*seen(b, "self_exp"))
                    link(V_.reduce_sum(rsum[:, 0:8], sc.rearrange("t (h k) -> t h k", h=SH), AX))
                    link(V_.reciprocal(rsum[:, 0:8], rsum[:, 0:8]))
                    dve.wait_ge(*seen(b, "self_out"))
                    V_.tensor_tensor(so.rearrange("t (h d) -> t h d", h=SH),
                                     bank[4][0:T, :].rearrange("t (h d) -> t h d", h=SH),
                                     rsum[:, 0:8].unsqueeze(2).to_broadcast([T, SH, SD]), ALU.mult
                                     ).then_inc(*did("self_normed"))
                    dve.wait_ge(*seen(b, "self_normed"))
                    for h in range(Z_HEADS):
                        ins = V_.tensor_tensor(kept_heads[:, h * 320:(h + 1) * 320].rearrange("t (e d) -> t e d", e=SE),
                                               so[:, h * SD:(h + 1) * SD].unsqueeze(1).to_broadcast([T, SE, SD]),
                                               msk[:, 40 + 5 * h:45 + 5 * h].unsqueeze(2).to_broadcast([T, SE, SD]),
                                               ALU.mult)
                    link(ins)
                    link(V_.reduce_sum(sz, kept_heads[:, 0:Z_HEADS * 320].rearrange("t (h n) -> t n h", h=Z_HEADS), AX))
                    dve.wait_ge(*seen(b, "z_part", SH - 1))
                    V_.tensor_tensor(sz, sz, sz_part, ALU.add).then_inc(*did("switch_z"))
                    add_y(3, bank[7][0:T, 0:D])

                for l in range(4):
                    norm(2 * l)
                    if l != 1:
                        q_path(l)
                    else:
                        q_wide()
                    if l == 3:
                        mask_row()
                    maxima(l, 0)
                    if l == 0:
                        dve.wait_ge(*seen(b, "mask_in"))
                        V_.tensor_scalar(absent[:, :], mask_in, 0.0, NEG, ALU.is_equal, ALU.mult).then_inc(*did("absent"))
                        dve.wait_ge(*seen(b, "absent"))
                    for g in range(GROUPS):
                        if g + 1 < GROUPS:
                            maxima(l, g + 1)
                    if l == 1:
                        sums_out(GROUPS - 2)
                        sums_out(GROUPS - 1)
                    if l != 1:
                        k_split(NEXT_SMALL[l])
                        dve.wait_ge(*seen(b, "values", l, GROUPS - 1, CT - 1))
                        for u in range(3):
                            v_bias(NEXT_SMALL[l], u)
                        dve.wait_ge(*seen(b, "heads", l, GROUPS - 1))
                        o3 = bank[6][0:T, 0:H * VW].rearrange("t (h d) -> t h d", h=H)
                        link(V_.reciprocal(rsum[:, :], o3[:, :, DH:VW].rearrange("t h d -> t (h d)")))
                        V_.tensor_tensor(attn[:, :].rearrange("t (h d) -> t h d", h=H), o3[:, :, 0:DH],
                                         rsum[:, :].unsqueeze(2).to_broadcast([T, H, DH]), ALU.mult
                                         ).then_inc(*did("attn", l))
                        add_y(2 * l, bank[6][0:T, 0:D], w["bo", l][0:T, :])
                        experts(l)
                    else:
                        add_y(2, bank[6][0:T, 0:D])
                        switch()
                dve.sem_inc(st.sem("turn_open"), 1)
        return st.result()


def layout(i):
    import numpy as np
    f = np.float32
    r = lambda v: np.ascontiguousarray(v)
    wide = lambda v: r(np.broadcast_to(np.asarray(v)[None, :], (128, v.shape[0])))
    once_more = lambda v: r(np.concatenate([v, v[-1:]], 0))
    rows = np.minimum(np.arange(SP_), S - 1)
    ctx = np.asarray(i["ctx_1024"])[:, rows]
    a = {
        "x": once_more(i["x"]),
        "ctxT": once_more(ctx.transpose(0, 2, 1)),
        "ctxN": r(ctx.reshape(B, CT, CW, D).transpose(0, 2, 1, 3)),
        "mask": r(np.asarray(i["mask_BxSxS2_if1"])[:, :, rows]),
        "ident": np.eye(128, dtype=f),
    }
    m = np.zeros((B, 1, SP_), np.uint8)
    m[:, 0, :S] = np.asarray(i["mask_BxS2_bk0"]).view(np.uint8)
    a["mrow"] = once_more(m.view(np.int32))
    p = np.arange(128)
    a["headsum"] = (p[:, None] // DH == p[None, :] // DH).astype(f)
    picks = np.zeros((128, GH, VW), f)
    for k in range(GH):
        for d in range(VW):
            picks[p % 32 == (VW * k if k < 3 else 0) + d, k, d] = 1
    a["picks"] = picks
    own = np.zeros((128, 2, 16), f)
    own[:, 0, :DH] = own[:, 1, DH:] = DH ** -0.5
    a["own_dims"] = own
    a["before"] = (p[:, None] < p[None, :]).astype(f)
    q = np.arange(16)
    a["earlier"] = r(np.broadcast_to((q[None, :] < q[:, None]).astype(f)[None], (128, 16, 16)))
    pad = np.zeros((1, SP_), f)
    pad[:, S:] = NEG
    a["padrow_f"] = pad

    def values(v):
        v = v.reshape(v.shape[0], H, DH)
        return r(np.concatenate([v, np.zeros((v.shape[0], H, 1), f)], 2).reshape(v.shape[0], H * VW))

    def value_bias(v):
        v = v.reshape(1, H, DH)
        v = np.concatenate([v, np.ones((1, H, 1), f)], 2).reshape(H * VW)
        return wide(v)

    for l, wq, bq, wk, bk, wv, bv, wo in (
        (0, i["L0_xattn_Wq"].T, i["L0_xattn_bq"], i["L0_xattn_Wkv"][:128].T, i["L0_xattn_bkv"][:128],
         i["L0_xattn_Wkv"][128:].T, i["L0_xattn_bkv"][128:], i["L0_xattn_Wo"].T),
        (2, i["L2_xattn_Wq"], i["L2_xattn_bq"], i["L2_xattn_Wk"], i["L2_xattn_bk"],
         i["L2_xattn_Wv"], i["L2_xattn_bv"], i["L2_xattn_Wo"]),
        (3, i["L3_xattn_Wq"].T, i["L3_xattn_bq"], i["L3_xattn_Wk"].T, i["L3_xattn_bk"],
         i["L3_xattn_Wv"].T, i["L3_xattn_bv"], i["L3_xattn_Wo"].T),
    ):
        a[f"wq{l}"], a[f"wk{l}"], a[f"wo{l}"] = r(wq), r(wk), r(wo)
        a[f"wv{l}"] = values(np.asarray(wv))
        a[f"bq{l}"], a[f"bo{l}"] = wide(bq), wide(i[f"L{l}_xattn_bo"])
        a[f"bk{l}"] = r(np.asarray(bk)[:, None])
        a[f"bv{l}"] = value_bias(np.asarray(bv))
    a["gqk"] = r(np.stack([wide(i["L0_xattn_gq"].reshape(128)), wide(i["L0_xattn_gk"].reshape(128))], 1))

    def in_rows(v):
        return r(v.reshape(-1, 128, v.shape[1]).transpose(1, 0, 2))

    w13 = i["L0_ffn_w13_weight"]
    a["gw0"] = r(i["L0_ffn_gate_w"].T)
    a["wa0"] = r(w13[:, :256].reshape(-1, 128).T)
    a["wb0"] = r(w13[:, 256:].reshape(-1, 128).T)
    a["w20"] = in_rows(i["L0_ffn_w2_weight"].transpose(0, 2, 1).reshape(-1, 128))
    a["gw2"] = r(i["L2_ffn_gate_w"].T)
    a["wa2"] = r(i["L2_ffn_w1"].transpose(1, 0, 2).reshape(128, -1))
    a["wb2"] = r(i["L2_ffn_w3"].transpose(1, 0, 2).reshape(128, -1))
    a["w22"] = in_rows(i["L2_ffn_w2"].reshape(-1, 128))
    fc = i["L3_ffn_c_fc"]
    a["gw3"] = r(i["L3_ffn_w_gate"])
    a["wa3"] = r(fc[:, :, :192].transpose(1, 0, 2).reshape(128, -1))
    a["wb3"] = r(fc[:, :, 192:].transpose(1, 0, 2).reshape(128, -1))
    a["w23"] = in_rows(i["L3_ffn_c_proj"].reshape(-1, 128))
    a["wq1"] = r(i["L1_xattn_Wq"])
    a["wk1"] = r(i["L1_xattn_Wk"].T.reshape(8, 128, 128).transpose(1, 0, 2).reshape(128, 1024))
    a["wv1"] = r(i["L1_xattn_Wv"])
    a["wo1"] = r(i["L1_xattn_Wo"].reshape(8, 128, 128).transpose(1, 0, 2).reshape(128, 1024))
    a["swd"] = r(np.concatenate([i["L1_ffn_Ws"], i["L1_ffn_Wd"]], 1))
    for n, v in (("swq", i["L1_ffn_Wq"]), ("swk", i["L1_ffn_Wkv"][:, :SQ]), ("swv", i["L1_ffn_Wkv"][:, SQ:])):
        a[n] = r(v.reshape(128, SH, SE, SD).transpose(0, 2, 1, 3).reshape(128, SQ))
    wo = i["L1_ffn_Wo"].reshape(64, SE, 128).transpose(1, 0, 2).reshape(320, 128)
    wo = np.concatenate([wo, np.zeros((64, 128), f)], 0)
    a["swo"] = in_rows(wo)
    return a


def kernel(**inputs):
    import ml_dtypes
    import numpy as np
    import concourse.bacc as bacc
    from concourse.bass_utils import run_bass_kernel_spmd

    arrays = layout({k: np.asarray(v) for k, v in inputs.items()})
    arrays["padrow"] = arrays.pop("padrow_f").astype(ml_dtypes.bfloat16)
    known = None
    for _ in range(2):
        nc = bacc.Bacc("TRN2", target_bir_lowering=False, num_devices=1)
        a = {n: nc.dram_tensor(f"in_{n}", v.shape, mybir.dt.from_np(v.dtype), kind="ExternalInput").ap()
             for n, v in arrays.items()}
        a["scratch_k"] = nc.dram_tensor("scratch_k", (128, PARTS, SP_), BF16, kind="Internal").ap()
        a["out"] = nc.dram_tensor("out_x", (B, T, D), F32, kind="ExternalOutput").ap()
        known = build(nc, a, known)
    r = run_bass_kernel_spmd(nc, [{f"in_{n}": v for n, v in arrays.items()}], core_ids=[0])
    return r.results[0]["out_x"]
```
